# Optimizing a Trainium2 kernel written in Bass

```python
import numpy as np
import jax
import jax.numpy as jnp

def _softmax(x, axis=-1):
    return jax.nn.softmax(x, axis=axis)

def _gelu(x):
    return jax.nn.gelu(x, approximate=True)

def _silu(x):
    return jax.nn.silu(x)

def _sigmoid(x):
    return jax.nn.sigmoid(x)

def _layernorm(x, axis=-1, eps=1e-05):
    m = jnp.mean(x, axis=axis, keepdims=True)
    v = jnp.var(x, axis=axis, keepdims=True)
    return (x - m) / jnp.sqrt(v + eps)

def _scatter_add(tgt, idx, src, axis=0):
    return tgt.at[idx].add(src)

def _segment_sum(src, seg, n):
    return jax.ops.segment_sum(src, seg, n)
kernel_name = 'mk_prb_d2_jaxref_r8_20e143'

def setup_inputs(seed: int=0):
    np.random.seed(seed)
    _w = jnp.asarray

    def _L0_attn_setup():
        import jax, jax.numpy as jnp
        import numpy as np
        import math
        D_MODEL, D_C, D_R, NH = (128, 128, 32, 16)
        HD = D_MODEL // NH
        B, T = (2, 256)

        def _rope_tables(T, d_R):
            inv_freq = 1.0 / 10000.0 ** (jnp.arange(0, d_R, 2, dtype=jnp.float32) / d_R)
            t = jnp.arange(T, dtype=jnp.float32)
            freqs = jnp.outer(t, inv_freq)
            return (jnp.cos(freqs), jnp.sin(freqs))

        def _rotary_apply(x, cos, sin):
            d = x.shape[-1]
            x1, x2 = (x[..., :d // 2], x[..., d // 2:])
            return jnp.concatenate([x1 * cos - x2 * sin, x2 * cos + x1 * sin], axis=-1)
        key = jax.random.key(seed)
        ks = jax.random.split(key, 8)
        s = lambda fan_in: 1.0 / math.sqrt(fan_in)
        return {'x': jax.random.normal(ks[0], (B, T, D_MODEL), jnp.float32), 'W_kv_down': jax.random.normal(ks[1], (D_MODEL, D_C), jnp.float32) * s(D_MODEL), 'W_k_up': jax.random.normal(ks[2], (D_C, D_MODEL), jnp.float32) * s(D_C), 'W_v_up': jax.random.normal(ks[3], (D_C, D_MODEL), jnp.float32) * s(D_C), 'W_q': jax.random.normal(ks[4], (D_MODEL, D_MODEL), jnp.float32) * s(D_MODEL), 'W_q_rope': jax.random.normal(ks[5], (D_MODEL, D_R), jnp.float32) * s(D_MODEL), 'W_k_rope': jax.random.normal(ks[6], (D_C, D_R), jnp.float32) * s(D_C), 'W_o': jax.random.normal(ks[7], (D_MODEL, D_MODEL), jnp.float32) * s(D_MODEL)}
    _L0_attn_in = _L0_attn_setup()

    def _L0_ffn_setup():
        import jax, jax.numpy as jnp
        import numpy as np
        B, SEQ, DIM = (2, 512, 128)
        E, S = (8, 64)
        HID = 4 * DIM
        SCALE = DIM ** 0.5

        def rmsnorm(x, gamma):
            n = jnp.linalg.norm(x, axis=-1, keepdims=True)
            return x / jnp.maximum(n, 1e-12) * SCALE * gamma
        key = jax.random.key(seed)
        ks = jax.random.split(key, 4)
        w_init = lambda k, shape: jax.random.normal(k, shape, dtype=jnp.float32) * 0.02
        return {'x': jax.random.normal(ks[0], (B, SEQ, DIM), dtype=jnp.float32), 'norm_gamma': jnp.ones((DIM,), jnp.float32), 'slot_norm_gamma': jnp.ones((DIM,), jnp.float32), 'slot_embeds': jax.random.normal(ks[1], (E, S, DIM), dtype=jnp.float32), 'w1': w_init(ks[2], (E, DIM, HID)), 'b1': jnp.zeros((E, HID), jnp.float32), 'w2': w_init(ks[3], (E, HID, DIM)), 'b2': jnp.zeros((E, DIM), jnp.float32)}
    _L0_ffn_in = _L0_ffn_setup()

    def _L1_attn_setup():
        import jax, jax.numpy as jnp
        import numpy as np
        B, T, C = (64, 32, 128)
        N_HEAD, HEAD_SIZE, KV_RANK = (16, 64, 128)
        BLOCK_SIZE = 32
        key = jax.random.key(seed)
        ks = jax.random.split(key, 5)
        HD = N_HEAD * HEAD_SIZE

        def init(k, shape):
            fan_in = shape[0]
            bound = 1.0 / np.sqrt(fan_in)
            return jax.random.uniform(k, shape, jnp.float32, -bound, bound)
        return {'x': jax.random.normal(ks[0], (B, T, C), jnp.float32), 'w_kv_down': init(ks[1], (C, KV_RANK)), 'w_kv_up': init(ks[2], (KV_RANK, 2 * HD)), 'w_q': init(ks[3], (C, HD)), 'w_out': init(ks[4], (HD, C))}
    _L1_attn_in = _L1_attn_setup()

    def _L1_ffn_setup():
        import jax, jax.numpy as jnp
        import numpy as np
        B, S, D = (2, 64, 128)
        E, K, I = (16, 8, 128)
        I_SH = 128
        ROUTE_SCALE = 2.826
        key = jax.random.key(seed)
        ks = jax.random.split(key, 8)
        s = 0.02
        return {'x': jax.random.normal(ks[0], (B, S, D), dtype=jnp.float32), 'gate_w': jax.random.normal(ks[1], (E, D), dtype=jnp.float32) * s, 'expert_bias': jnp.zeros((E,), dtype=jnp.float32), 'w_gate': jax.random.normal(ks[2], (E, I, D), dtype=jnp.float32) * s, 'w_up': jax.random.normal(ks[3], (E, I, D), dtype=jnp.float32) * s, 'w_down': jax.random.normal(ks[4], (E, D, I), dtype=jnp.float32) * s, 'shared_gate_w': jax.random.normal(ks[5], (I_SH, D), dtype=jnp.float32) * s, 'shared_up_w': jax.random.normal(ks[6], (I_SH, D), dtype=jnp.float32) * s, 'shared_down_w': jax.random.normal(ks[7], (D, I_SH), dtype=jnp.float32) * s}
    _L1_ffn_in = _L1_ffn_setup()
    _d = {'L0_attn_x': _L0_attn_in['x'], 'L0_attn_W_kv_down': _L0_attn_in['W_kv_down'], 'L0_attn_W_k_up': _L0_attn_in['W_k_up'], 'L0_attn_W_v_up': _L0_attn_in['W_v_up'], 'L0_attn_W_q': _L0_attn_in['W_q'], 'L0_attn_W_q_rope': _L0_attn_in['W_q_rope'], 'L0_attn_W_k_rope': _L0_attn_in['W_k_rope'], 'L0_attn_W_o': _L0_attn_in['W_o'], 'L0_ffn_norm_gamma': _L0_ffn_in['norm_gamma'], 'L0_ffn_slot_norm_gamma': _L0_ffn_in['slot_norm_gamma'], 'L0_ffn_slot_embeds': _L0_ffn_in['slot_embeds'], 'L0_ffn_w1': _L0_ffn_in['w1'], 'L0_ffn_b1': _L0_ffn_in['b1'], 'L0_ffn_w2': _L0_ffn_in['w2'], 'L0_ffn_b2': _L0_ffn_in['b2'], 'L1_attn_w_kv_down': _L1_attn_in['w_kv_down'], 'L1_attn_w_kv_up': _L1_attn_in['w_kv_up'], 'L1_attn_w_q': _L1_attn_in['w_q'], 'L1_attn_w_out': _L1_attn_in['w_out'], 'L1_ffn_gate_w': _L1_ffn_in['gate_w'], 'L1_ffn_expert_bias': _L1_ffn_in['expert_bias'], 'L1_ffn_w_gate': _L1_ffn_in['w_gate'], 'L1_ffn_w_up': _L1_ffn_in['w_up'], 'L1_ffn_w_down': _L1_ffn_in['w_down'], 'L1_ffn_shared_gate_w': _L1_ffn_in['shared_gate_w'], 'L1_ffn_shared_up_w': _L1_ffn_in['shared_up_w'], 'L1_ffn_shared_down_w': _L1_ffn_in['shared_down_w']}
    _x0 = _d['L0_attn_x']
    _d['L0_attn_x'] = jax.random.normal(jax.random.fold_in(jax.random.key(seed), 1), (16, 512, 128), dtype=_x0.dtype)
    del _x0
    return _d

def reference(L0_attn_x, L0_attn_W_kv_down, L0_attn_W_k_up, L0_attn_W_v_up, L0_attn_W_q, L0_attn_W_q_rope, L0_attn_W_k_rope, L0_attn_W_o, L0_ffn_norm_gamma, L0_ffn_slot_norm_gamma, L0_ffn_slot_embeds, L0_ffn_w1, L0_ffn_b1, L0_ffn_w2, L0_ffn_b2, L1_attn_w_kv_down, L1_attn_w_kv_up, L1_attn_w_q, L1_attn_w_out, L1_ffn_gate_w, L1_ffn_expert_bias, L1_ffn_w_gate, L1_ffn_w_up, L1_ffn_w_down, L1_ffn_shared_gate_w, L1_ffn_shared_up_w, L1_ffn_shared_down_w):

    def _L0_attn_ref(x, W_kv_down, W_k_up, W_v_up, W_q, W_q_rope, W_k_rope, W_o):
        import jax, jax.numpy as jnp
        import numpy as np
        import math
        D_MODEL, D_C, D_R, NH = (128, 128, 32, 16)
        HD = D_MODEL // NH
        B, T = (2, 256)

        def _rope_tables(T, d_R):
            inv_freq = 1.0 / 10000.0 ** (jnp.arange(0, d_R, 2, dtype=jnp.float32) / d_R)
            t = jnp.arange(T, dtype=jnp.float32)
            freqs = jnp.outer(t, inv_freq)
            return (jnp.cos(freqs), jnp.sin(freqs))

        def _rotary_apply(x, cos, sin):
            d = x.shape[-1]
            x1, x2 = (x[..., :d // 2], x[..., d // 2:])
            return jnp.concatenate([x1 * cos - x2 * sin, x2 * cos + x1 * sin], axis=-1)
        Bb, Tt, _ = x.shape
        cos, sin = _rope_tables(Tt, D_R)
        cos = cos[None]
        sin = sin[None]
        c_kv = x @ W_kv_down
        k_rope = _rotary_apply(c_kv @ W_k_rope, cos, sin)
        k = (c_kv @ W_k_up).reshape(Bb, Tt, NH, HD)
        v = (c_kv @ W_v_up).reshape(Bb, Tt, NH, HD)
        q = (x @ W_q).reshape(Bb, Tt, NH, HD)
        q_rope = _rotary_apply(x @ W_q_rope, cos, sin)
        scale = math.sqrt(HD + D_R)
        scores = jnp.einsum('bqhd,bkhd->bhqk', q, k)
        scores = scores + jnp.einsum('bqr,bkr->bqk', q_rope, k_rope)[:, None]
        scores = scores / scale
        causal = jnp.triu(jnp.ones((Tt, Tt), dtype=bool), k=1)
        scores = jnp.where(causal[None, None], -jnp.inf, scores)
        w = jax.nn.softmax(scores, axis=-1)
        attn = jnp.einsum('bhqk,bkhd->bqhd', w, v).reshape(Bb, Tt, D_MODEL)
        return attn @ W_o

    def _L0_ffn_ref(x, norm_gamma, slot_norm_gamma, slot_embeds, w1, b1, w2, b2):
        import jax, jax.numpy as jnp
        import numpy as np
        B, SEQ, DIM = (2, 512, 128)
        E, S = (8, 64)
        HID = 4 * DIM
        SCALE = DIM ** 0.5

        def rmsnorm(x, gamma):
            n = jnp.linalg.norm(x, axis=-1, keepdims=True)
            return x / jnp.maximum(n, 1e-12) * SCALE * gamma
        xn = rmsnorm(x, norm_gamma)
        sn = rmsnorm(slot_embeds, slot_norm_gamma)
        logits = jnp.einsum('bnd,esd->bnes', xn, sn)
        dispatch = jax.nn.softmax(logits, axis=1)
        b, n, e, s = logits.shape
        combine = jax.nn.softmax(logits.reshape(b, n, e * s), axis=-1)
        slots = jnp.einsum('bnd,bnes->besd', xn, dispatch)
        h = jnp.einsum('besd,edh->besh', slots, w1) + b1[None, :, None, :]
        h = jax.nn.gelu(h, approximate=False)
        eo = jnp.einsum('besh,ehd->besd', h, w2) + b2[None, :, None, :]
        eo = eo.reshape(b, e * s, DIM)
        out = jnp.einsum('bmd,bnm->bnd', eo, combine)
        return out

    def _L1_attn_ref(x, w_kv_down, w_kv_up, w_q, w_out):
        import jax, jax.numpy as jnp
        import numpy as np
        B, T, C = (64, 32, 128)
        N_HEAD, HEAD_SIZE, KV_RANK = (16, 64, 128)
        BLOCK_SIZE = 32
        Bx, Tx, Cx = x.shape
        HD = N_HEAD * HEAD_SIZE
        latent_kv = x @ w_kv_down
        kv = latent_kv @ w_kv_up
        k, v = (kv[..., :HD], kv[..., HD:])
        k = k.reshape(Bx, Tx, N_HEAD, HEAD_SIZE)
        v = v.reshape(Bx, Tx, N_HEAD, HEAD_SIZE)
        q = (x @ w_q).reshape(Bx, Tx, N_HEAD, HEAD_SIZE)
        scale = HEAD_SIZE ** (-0.5)
        att = jnp.einsum('bqhd,bkhd->bhqk', q, k) * scale
        causal = jnp.tril(jnp.ones((Tx, Tx), dtype=bool))
        att = jnp.where(causal, att, -jnp.inf)
        att = jax.nn.softmax(att, axis=-1)
        y = jnp.einsum('bhqk,bkhd->bqhd', att, v)
        y = y.reshape(Bx, Tx, HD)
        return y @ w_out

    def _L1_ffn_ref(x, gate_w, expert_bias, w_gate, w_up, w_down, shared_gate_w, shared_up_w, shared_down_w):
        import jax, jax.numpy as jnp
        import numpy as np
        B, S, D = (2, 64, 128)
        E, K, I = (16, 8, 128)
        I_SH = 128
        ROUTE_SCALE = 2.826
        gates = jnp.einsum('bsd,ed->bse', x, gate_w)
        scores = jax.nn.sigmoid(gates.astype(jnp.float32))
        sel_scores = scores + expert_bias
        _, inds = jax.lax.top_k(sel_scores, K)
        selected = jnp.take_along_axis(scores, inds, axis=-1)
        selected = selected / selected.sum(axis=-1, keepdims=True)
        selected = selected * ROUTE_SCALE
        onehot = jax.nn.one_hot(inds, E, dtype=selected.dtype)
        combine = jnp.einsum('bske,bsk->bse', onehot, selected)
        hg = jnp.einsum('bsd,eid->bsei', x, w_gate)
        hu = jnp.einsum('bsd,eid->bsei', x, w_up)
        h = jax.nn.silu(hg) * hu
        ye = jnp.einsum('bsei,edi->bsed', h, w_down)
        y = jnp.einsum('bsed,bse->bsd', ye, combine).astype(x.dtype)
        g = jnp.einsum('bsd,id->bsi', x, shared_gate_w)
        u = jnp.einsum('bsd,id->bsi', x, shared_up_w)
        y = y + jnp.einsum('bsi,di->bsd', jax.nn.silu(g) * u, shared_down_w)
        return y
    x = L0_attn_x
    xn = _layernorm(x, axis=-1)
    x = x + _L0_attn_ref(xn, L0_attn_W_kv_down, L0_attn_W_k_up, L0_attn_W_v_up, L0_attn_W_q, L0_attn_W_q_rope, L0_attn_W_k_rope, L0_attn_W_o) + _L0_ffn_ref(xn, L0_ffn_norm_gamma, L0_ffn_slot_norm_gamma, L0_ffn_slot_embeds, L0_ffn_w1, L0_ffn_b1, L0_ffn_w2, L0_ffn_b2)
    xn = _layernorm(x, axis=-1)
    x = x + _L1_attn_ref(xn, L1_attn_w_kv_down, L1_attn_w_kv_up, L1_attn_w_q, L1_attn_w_out) + _L1_ffn_ref(xn, L1_ffn_gate_w, L1_ffn_expert_bias, L1_ffn_w_gate, L1_ffn_w_up, L1_ffn_w_down, L1_ffn_shared_gate_w, L1_ffn_shared_up_w, L1_ffn_shared_down_w)
    return x

_drawn_inputs = setup_inputs


def setup_inputs(seed=0):
    import zlib

    import numpy as np

    out = dict(_drawn_inputs(seed))
    spreads = {'L0_ffn_norm_gamma': (1.0, 0.2),
     'L0_ffn_slot_norm_gamma': (1.0, 0.2),
     'L0_ffn_b1': (0.0, 0.385),
     'L0_ffn_b2': (0.0, 0.1),
     'L1_ffn_expert_bias': (0.0, 0.8)}
    factors = {'L1_attn_w_q': 53.161,
     'L1_ffn_gate_w': 8.0,
     'L1_ffn_w_gate': 8.0,
     'L1_ffn_w_up': 8.0,
     'L1_ffn_w_down': 8.0,
     'L1_ffn_shared_gate_w': 8.0,
     'L1_ffn_shared_up_w': 8.0,
     'L1_ffn_shared_down_w': 8.0,
     'L1_attn_w_kv_down': 6.079,
     'L1_attn_w_kv_up': 5.588,
     'L1_attn_w_out': 5.61}
    for name, (base, spread) in spreads.items():
        noise = np.random.default_rng([zlib.crc32(name.encode()), seed]).standard_normal(out[name].shape)
        drawn = base * np.exp(spread * noise) if base else spread * noise
        out[name] = jnp.asarray(drawn.astype(out[name].dtype))
    for name, factor in factors.items():
        out[name] = (out[name] * factor).astype(out[name].dtype)
    return out
```

```python
from contextlib import ExitStack

import numpy as np

import concourse.bass as bass
from concourse import mybir

ALU = mybir.AluOpType
ACT = mybir.ActivationFunctionType
AX = mybir.AxisListType
F32 = mybir.dt.float32
F16 = mybir.dt.float16
BF16 = mybir.dt.bfloat16

P = 128
D = 128
T = 512
TB = T // P
H = 16
G = 4
HD0, DR = 8, 32
HD1 = 64
E0, S0 = 8, 64
HID = 512
HB = HID // P
E1 = 16
TOP = 8
EPS = 1e-5
ROUTE = 2.826
SHIFT = 256.0
K_ROPE = 3 * DR
K_MAX0 = K_ROPE + 3 * HD0
K_ALL0 = K_MAX0 + 1

MAX_UNITS = [(0, (0, 1, 2, 3)), (1, (0, 1)), (1, (2, 3))] + [(t, (h,)) for t in (2, 3) for h in range(4)]
NM = len(MAX_UNITS)
EXP0 = ([[(h, 0, 0)] for h in range(4)] + [[(h, 1, 0), (h, 3, 384)] for h in range(4)]
        + [[(h, 2, 0), (h + 1, 2, 256)] for h in (0, 2)])
PARTS0 = ((0, 4), (4, 8), (8, 10))
SM_BANKS, ST_BANKS = 3, 2


class Signal:

    def __init__(self, ctx, nc, name, per, begun=0):
        self.sem = ctx.enter_context(nc.semaphore(name))
        self.per, self.begun = per, begun

    def at(self, i, n):
        assert n + self.begun > 0
        return i * self.per + (n + self.begun)


class Fills:

    def __init__(self, plan):
        self.names = [n for n, _ in plan]
        self.reader = dict(plan)
        assert len(plan) == len(self.reader) and len(plan) % 2 == 0

    def count(self, reader):
        return sum(1 for n in self.names if self.reader[n] == reader)

    def index(self, name):
        return self.names.index(name)

    def reads(self, name):
        return sum(1 for n in self.names[:self.index(name) + 1] if self.reader[n] == self.reader[name])


def release(eng, passed):
    eng.sem_inc(passed, 1)


def rotary_tables():
    inv = np.float32(1.0) / np.float32(10000.0) ** (np.arange(0, DR, 2, dtype=np.float32) / np.float32(DR))
    angle = np.outer(np.arange(T, dtype=np.float32), inv).T
    cos, sin = np.cos(angle), np.sin(angle)
    rows = [np.concatenate([cos, cos]), np.concatenate([-sin, sin])]
    return [np.concatenate([x, x]).astype(np.float32) for x in rows]


LAYER0 = [("logits_s", 0), ("max", 0), ("dispatch", 0), ("turn_max", 0), ("heads", 0), ("logits_c", 0),
          ("turn_max", 1), ("heads", 1), ("heads_out", 0), ("experts", 0), ("turn_max", 2), ("heads", 2),
          ("heads_out", 1), ("combine", 0), ("turn_max", 3), ("heads", 3), ("heads_out", 2), ("last", 0),
          ("heads_out", 3)]


def layer0_fills():
    plan = [("xnT", "act"), ("xfT", "act"), ("ckv", "act"), ("q", "dve"), ("r", "dve"), ("k", "dve"),
            ("v", "act")]
    both = ("act", "dve")
    for stage, n in LAYER0:
        plan += {"logits_s": [(f"ls{b}", "act") for b in range(4)],
                 "dispatch": [(f"dT{t}", both[t % 2]) for t in range(4)] + [("slots", "act")],
                 "logits_c": [(f"lc{b}", "act") for b in range(4)],
                 "experts": [(f"h{b}", "act") for b in range(4)] + [("eo", "dve")],
                 "combine": [(f"cT{b}", both[b % 2]) for b in range(4)],
                 "turn_max": [(f"m{n}", "act")],
                 "heads_out": [(f"y{n}", "dve")]}.get(stage, [])
    return Fills(plan + [("atT", "act"), ("out", "act"), ("outT", "dve")])


def layer0(nc, a, x1_dram, batches):
    with ExitStack() as ctx:
        def sb(name, shape, dt=F32):
            return ctx.enter_context(nc.sbuf_tensor(name, shape, dt))

        def sig(name, per, begun=0):
            return Signal(ctx, nc, name, per, begun)

        def plain(name):
            return ctx.enter_context(nc.semaphore(name))

        stack_dram = nc.dram_tensor("stack_scratch", [2, H, 3 * HD0, T], F16, kind="Internal").ap()
        ps_max = ctx.enter_context(nc.psum_tensor("ps_max", [P, SM_BANKS, T], F32))
        ps_exp = ctx.enter_context(nc.psum_tensor("ps_exp", [P, ST_BANKS, T], F32))
        ps_out = ctx.enter_context(nc.psum_tensor("ps_out", [P, T], F32))
        ps_any = ctx.enter_context(nc.psum_tensor("ps_any", [P, 2, T], F32))

        ident = sb("ident", [P, P])
        ident_h = sb("ident_h", [P, P], BF16)
        mask = sb("mask", [P, P])
        mask_h = sb("mask_h", [P, P], BF16)
        cos = sb("cos", [2 * DR, T])
        sin = sb("sin", [2 * DR, T])
        w_kvd = sb("w_kvd", [P, D])
        w_q = sb("w_q", [P, D])
        w_k = sb("w_k", [P, D])
        w_v = sb("w_v", [P, D])
        w_o = sb("w_o", [P, D])
        w_qr = sb("w_qr", [P, 2, DR])
        w_kr = sb("w_kr", [P, 2, DR])
        gamma = sb("gamma", [P, D])
        slot_gamma = sb("slot_gamma", [P, D])
        w1 = sb("w1", [P, E0, HID])
        w2 = sb("w2", [P, E0, HB, D])
        b1 = sb("b1", [P, E0, HB])
        b2 = sb("b2", [P, E0 // 2, D])
        slot_nat = sb("slot_nat", [P, 4, D])
        slot_n = sb("slot_n", [P, 4, D])
        slot_ss = sb("slot_ss", [P, 4])
        slot_sm = sb("slot_sm", [P, 4])
        slot_r = sb("slot_r", [P, 4])
        snT = sb("snT", [P, T])
        neg_half = sb("neg_half", [P, 4])

        x_in = sb("x_in", [P, TB, D])
        x_res = sb("x_res", [P, TB, D])
        stats = sb("stats", [P, TB, 6])
        mv = sb("mv", [P, TB, 2])
        var_eps = sb("var_eps", [P, TB])
        rstd = sb("rstd", [P, TB])
        xn = sb("xn", [P, TB, D])
        squares = sb("squares", [P, TB, D])
        ss = sb("ss", [P, TB])
        ss_m = sb("ss_m", [P, TB])
        rnorm = sb("rnorm", [P, TB])
        xf = sb("xf", [P, TB, D])
        xnT = sb("xnT", [P, T])
        xfT = sb("xfT", [P, T])
        ckvT = sb("ckvT", [P, T])
        q_hi = sb("q_hi", [P, T], F16)
        q_lo = sb("q_lo", [P, T], F16)
        k_hi = sb("k_hi", [P, T], F16)
        k_lo = sb("k_lo", [P, T], F16)
        rot_a = sb("rot_a", [2 * DR, T])
        rot_b = sb("rot_b", [2 * DR, T])
        rot = sb("rot", [2 * DR, T])
        rot_hi = sb("rot_hi", [2 * DR, T], F16)
        rot_lo = sb("rot_lo", [2 * DR, T], F16)
        q_st = sb("q_st", [P, 2, G, T], F16)
        k_st = sb("k_st", [P, 2, G, T], F16)
        v_aug = sb("v_aug", [P, TB, H, DR])
        neg_max = sb("neg_max", [P, 2, G, TB])
        max_row = sb("max_row", [G * TB, 2, P], F16)
        probs = sb("probs", [P, len(EXP0), T])
        y_un = sb("y_un", [P, T])
        y_rec = sb("y_rec", [P, TB, G])
        attn = sb("attn", [P, TB, D])
        attnT = sb("attnT", [P, T])
        s_neg = sb("s_neg", [P, 4])
        s_sum = sb("s_sum", [P, 4])
        s_rec = sb("s_rec", [P, 4])
        c_neg = sb("c_neg", [P, 4])
        c_sum = sb("c_sum", [P, 4])
        c_rec = sb("c_rec", [P, 4])
        disp_s = sb("disp_s", [P, 4, T])
        disp_n = sb("disp_n", [P, TB, T])
        comb_n = disp_s
        comb_s = disp_n
        slotsT = sb("slotsT", [P, T])
        hT = sb("hT", [P, 4, HB, 2 * S0])
        eo = sb("eo", [P, 4, D])
        outT = sb("outT", [P, T])
        x1 = sb("x1", [P, TB, D])

        fills = layer0_fills()

        loaded, prep, prep_pool, prep_pe, prep_act = [plain(f"l0_{n}") for n in ("loaded", "prep", "prep_pool",
                                                                                 "prep_pe", "prep_act")]
        sp_passed, pool_passed, dve_passed = [plain(f"l0_{n}_passed") for n in ("sp", "pool", "dve")]
        x_loaded = sig("x_loaded", 16)
        res_loaded = sig("res_loaded", 16)
        scratch_in = sig("scratch_in", 16 * 6)
        stacked = sig("stacked", 16 * (2 * 6 + 2 * G))
        row_in = sig("row_in", 16 * G)
        stored = sig("l0_stored", 16, 16)
        stats_ok = sig("stats_ok", 2 * TB + 1)
        rstd_ok = sig("rstd_ok", 1)
        xn_ok = sig("xn_ok", TB, 1)
        ss_ok = sig("ss_ok", TB + 1)
        rnorm_ok = sig("rnorm_ok", 1)
        xf_ok = sig("xf_ok", TB)
        filled = sig("filled", len(fills.names))
        read = {"act": sig("read_act", fills.count("act"), 1), "dve": sig("read_dve", fills.count("dve"), 1)}
        hi_ok = sig("hi_ok", 2)
        rot_ok = sig("rot_ok", 4)
        max_full = sig("max_full", NM * G)
        max_read = sig("max_read", NM * G, 1)
        exp_full = sig("exp_full", 10 * G)
        exp_done = sig("exp_done", 10 * G, 1)
        masked = sig("masked", 4 * G)
        pv_done = sig("pv_done", 3 * G)
        pv_read = sig("pv_read", G, 1)
        rec_ok = sig("rec_ok", G)
        neg_ok = sig("neg_ok", 8)
        srec_ok = sig("srec_ok", 8)
        scaled = sig("scaled", 8)

        def emptied(eng, i, name):
            s = read[fills.reader[name]]
            eng.wait_ge(s.sem, s.at(i, fills.reads(name)))

        def full(eng, i, name):
            eng.wait_ge(filled.sem, filled.at(i, fills.index(name) + 1))
            return ps_any[:, fills.index(name) % 2]

        block = ctx.enter_context(nc.Block())

        rope = [(dst[:, n, c], a[src][:, s]) for dst, src in ((w_qr, "L0_attn_W_q_rope"), (w_kr, "L0_attn_W_k_rope"))
                for n, c, s in ((0, slice(0, DR), slice(0, DR)), (1, slice(0, DR // 2), slice(DR // 2, DR)),
                                (1, slice(DR // 2, DR), slice(0, DR // 2)))]
        loads = [(ident[:], a["ident"]), (mask[:], a["mask"]), (cos[:], a["cos"]), (sin[:], a["sin"]),
                 (slot_nat[:], a["L0_ffn_slot_embeds"].rearrange("e s d -> (e s) d").rearrange("(m p) d -> p m d", p=P)),
                 (slot_gamma[:], a["L0_ffn_slot_norm_gamma"].partition_broadcast(P)),
                 (gamma[:], a["L0_ffn_norm_gamma"].partition_broadcast(P)),
                 (w_kvd[:], a["L0_attn_W_kv_down"]), (w_q[:], a["L0_attn_W_q"]), (w_k[:], a["L0_attn_W_k_up"]),
                 (w_v[:], a["L0_attn_W_v_up"]), (w_o[:], a["L0_attn_W_o"])] + rope + [
                 (b1[:], a["L0_ffn_b1"]),
                 (w1[:], a["L0_ffn_w1"].rearrange("e d h -> d e h")),
                 (w2[:], a["L0_ffn_w2"].rearrange("e (b p) d -> p e b d", p=P))]
        loads += [(b2[S0 * (e % 2):S0 * (e % 2) + S0, e // 2, :], a["L0_ffn_b2"][e].partition_broadcast(S0))
                  for e in range(E0)]
        all_loaded = 16 * len(loads)

        @block.sync
        def _(sp):
            for dst, src in loads:
                sp.dma_start(dst, src).then_inc(loaded, 16)
            with sp.Fori(0, batches) as i:
                sp.wait_ge(xn_ok.sem, xn_ok.at(i, 0))
                release(sp, sp_passed)
                sp.dma_start(x_in[:], a["L0_attn_x"][i].rearrange("(t p) d -> p t d", p=P)).then_inc(x_loaded.sem, 16)
                sp.wait_ge(read["dve"].sem, read["dve"].at(i, 0))
                release(sp, sp_passed)
                sp.dma_start(x_res[:], a["L0_attn_x"][i].rearrange("(t p) d -> p t d", p=P)).then_inc(res_loaded.sem, 16)
                for side, name, parts in ((0, "q", (q_hi, q_lo, q_hi)), (1, "k", (k_hi, k_hi, k_lo))):
                    emptied(sp, i, name)
                    for n in range(3):
                        sp.dma_start(stack_dram[side, :, n * HD0:(n + 1) * HD0, :], parts[n][:]
                                     ).then_inc(scratch_in.sem, 16)
                    if side == 0:
                        sp.wait_ge(rot_ok.sem, rot_ok.at(i, 4))
                        for s in range(2):
                            for n, (qp, kp) in enumerate(((rot_hi, rot_hi), (rot_lo, rot_hi), (rot_hi, rot_lo))):
                                for st, src in ((q_st, qp[0:DR]), (k_st, kp[DR:2 * DR])):
                                    sp.dma_start(st[n * DR:(n + 1) * DR, s], src.unsqueeze(1).to_broadcast([DR, G, T])
                                                 ).then_inc(stacked.sem, 16)
                sp.wait_ge(scratch_in.sem, scratch_in.at(i, 16 * 6))

                def heads_rows(g):
                    for side, st in ((0, q_st), (1, k_st)):
                        sp.dma_start(st[K_ROPE:K_MAX0, g % 2],
                                     stack_dram[side, G * g:G * g + G].rearrange("h r t -> r h t")
                                     ).then_inc(stacked.sem, 16)

                def max_rows(g):
                    emptied(sp, i, f"m{g}")
                    sp.dma_start(q_st[K_MAX0:K_ALL0, g % 2], max_row[:, g % 2]).then_inc(row_in.sem, 16)

                heads_rows(0)
                heads_rows(1)
                for g in range(G):
                    max_rows(g)
                    if g + 2 < G:
                        sp.wait_ge(exp_full.sem, exp_full.at(i, 10 * (g + 1)))
                        heads_rows(g + 2)

        @block.gpsimd
        def _(pool):
            nc.gpsimd.memset(neg_half[:], -0.5).then_inc(prep_pool, 1)
            pool.wait_ge(prep, 7)
            pool.wait_ge(prep_pool, 1)
            nc.gpsimd.tensor_tensor(slot_r[:], slot_sm[:], neg_half[:], ALU.pow).then_inc(prep_pool, 1)
            with pool.Fori(0, batches) as i:
                pool.wait_ge(stats_ok.sem, stats_ok.at(i, 2 * TB + 1))
                nc.gpsimd.tensor_tensor(rstd[:], var_eps[:], neg_half[:], ALU.pow).then_inc(rstd_ok.sem, 1)
                pool.wait_ge(ss_ok.sem, ss_ok.at(i, TB + 1))
                nc.gpsimd.tensor_tensor(rnorm[:], ss_m[:], neg_half[:], ALU.pow).then_inc(rnorm_ok.sem, 1)

                def scale(w, rec, n):
                    for b in range(4):
                        pool.wait_ge(srec_ok.sem, srec_ok.at(i, n + b + 1))
                        release(pool, pool_passed)
                        nc.gpsimd.tensor_scalar(w[:, b], w[:, b], rec[:, b:b + 1], None, ALU.mult
                                                ).then_inc(scaled.sem, 1)

                def heads(g):
                    late = probs[:, 8:10].rearrange("p u (c q) -> p (u c) q", q=2 * P)
                    for last, v in ((4, probs[:, 0:4, 0:P]), (8, probs[:, 4:8, 0:P]), (8, probs[:, 4:8, 3 * P:T]),
                                    (10, late[:, :, 0:P])):
                        pool.wait_ge(exp_done.sem, exp_done.at(i, 10 * g + last))
                        release(pool, pool_passed)
                        nc.gpsimd.affine_select(out=v, in_=v, compare_op=ALU.is_ge, fill=0.0, base=0,
                                                pattern=[[0, 4], [1, P]], channel_multiplier=-1).then_inc(masked.sem, 1)

                for stage, n in LAYER0:
                    if stage == "dispatch":
                        scale(disp_s, s_rec, 0)
                    if stage == "experts":
                        scale(comb_n, c_rec, 4)
                    if stage == "heads":
                        heads(n)

        @block.scalar
        def _(act):
            for s in (read["act"], exp_done, pv_read, stored):
                act.sem_inc(s.sem, s.begun)
            act.wait_ge(prep_pe, 1)
            nc.scalar.activation(snT[:], ps_any[:, 0], ACT.Copy).then_inc(prep_act, 1)
            act.wait_ge(prep, 13)
            act.wait_ge(loaded, all_loaded)
            with act.Fori(0, batches) as i:
                def copy(name, dst):
                    nc.scalar.activation(dst, full(act, i, name), ACT.Copy).then_inc(read["act"].sem, 1)

                def softmax(b, name, neg, w, sums, n):
                    act.wait_ge(neg_ok.sem, neg_ok.at(i, n + b + 1))
                    nc.scalar.activation(w[:, b], full(act, i, name), ACT.Exp, bias=neg[:, b:b + 1],
                                         accum_out=sums[:, b:b + 1]).then_inc(read["act"].sem, 1)

                copy("xnT", xnT[:])
                copy("xfT", xfT[:])
                copy("ckv", ckvT[:])
                for name, dst in (("q", q_hi), ("k", k_hi)):
                    nc.scalar.activation(dst[:], full(act, i, name), ACT.Copy).then_inc(hi_ok.sem, 1)
                nc.scalar.activation(v_aug[:, :, :, 0:HD0], full(act, i, "v").rearrange("p (t h d) -> p t h d", t=TB, h=H),
                                     ACT.Copy).then_inc(read["act"].sem, 1)

                def heads(g):
                    for u in range(10):
                        n = 10 * g + u
                        if u == 4 and g >= 1:
                            out_rows(g - 1)
                        part = (0 if u < 4 else 1 if u < 8 else 2)
                        if g >= 1:
                            act.wait_ge(pv_done.sem, pv_done.at(i, 3 * (g - 1) + part + 1))
                        act.wait_ge(exp_full.sem, exp_full.at(i, n + 1))
                        nc.scalar.activation(probs[:, u], ps_exp[:, n % ST_BANKS], ACT.Exp,
                                             scale=float(HD0 + DR) ** -0.5).then_inc(exp_done.sem, 1)

                def out_rows(g):
                    act.wait_ge(pv_done.sem, pv_done.at(i, 3 * g + 3))
                    if g >= 1:
                        act.wait_ge(filled.sem, filled.at(i, fills.index(f"y{g - 1}") + 1))
                    nc.scalar.activation(y_un[:], ps_out[:], ACT.Copy).then_inc(pv_read.sem, 1)

                for stage, n in LAYER0:
                    if stage == "logits_s":
                        for b in range(4):
                            softmax(b, f"ls{b}", s_neg, disp_s, s_sum, 0)
                    if stage == "dispatch":
                        for t in (0, 2):
                            copy(f"dT{t}", disp_n[:, t])
                        copy("slots", slotsT[:])
                    if stage == "turn_max":
                        nc.scalar.activation(max_row[:, n % 2], full(act, i, f"m{n}")[0:G * TB, 0:P], ACT.Copy,
                                             scale=1.0 / SHIFT).then_inc(read["act"].sem, 1)
                    if stage == "heads":
                        heads(n)
                    if stage == "last":
                        out_rows(G - 1)
                    if stage == "logits_c":
                        for b in range(4):
                            softmax(b, f"lc{b}", c_neg, comb_n, c_sum, 4)
                    if stage == "experts":
                        for b in range(4):
                            bank = full(act, i, f"h{b}")
                            for hb in range(HB):
                                for ee in range(2):
                                    c = (hb * 2 + ee) * S0
                                    ins = nc.scalar.activation(hT[:, b, hb, ee * S0:ee * S0 + S0], bank[:, c:c + S0],
                                                               ACT.Gelu, bias=b1[:, 2 * b + ee, hb:hb + 1])
                            ins.then_inc(read["act"].sem, 1)
                    if stage == "combine":
                        for b in (0, 2):
                            copy(f"cT{b}", comb_s[:, b])
                copy("atT", attnT[:])
                copy("out", outT[:])
                emptied(act, i, "outT")
                act.dma_start(x1_dram[i].rearrange("(t p) d -> p t d", p=P), x1[:]).then_inc(stored.sem, 16)
            act.wait_ge(stored.sem, 16 * batches + 16)

        @block.vector
        def _(dve):
            for s in (read["dve"], xn_ok, max_read):
                dve.sem_inc(s.sem, s.begun)
            nc.vector.memset(v_aug[:], 0.0).then_inc(prep, 1)
            nc.vector.memset(k_st[K_ROPE:P], SHIFT).then_inc(prep, 1)
            dve.wait_ge(loaded, all_loaded)
            for b in range(4):
                nc.vector.tensor_tensor_reduce(squares[:, b], slot_nat[:, b], slot_nat[:, b], 1.0 / D, 0.0, ALU.mult,
                                               ALU.add, slot_ss[:, b:b + 1]).then_inc(prep, 1)
            dve.wait_ge(prep, 6)
            nc.vector.tensor_scalar(slot_sm[:], slot_ss[:], 1e-24 / D, None, ALU.max).then_inc(prep, 1)
            dve.wait_ge(prep_pool, 2)
            for b in range(4):
                nc.vector.scalar_tensor_tensor(out=slot_n[:, b], in0=slot_nat[:, b], scalar=slot_r[:, b:b + 1],
                                               in1=slot_gamma[:], op0=ALU.mult, op1=ALU.mult).then_inc(prep, 1)
            nc.vector.tensor_copy(ident_h[:], ident[:]).then_inc(prep, 1)
            dve.wait_ge(prep, 12)
            nc.vector.memset(v_aug[:, :, :, HD0:HD0 + 1], 1.0).then_inc(prep, 1)
            nc.vector.tensor_copy(mask_h[:], mask[:]).then_inc(prep, 1)

            with dve.Fori(0, batches) as i:
                dve.wait_ge(x_loaded.sem, x_loaded.at(i, 16))
                for t in range(TB):
                    nc.vector.bn_stats(stats[:, t], x_in[:, t]).then_inc(stats_ok.sem, 1)
                dve.wait_ge(stats_ok.sem, stats_ok.at(i, TB))
                release(dve, dve_passed)
                for t in range(TB):
                    nc.vector.bn_aggr(mv[:, t], stats[:, t]).then_inc(stats_ok.sem, 1)
                dve.wait_ge(stats_ok.sem, stats_ok.at(i, 2 * TB))
                nc.vector.tensor_scalar(var_eps[:], mv[:, :, 1], EPS, None, ALU.add).then_inc(stats_ok.sem, 1)
                dve.wait_ge(rstd_ok.sem, rstd_ok.at(i, 1))
                for t in range(TB):
                    nc.vector.tensor_scalar(xn[:, t], x_in[:, t], mv[:, t, 0:1], rstd[:, t:t + 1], ALU.subtract,
                                            ALU.mult).then_inc(xn_ok.sem, 1)
                for t in range(TB):
                    dve.wait_ge(xn_ok.sem, xn_ok.at(i, t + 1))
                    nc.vector.tensor_tensor_reduce(squares[:, t], xn[:, t], xn[:, t], 1.0 / D, 0.0, ALU.mult, ALU.add,
                                                   ss[:, t:t + 1]).then_inc(ss_ok.sem, 1)
                dve.wait_ge(ss_ok.sem, ss_ok.at(i, TB))
                nc.vector.tensor_scalar(ss_m[:], ss[:], 1e-24 / D, None, ALU.max).then_inc(ss_ok.sem, 1)
                dve.wait_ge(rnorm_ok.sem, rnorm_ok.at(i, 1))
                for t in range(TB):
                    nc.vector.scalar_tensor_tensor(out=xf[:, t], in0=xn[:, t], scalar=rnorm[:, t:t + 1], in1=gamma[:],
                                                   op0=ALU.mult, op1=ALU.mult).then_inc(xf_ok.sem, 1)

                def low_part(name, n, hi, lo):
                    dve.wait_ge(hi_ok.sem, hi_ok.at(i, n))
                    nc.vector.tensor_tensor(lo[:], full(dve, i, name), hi[:], ALU.subtract).then_inc(read["dve"].sem, 1)

                low_part("q", 1, q_hi, q_lo)
                bank = full(dve, i, "r")
                nc.vector.tensor_tensor(rot_a[:], bank[0:2 * DR], cos[:], ALU.mult).then_inc(rot_ok.sem, 1)
                nc.vector.tensor_tensor(rot_b[:], bank[2 * DR:P], sin[:], ALU.mult).then_inc(read["dve"].sem, 1)
                dve.wait_ge(rot_ok.sem, rot_ok.at(i, 1))
                emptied(dve, i, "r")
                nc.vector.tensor_tensor(rot[:], rot_a[:], rot_b[:], ALU.add).then_inc(rot_ok.sem, 1)
                dve.wait_ge(rot_ok.sem, rot_ok.at(i, 2))
                nc.vector.tensor_copy(rot_hi[:], rot[:]).then_inc(rot_ok.sem, 1)
                dve.wait_ge(rot_ok.sem, rot_ok.at(i, 3))
                nc.vector.tensor_tensor(rot_lo[:], rot[:], rot_hi[:], ALU.subtract).then_inc(rot_ok.sem, 1)
                low_part("k", 2, k_hi, k_lo)

                def bank_max(b, name, neg):
                    nc.vector.tensor_reduce(neg[:, b:b + 1], full(dve, i, name), AX.X, ALU.max, negate=True
                                            ).then_inc(neg_ok.sem, 1)

                def row_max(g):
                    if g >= 2:
                        dve.wait_ge(filled.sem, filled.at(i, fills.index(f"m{g - 2}") + 1))
                    for u, (t, heads) in enumerate(MAX_UNITS):
                        n = NM * g + u
                        k = len(heads)
                        dve.wait_ge(max_full.sem, max_full.at(i, n + 1))
                        src = ps_max[:, n % SM_BANKS, 0:k * (t + 1) * P].rearrange("p (h k) -> p h k", h=k)
                        nc.vector.tensor_reduce(neg_max[:, g % 2, heads[0]:heads[0] + k, t], src, AX.X, ALU.max,
                                                negate=True).then_inc(max_read.sem, 1)

                def heads_out(g):
                    bank = full(dve, i, f"y{g}").rearrange("p (t s c) -> p t s c", t=TB, s=G)
                    if g >= 1:
                        emptied(dve, i, f"y{g - 1}")
                    nc.vector.reciprocal(y_rec[:], bank[:, :, :, HD0]).then_inc(rec_ok.sem, 1)
                    dve.wait_ge(rec_ok.sem, rec_ok.at(i, g + 1))
                    nc.vector.tensor_tensor(attn[:, :, g * 32:g * 32 + 32].rearrange("p t (s d) -> p t s d", s=G),
                                            bank[:, :, :, 0:HD0], y_rec[:].unsqueeze(3).to_broadcast([P, TB, G, HD0]),
                                            ALU.mult).then_inc(read["dve"].sem, 1)

                for stage, n in LAYER0:
                    if stage == "logits_s":
                        for b in range(4):
                            bank_max(b, f"ls{b}", s_neg)
                    if stage == "dispatch":
                        for b in range(4):
                            emptied(dve, i, f"ls{b}")
                            nc.vector.reciprocal(s_rec[:, b:b + 1], s_sum[:, b:b + 1]).then_inc(srec_ok.sem, 1)
                        for t in (1, 3):
                            nc.vector.tensor_copy(disp_n[:, t], full(dve, i, f"dT{t}")).then_inc(read["dve"].sem, 1)
                    if stage == "max":
                        row_max(n)
                    if stage == "heads" and n + 1 < G:
                        row_max(n + 1)
                    if stage == "logits_c":
                        for b in range(4):
                            bank_max(b, f"lc{b}", c_neg)
                    if stage == "heads_out":
                        heads_out(n)
                    if stage == "experts":
                        for b in range(4):
                            emptied(dve, i, f"lc{b}")
                            nc.vector.reciprocal(c_rec[:, b:b + 1], c_sum[:, b:b + 1]).then_inc(srec_ok.sem, 1)
                        nc.vector.tensor_tensor(eo[:].rearrange("p m d -> p (m d)"), full(dve, i, "eo"),
                                                b2[:].rearrange("p m d -> p (m d)"), ALU.add).then_inc(read["dve"].sem, 1)
                    if stage == "combine":
                        for b in (1, 3):
                            nc.vector.tensor_copy(comb_s[:, b], full(dve, i, f"cT{b}")).then_inc(read["dve"].sem, 1)
                dve.wait_ge(res_loaded.sem, res_loaded.at(i, 16))
                dve.wait_ge(stored.sem, stored.at(i, 0))
                nc.vector.tensor_tensor(x1[:].rearrange("p t d -> p (t d)"), full(dve, i, "outT"),
                                        x_res[:].rearrange("p t d -> p (t d)"), ALU.add).then_inc(read["dve"].sem, 1)

        @block.tensor
        def _(pe):
            pe.wait_ge(loaded, all_loaded)
            pe.wait_ge(prep, 14)
            for b in range(4):
                ins = pe.transpose(ps_any[:, 0, b * P:b * P + P], slot_n[:, b], ident[:])
            ins.then_inc(prep_pe, 1)
            pe.wait_ge(prep_act, 1)
            with pe.Fori(0, batches) as i:
                def bank(name):
                    k = fills.index(name)
                    if k >= 2:
                        emptied(pe, i, fills.names[k - 2])
                    else:
                        for s in read.values():
                            pe.wait_ge(s.sem, s.at(i, 0))
                    return ps_any[:, k % 2]

                def turn(name, blocks):
                    out = bank(name)
                    for b, src in enumerate(blocks):
                        ins = pe.transpose(out[:, b * P:b * P + P], src, ident[:])
                    ins.then_inc(filled.sem, 1)

                def product(name, w, x, n=P):
                    pe.matmul(bank(name)[0:n], w, x, start=True, stop=True).then_inc(filled.sem, 1)

                pe.wait_ge(xn_ok.sem, xn_ok.at(i, TB))
                turn("xnT", [xn[:, t] for t in range(TB)])
                pe.wait_ge(xf_ok.sem, xf_ok.at(i, TB))
                turn("xfT", [xf[:, t] for t in range(TB)])
                emptied(pe, i, "xnT")
                product("ckv", w_kvd[:], xnT[:])
                product("q", w_q[:], xnT[:])
                emptied(pe, i, "ckv")
                out = bank("r")
                for n in range(2):
                    pe.matmul(out[2 * n * DR:(2 * n + 1) * DR], w_qr[:, n], xnT[:], start=True, stop=True)
                    ins = pe.matmul(out[(2 * n + 1) * DR:(2 * n + 2) * DR], w_kr[:, n], ckvT[:], start=True, stop=True)
                ins.then_inc(filled.sem, 1)
                product("k", w_k[:], ckvT[:])
                out = bank("v")
                for t in range(TB):
                    ins = pe.matmul(out[:, t * P:t * P + P], ckvT[:, t * P:t * P + P], w_v[:], start=True, stop=True)
                ins.then_inc(filled.sem, 1)

                def max_unit(g, u):
                    t, heads = MAX_UNITS[u]
                    n = NM * g + u
                    w = (t + 1) * P
                    if u == 0:
                        pe.wait_ge(stacked.sem, stacked.at(i, 16 * (12 + 2 * max(g + 1, 2))))
                    pe.wait_ge(max_read.sem, max_read.at(i, max(n + 1 - SM_BANKS, 0)))
                    for c, h in enumerate(heads):
                        out = ps_max[:, n % SM_BANKS, c * w:c * w + w]
                        pe.matmul(out, q_st[0:K_MAX0, g % 2, h, t * P:t * P + P], k_st[0:K_MAX0, g % 2, h, 0:w],
                                  start=True, stop=False)
                        ins = pe.matmul(out[:, t * P:w], ident_h[:], mask_h[:], start=False, stop=True)
                    ins.then_inc(max_full.sem, 1)

                def exp_unit(g, u):
                    n = 10 * g + u
                    if u == 0:
                        pe.wait_ge(row_in.sem, row_in.at(i, 16 * (g + 1)))
                    pe.wait_ge(exp_done.sem, exp_done.at(i, max(n + 1 - ST_BANKS, 0)))
                    for h, j, c in EXP0[u]:
                        w = T - j * P
                        ins = pe.matmul(ps_exp[:, n % ST_BANKS, c:c + w], k_st[0:K_ALL0, g % 2, h, j * P:j * P + P],
                                        q_st[0:K_ALL0, g % 2, h, j * P:T], start=True, stop=True)
                    ins.then_inc(exp_full.sem, 1)

                def values(g, part):
                    pe.wait_ge(masked.sem, masked.at(i, 4 * g + (1, 3, 4)[part]))
                    if part == 0:
                        pe.wait_ge(pv_read.sem, pv_read.at(i, g))
                        emptied(pe, i, "v")
                    first, last = PARTS0[part]
                    pieces = [(u, h, j, c) for u in range(first, last) for h, j, c in EXP0[u]]
                    pieces.sort(key=lambda x: (x[2], x[1]))
                    for u, h, j, c in pieces:
                        w = T - j * P
                        ins = pe.matmul(ps_out[32 * h:32 * h + 32, j * P:T], v_aug[:, j, G * g + h],
                                        probs[:, u, c:c + w], start=(part == 0), stop=(part == 2))
                    ins.then_inc(pv_done.sem, 1)

                def heads(g):
                    turns = list(range(NM)) if g + 1 < G else []
                    for part, (first, last) in enumerate(PARTS0):
                        for u in range(first, last):
                            exp_unit(g, u)
                            for _ in range(2 if u % 4 == 3 else 1):
                                if turns:
                                    max_unit(g + 1, turns.pop(0))
                        if 3 * g + part >= 1:
                            values(*divmod(3 * g + part - 1, 3))
                    while turns:
                        max_unit(g + 1, turns.pop(0))

                for stage, n in LAYER0:
                    if stage == "logits_s":
                        emptied(pe, i, "xfT")
                        for b in range(4):
                            product(f"ls{b}", snT[:, b * P:b * P + P], xfT[:])
                    if stage == "max":
                        for u in range(NM):
                            max_unit(n, u)
                    if stage == "turn_max":
                        pe.wait_ge(max_read.sem, max_read.at(i, NM * (n + 1)))
                        pe.transpose(bank(f"m{n}")[0:G * TB, 0:P], neg_max[:, n % 2].rearrange("p h t -> p (h t)"),
                                     ident[:]).then_inc(filled.sem, 1)
                    if stage == "heads":
                        heads(n)
                    if stage == "last":
                        values(G - 1, 2)
                    if stage == "heads_out":
                        pe.wait_ge(pv_read.sem, pv_read.at(i, n + 1))
                        turn(f"y{n}", [y_un[:, t * P:t * P + P] for t in range(TB)])
                    if stage == "dispatch":
                        pe.wait_ge(scaled.sem, scaled.at(i, 4))
                        for t in range(TB):
                            turn(f"dT{t}", [disp_s[:, b, t * P:t * P + P] for b in range(4)])
                        out = bank("slots")
                        for t in range(TB):
                            emptied(pe, i, f"dT{t}")
                            ins = pe.matmul(out, xf[:, t], disp_n[:, t], start=(t == 0), stop=(t == TB - 1))
                        ins.then_inc(filled.sem, 1)
                    if stage == "logits_c":
                        for b in range(4):
                            product(f"lc{b}", xfT[:, b * P:b * P + P], snT[:])
                    if stage == "experts":
                        emptied(pe, i, "slots")
                        for b in range(4):
                            out = bank(f"h{b}")
                            for hb in range(HB):
                                for ee in range(2):
                                    c, e = (hb * 2 + ee) * S0, 2 * b + ee
                                    ins = pe.matmul(out[:, c:c + S0], w1[:, e, hb * P:hb * P + P],
                                                    slotsT[:, e * S0:e * S0 + S0], start=True, stop=True)
                            ins.then_inc(filled.sem, 1)
                        out = bank("eo")
                        for b in range(4):
                            emptied(pe, i, f"h{b}")
                            for hb in range(HB):
                                for ee in range(2):
                                    ins = pe.matmul(out[S0 * ee:S0 * ee + S0, b * D:b * D + D],
                                                    hT[:, b, hb, ee * S0:ee * S0 + S0], w2[:, 2 * b + ee, hb],
                                                    start=(hb == 0), stop=(hb == HB - 1))
                        ins.then_inc(filled.sem, 1)
                    if stage == "combine":
                        pe.wait_ge(scaled.sem, scaled.at(i, 8))
                        for b in range(4):
                            turn(f"cT{b}", [comb_n[:, t, b * P:b * P + P] for t in range(TB)])
                emptied(pe, i, f"y{G - 1}")
                turn("atT", [attn[:, t] for t in range(TB)])
                out = bank("out")
                emptied(pe, i, "eo")
                for b in range(4):
                    emptied(pe, i, f"cT{b}")
                    pe.matmul(out, eo[:, b], comb_s[:, b], start=(b == 0), stop=False)
                emptied(pe, i, "atT")
                pe.matmul(out, w_o[:], attnT[:], start=False, stop=True).then_inc(filled.sem, 1)
                emptied(pe, i, "out")
                turn("outT", [outT[:, t * P:t * P + P] for t in range(TB)])


EXP1 = [[(0, 0, 0)], [(1, 0, 0)], [(0, 1, 0), (0, 3, 384)], [(1, 1, 0), (1, 3, 384)], [(0, 2, 0), (1, 2, 256)]]
K_B = HD1 + 1
PAIRS = H // 2
CHUNK = 4

LAYER1 = [("qk", 0), ("values_in", 0), ("max", 0), ("route", 0), ("qk", 1), ("turn_max", 0), ("heads", 0),
          ("moe", 0), ("qk", 2), ("turn_max", 1), ("heads", 1), ("sums", 0),
          ("moe", 1), ("qk", 3), ("turn_max", 2), ("heads", 2), ("sums", 1),
          ("moe", 2), ("turn_max", 3), ("heads", 3), ("sums", 2), ("moe", 3), ("last", 0), ("sums", 3), ("moe", 4)]


def experts_of(chunk):
    return range(CHUNK * chunk, min(CHUNK * chunk + CHUNK, E1 + 1))


def layer1_fills():
    plan = [("xnT", "act"), ("lat", "act"), ("gate", "act")]
    for stage, n in LAYER1:
        if stage == "moe":
            plan += [(f"{x}{e}", "dve") for e in experts_of(n) for x in "gu"] + [(f"d{n - 1}", "dve")] * (n >= 1)
        else:
            plan += {"qk": [(f"{x}{2 * n + r}", "dve") for x in "qk" for r in range(2)],
                     "values_in": [(f"v{t}{half}", "act") for t in range(TB) for half in range(2)],
                     "route": [("cT", "act")],
                     "turn_max": [(f"m{n}", "act")],
                     "sums": [(f"s{n}", "dve")]}.get(stage, [])
    return Fills(plan + [("out", "dve"), ("outT", "dve")])


def layer1(nc, a, x1_dram, out_dram, batches):
    with ExitStack() as ctx:
        def sb(name, shape, dt=F32):
            return ctx.enter_context(nc.sbuf_tensor("l1_" + name, shape, dt))

        def sig(name, per, begun=0):
            return Signal(ctx, nc, "l1_" + name, per, begun)

        def plain(name):
            return ctx.enter_context(nc.semaphore("l1_" + name))

        route_dram = nc.dram_tensor("route_scratch", [E1, T], F32, kind="Internal").ap()
        rec_dram = nc.dram_tensor("rec_scratch", [G, G, T], F32, kind="Internal").ap()
        ps_max = ctx.enter_context(nc.psum_tensor("l1_ps_max", [P, SM_BANKS, T], F32))
        ps_exp = ctx.enter_context(nc.psum_tensor("l1_ps_exp", [P, ST_BANKS, T], F32))
        ps_out = ctx.enter_context(nc.psum_tensor("l1_ps_out", [P, T], F32))
        ps_any = ctx.enter_context(nc.psum_tensor("l1_ps_any", [P, 2, T], F32))

        ident = sb("ident", [P, P])
        ident_h = sb("ident_h", [P, P], BF16)
        masks = sb("masks", [P, 2, P])
        masks_h = sb("masks_h", [P, 2, P], BF16)
        w_kvd = sb("w_kvd", [P, D])
        w_kvu = sb("w_kvu", [P, 2, H * HD1])
        w_q = sb("w_q", [P, H * HD1])
        w_out = sb("w_out", [P, PAIRS, D])
        gate_w = sb("gate_w", [P, E1])
        bias = sb("bias", [P, E1])
        w_g = sb("w_g", [P, E1 + 1, D])
        w_u = sb("w_u", [P, E1 + 1, D])
        w_d = sb("w_d", [P, E1 + 1, D])
        one_col = sb("one_col", [P, G, 32])
        neg_half = sb("neg_half", [P, TB])

        x_in = sb("x_in", [P, TB, D])
        x_res = sb("x_res", [P, TB, D])
        stats = sb("stats", [P, TB, 6])
        mv = sb("mv", [P, TB, 2])
        var_eps = sb("var_eps", [P, TB])
        rstd = sb("rstd", [P, TB])
        xn = sb("xn", [P, TB, D])
        xnT = sb("xnT", [P, T])
        latT = sb("latT", [P, T])
        q_hi = sb("q_hi", [P, 2, T], F16)
        q_lo = sb("q_lo", [P, 2, T], F16)
        k_hi = sb("k_hi", [P, 2, T], F16)
        k_lo = sb("k_lo", [P, 2, T], F16)
        q_a = sb("q_a", [P, 2, G, T], F16)
        k_a = sb("k_a", [P, 2, G, T], F16)
        q_b = sb("q_b", [P, 2, G, T], F16)
        k_b = sb("k_b", [P, 2, G, T], F16)
        v = sb("v", [P, TB, H * HD1])
        neg_max = sb("neg_max", [P, 2, G, TB])
        max_row = sb("max_row", [G * TB, 2, P], F16)
        probs = sb("probs", [P, 2, 5, T])
        key_sum = sb("key_sum", [P, G, T])
        yT = sb("yT", [P, PAIRS, T])
        sums = sb("sums", [P, T])
        rec = sb("rec", [P, T])
        spread = sb("spread", [P, 2, CHUNK, T])
        th = sb("th", [P, TB, E1])
        score = sb("score", [P, TB, E1])
        select = sb("select", [P, TB, E1])
        top = sb("top", [P, TB, TOP])
        rest = sb("rest", [P, TB, E1])
        keep = sb("keep", [P, TB, E1])
        kept = sb("kept", [P, TB, E1])
        kept_sum = sb("kept_sum", [P, TB])
        kept_rec = sb("kept_rec", [P, TB])
        weight = sb("weight", [P, TB, E1])
        weightT = sb("weightT", [E1, T])
        tanh = sb("tanh", [P, 2, T])
        gated = sb("gated", [P, T])
        hidden = sb("hidden", [P, 2, T])
        hw = sb("hw", [P, 2, CHUNK, T])
        acc = sb("acc", [P, T])
        outT = gated

        fills = layer1_fills()

        loaded, prep, prep_pool = [plain(n) for n in ("loaded", "prep", "prep_pool")]
        sp_passed, pool_passed, dve_passed = [plain(f"{n}_passed") for n in ("sp", "pool", "dve")]
        x_loaded = sig("x_loaded", 16)
        res_loaded = sig("res_loaded", 16)
        stacked = sig("stacked", 16 * 12 * G)
        row_in = sig("row_in", 16 * G)
        route_out = sig("route_out", 16)
        spread_in = sig("spread_in", 16 * E1 // CHUNK)
        rec_out = sig("rec_out", 16 * G)
        rec_in = sig("rec_in", 16 * G)
        stored = sig("stored", 16, 16)
        stats_ok = sig("stats_ok", 2 * TB + 1)
        rstd_ok = sig("rstd_ok", 1)
        xn_ok = sig("xn_ok", TB, 1)
        filled = sig("filled", len(fills.names))
        read = {"act": sig("read_act", fills.count("act"), 1), "dve": sig("read_dve", fills.count("dve"), 1)}
        hi_ok = sig("hi_ok", 4 * G)
        max_full = sig("max_full", NM * G)
        max_read = sig("max_read", NM * G, 1)
        exp_full = sig("exp_full", 5 * PAIRS)
        exp_done = sig("exp_done", 5 * PAIRS, 1)
        added = sig("added", 4 * PAIRS)
        pv_done = sig("pv_done", PAIRS)
        pv_read = sig("pv_read", PAIRS, 1)
        rec_ok = sig("rec_ok", 1)
        normed = sig("normed", PAIRS)
        route_ok = sig("route_ok", 15)
        tanh_ok = sig("tanh_ok", E1 + 1)
        hw_ok = sig("hw_ok", E1 + 1)

        def emptied(eng, i, name):
            s = read[fills.reader[name]]
            eng.wait_ge(s.sem, s.at(i, fills.reads(name)))

        def full(eng, i, name):
            eng.wait_ge(filled.sem, filled.at(i, fills.index(name) + 1))
            return ps_any[:, fills.index(name) % 2]

        def chunk_done(eng, i, chunk):
            eng.wait_ge(filled.sem, filled.at(i, fills.index(f"d{chunk}") + 1))

        block = ctx.enter_context(nc.Block())

        loads = [(ident[:], a["ident"]), (masks[:, 0], a["mask"]), (masks[:, 1], a["maskT"]),
                 (w_kvd[:], a["L1_attn_w_kv_down"]), (gate_w[:], a["L1_ffn_gate_w"]),
                 (bias[:], a["L1_ffn_expert_bias"].partition_broadcast(P)), (w_q[:], a["L1_attn_w_q"]),
                 (w_kvu[:], a["L1_attn_w_kv_up"].rearrange("p (s n) -> p s n", s=2)),
                 (w_out[:], a["L1_attn_w_out"].rearrange("(k p) d -> p k d", p=P))]
        for w, name in ((w_g, "gate"), (w_u, "up"), (w_d, "down")):
            loads += [(w[:, 0:E1], a[f"L1_ffn_w_{name}"]), (w[:, E1], a[f"L1_ffn_shared_{name}_w"])]
        all_loaded = 16 * len(loads)

        @block.sync
        def _(sp):
            for dst, src in loads:
                sp.dma_start(dst, src).then_inc(loaded, 16)
            with sp.Fori(0, batches) as i:
                sp.wait_ge(xn_ok.sem, xn_ok.at(i, 0))
                release(sp, sp_passed)
                sp.dma_start(x_in[:], x1_dram[i].rearrange("(t p) d -> p t d", p=P)).then_inc(x_loaded.sem, 16)
                sp.wait_ge(stored.sem, stored.at(i, 0))
                release(sp, sp_passed)
                sp.dma_start(x_res[:], x1_dram[i].rearrange("(t p) d -> p t d", p=P)).then_inc(res_loaded.sem, 16)

                def stack(g):
                    emptied(sp, i, f"k{2 * g + 1}")
                    s = g % 2
                    if g >= 2:
                        release(sp, sp_passed)
                        sp.wait_ge(exp_full.sem, exp_full.at(i, 10 * (g - 1)))
                    for r in range(2):
                        rows = slice(HD1 * r, HD1 * r + HD1)
                        for dst, to, src in ((q_a, 0, q_hi), (q_a, HD1, q_hi), (k_a, 0, k_hi), (k_a, HD1, k_lo),
                                             (q_b, 0, q_lo), (k_b, 0, k_hi)):
                            sp.dma_start(dst[to:to + HD1, s].rearrange("p (q r) t -> p q r t", r=2)[:, :, r],
                                         src[rows]).then_inc(stacked.sem, 16)

                def spread_weights(c):
                    if c >= 2:
                        sp.wait_ge(hw_ok.sem, hw_ok.at(i, CHUNK * (c - 1)))
                    sp.dma_start(spread[:, c % 2], route_dram[CHUNK * c:CHUNK * c + CHUNK].partition_broadcast(P)
                                 ).then_inc(spread_in.sem, 16)

                for stage, n in LAYER1:
                    if stage == "qk":
                        stack(n)
                    if stage == "route":
                        emptied(sp, i, "cT")
                        sp.dma_start(route_dram, weightT[:]).then_inc(route_out.sem, 16)
                        sp.wait_ge(route_out.sem, route_out.at(i, 16))
                        spread_weights(0)
                        spread_weights(1)
                    if stage == "turn_max":
                        emptied(sp, i, f"m{n}")
                        sp.dma_start(q_b[HD1:K_B, n % 2], max_row[:, n % 2]).then_inc(row_in.sem, 16)
                    if stage == "moe" and 1 <= n < 3:
                        spread_weights(n + 1)
                sp.wait_ge(rec_ok.sem, rec_ok.at(i, 1))
                for h in range(G):
                    sp.dma_start(rec_dram[h], rec[32 * h:32 * h + G]).then_inc(rec_out.sem, 16)
                sp.wait_ge(rec_out.sem, rec_out.at(i, 16 * G))
                release(sp, sp_passed)
                sp.wait_ge(hw_ok.sem, hw_ok.at(i, E1))
                for h in range(G):
                    r, q = h % 2, h // 2
                    sp.dma_start(spread[HD1 * r:HD1 * r + HD1].rearrange("p c (g q) t -> p (c g) q t", q=2)[:, :, q],
                                 rec_dram[h].partition_broadcast(HD1)).then_inc(rec_in.sem, 16)

        @block.gpsimd
        def _(pool):
            nc.gpsimd.memset(neg_half[:], -0.5).then_inc(prep_pool, 1)
            pool.wait_ge(prep_pool, 1)
            pool.wait_ge(loaded, all_loaded)
            with pool.Fori(0, batches) as i:
                pool.wait_ge(stats_ok.sem, stats_ok.at(i, 2 * TB + 1))
                nc.gpsimd.tensor_tensor(rstd[:], var_eps[:], neg_half[:], ALU.pow).then_inc(rstd_ok.sem, 1)

                def add_keys(p):
                    s = key_sum[:, 2 * (p % 2):2 * (p % 2) + 2]
                    u = probs[:, p % 2]
                    if p >= 2:
                        g = p // 2 - 1
                        pool.wait_ge(filled.sem, filled.at(i, fills.index(f"s{g}") + 1))
                    pool.wait_ge(exp_done.sem, exp_done.at(i, 5 * p + 4))
                    release(pool, pool_passed)
                    nc.gpsimd.tensor_copy(s[:, :, 0:P], u[:, 0:2, 0:P]).then_inc(added.sem, 1)
                    nc.gpsimd.tensor_tensor(s[:, :, P:T], u[:, 0:2, P:T], u[:, 2:4, 0:3 * P], ALU.add
                                            ).then_inc(added.sem, 1)
                    pool.wait_ge(exp_done.sem, exp_done.at(i, 5 * p + 5))
                    pool.wait_ge(added.sem, added.at(i, 4 * p + 2))
                    nc.gpsimd.tensor_tensor(s[:, :, 2 * P:T], s[:, :, 2 * P:T],
                                            u[:, 4].rearrange("p (h q) -> p h q", h=2), ALU.add).then_inc(added.sem, 1)
                    pool.wait_ge(added.sem, added.at(i, 4 * p + 3))
                    nc.gpsimd.tensor_tensor(s[:, :, 3 * P:T], s[:, :, 3 * P:T], u[:, 2:4, 3 * P:T], ALU.add
                                            ).then_inc(added.sem, 1)

                for stage, n in LAYER1:
                    if stage == "heads":
                        add_keys(2 * n)
                        add_keys(2 * n + 1)
                    if stage == "moe":
                        if n >= 2:
                            chunk_done(pool, i, n - 2)
                        for e in experts_of(n):
                            emptied(pool, i, f"u{e}")
                            dst = hw[:, n % 2, e % CHUNK]
                            if e < E1:
                                pool.wait_ge(spread_in.sem, spread_in.at(i, 16 * (n + 1)))
                                nc.gpsimd.tensor_tensor(dst, hidden[:, e % 2], spread[:, n % 2, e % CHUNK], ALU.mult
                                                        ).then_inc(hw_ok.sem, 1)
                            else:
                                release(pool, pool_passed)
                                nc.gpsimd.tensor_scalar(dst, hidden[:, e % 2], 0.5, None, ALU.mult
                                                        ).then_inc(hw_ok.sem, 1)
                pool.wait_ge(rec_in.sem, rec_in.at(i, 16 * G))
                pool.wait_ge(pv_read.sem, pv_read.at(i, PAIRS))
                flat = spread[:].rearrange("p c g t -> p (c g) t")
                for p in range(PAIRS):
                    nc.gpsimd.tensor_tensor(yT[:, p], yT[:, p], flat[:, p], ALU.mult).then_inc(normed.sem, 1)

        @block.scalar
        def _(act):
            for s in (read["act"], exp_done, pv_read, stored):
                act.sem_inc(s.sem, s.begun)
            with act.Fori(0, batches) as i:
                def copy(name, dst):
                    nc.scalar.activation(dst, full(act, i, name), ACT.Copy).then_inc(read["act"].sem, 1)

                copy("xnT", xnT[:])
                copy("lat", latT[:])
                nc.scalar.activation(th[:].rearrange("p t e -> p (t e)"), full(act, i, "gate")[:, 0:TB * E1], ACT.Tanh,
                                     scale=0.5).then_inc(read["act"].sem, 1)

                def exp_pair(p):
                    if p >= 2:
                        act.wait_ge(pv_done.sem, pv_done.at(i, p - 1))
                        act.wait_ge(added.sem, added.at(i, 4 * (p - 1)))
                    for u in range(5):
                        n = 5 * p + u
                        act.wait_ge(exp_full.sem, exp_full.at(i, n + 1))
                        nc.scalar.activation(probs[:, p % 2, u], ps_exp[:, n % ST_BANKS], ACT.Exp,
                                             scale=float(HD1) ** -0.5).then_inc(exp_done.sem, 1)

                def out_rows(p):
                    act.wait_ge(pv_done.sem, pv_done.at(i, p + 1))
                    nc.scalar.activation(yT[:, p], ps_out[:], ACT.Copy).then_inc(pv_read.sem, 1)

                for stage, n in LAYER1:
                    if stage == "qk":
                        if n >= 1:
                            act.wait_ge(stacked.sem, stacked.at(i, 16 * 12 * n))
                        for k, (x, dst) in enumerate((("q", q_hi), ("k", k_hi))):
                            for r in range(2):
                                nc.scalar.activation(dst[:, r], full(act, i, f"{x}{2 * n + r}"), ACT.Copy
                                                     ).then_inc(hi_ok.sem, 1)
                    if stage == "values_in":
                        for t in range(TB):
                            for half in range(2):
                                copy(f"v{t}{half}", v[:, t, half * T:half * T + T])
                    if stage == "route":
                        nc.scalar.activation(weightT[:], full(act, i, "cT")[0:E1], ACT.Copy).then_inc(read["act"].sem, 1)
                    if stage == "turn_max":
                        nc.scalar.activation(max_row[:, n % 2], full(act, i, f"m{n}")[0:G * TB, 0:P], ACT.Copy,
                                             scale=1.0 / SHIFT).then_inc(read["act"].sem, 1)
                    if stage == "heads":
                        exp_pair(2 * n)
                        if n >= 1:
                            out_rows(2 * n - 1)
                        exp_pair(2 * n + 1)
                        out_rows(2 * n)
                    if stage == "last":
                        out_rows(PAIRS - 1)
                    if stage == "moe":
                        for e in experts_of(n):
                            if e >= 2:
                                emptied(act, i, f"g{e - 2}")
                            nc.scalar.activation(tanh[:, e % 2], full(act, i, f"g{e}"), ACT.Tanh, scale=0.5
                                                 ).then_inc(tanh_ok.sem, 1)
                emptied(act, i, "outT")
                act.dma_start(out_dram[i].rearrange("(t p) d -> p t d", p=P), x_res[:]).then_inc(stored.sem, 16)
            act.wait_ge(stored.sem, 16 * batches + 16)

        @block.vector
        def _(dve):
            for s in (read["dve"], xn_ok, max_read):
                dve.sem_inc(s.sem, s.begun)
            nc.vector.memset(k_b[HD1:P], SHIFT).then_inc(prep, 1)
            nc.vector.memset(one_col[:], 0.0).then_inc(prep, 1)
            dve.wait_ge(prep, 2)
            nc.vector.memset(one_col[:, :, G:32], 1.0).then_inc(prep, 1)
            for g in range(G):
                nc.vector.memset(one_col[:, g, g:g + 1], 1.0).then_inc(prep, 1)
            dve.wait_ge(loaded, all_loaded)
            nc.vector.tensor_copy(ident_h[:], ident[:]).then_inc(prep, 1)
            nc.vector.tensor_copy(masks_h[:], masks[:]).then_inc(prep, 1)

            with dve.Fori(0, batches) as i:
                dve.wait_ge(x_loaded.sem, x_loaded.at(i, 16))
                for t in range(TB):
                    nc.vector.bn_stats(stats[:, t], x_in[:, t]).then_inc(stats_ok.sem, 1)
                dve.wait_ge(stats_ok.sem, stats_ok.at(i, TB))
                release(dve, dve_passed)
                for t in range(TB):
                    nc.vector.bn_aggr(mv[:, t], stats[:, t]).then_inc(stats_ok.sem, 1)
                dve.wait_ge(stats_ok.sem, stats_ok.at(i, 2 * TB))
                nc.vector.tensor_scalar(var_eps[:], mv[:, :, 1], EPS, None, ALU.add).then_inc(stats_ok.sem, 1)
                dve.wait_ge(rstd_ok.sem, rstd_ok.at(i, 1))
                for t in range(TB):
                    nc.vector.tensor_scalar(xn[:, t], x_in[:, t], mv[:, t, 0:1], rstd[:, t:t + 1], ALU.subtract,
                                            ALU.mult).then_inc(xn_ok.sem, 1)

                def row_max(g):
                    if g >= 2:
                        dve.wait_ge(filled.sem, filled.at(i, fills.index(f"m{g - 2}") + 1))
                    for u, (t, heads) in enumerate(MAX_UNITS):
                        n = NM * g + u
                        k = len(heads)
                        dve.wait_ge(max_full.sem, max_full.at(i, n + 1))
                        src = ps_max[:, n % SM_BANKS, 0:k * (t + 1) * P].rearrange("p (h k) -> p h k", h=k)
                        nc.vector.tensor_reduce(neg_max[:, g % 2, heads[0]:heads[0] + k, t], src, AX.X, ALU.max,
                                                negate=True).then_inc(max_read.sem, 1)

                def route():
                    emptied(dve, i, "gate")
                    nc.vector.tensor_scalar(score[:], th[:], 0.5, 0.5, ALU.mult, ALU.add).then_inc(route_ok.sem, 1)
                    dve.wait_ge(route_ok.sem, route_ok.at(i, 1))
                    nc.vector.tensor_tensor(select[:], score[:], bias[:].unsqueeze(1).to_broadcast([P, TB, E1]), ALU.add
                                            ).then_inc(route_ok.sem, 1)
                    dve.wait_ge(route_ok.sem, route_ok.at(i, 2))
                    release(dve, dve_passed)
                    for t in range(TB):
                        nc.vector.max(top[:, t], select[:, t]).then_inc(route_ok.sem, 1)
                    dve.wait_ge(route_ok.sem, route_ok.at(i, 2 + TB))
                    release(dve, dve_passed)
                    for t in range(TB):
                        nc.vector.match_replace(out=rest[:, t], in_to_replace=top[:, t], in_values=select[:, t],
                                                imm_value=-1e30).then_inc(route_ok.sem, 1)
                    dve.wait_ge(route_ok.sem, route_ok.at(i, 10))
                    nc.vector.tensor_tensor(keep[:], select[:], rest[:], ALU.not_equal).then_inc(route_ok.sem, 1)
                    dve.wait_ge(route_ok.sem, route_ok.at(i, 11))
                    nc.vector.tensor_tensor(kept[:], score[:], keep[:], ALU.mult).then_inc(route_ok.sem, 1)
                    dve.wait_ge(route_ok.sem, route_ok.at(i, 12))
                    nc.vector.tensor_reduce(kept_sum[:], kept[:], AX.X, ALU.add).then_inc(route_ok.sem, 1)
                    dve.wait_ge(route_ok.sem, route_ok.at(i, 13))
                    nc.vector.reciprocal(kept_rec[:], kept_sum[:]).then_inc(route_ok.sem, 1)
                    dve.wait_ge(route_ok.sem, route_ok.at(i, 14))
                    nc.vector.scalar_tensor_tensor(out=weight[:], in0=kept[:], scalar=ROUTE / 2,
                                                   in1=kept_rec[:].unsqueeze(2).to_broadcast([P, TB, E1]),
                                                   op0=ALU.mult, op1=ALU.mult).then_inc(route_ok.sem, 1)

                for stage, n in LAYER1:
                    if stage == "qk":
                        for k, (x, hi, lo) in enumerate((("q", q_hi, q_lo), ("k", k_hi, k_lo))):
                            for r in range(2):
                                dve.wait_ge(hi_ok.sem, hi_ok.at(i, 4 * n + 2 * k + r + 1))
                                nc.vector.tensor_tensor(lo[:, r], full(dve, i, f"{x}{2 * n + r}"), hi[:, r],
                                                        ALU.subtract).then_inc(read["dve"].sem, 1)
                    if stage == "max":
                        row_max(n)
                    if stage == "heads" and n + 1 < G:
                        row_max(n + 1)
                    if stage == "route":
                        route()
                    if stage == "sums":
                        if n == 0:
                            nc.vector.tensor_copy(sums[:], full(dve, i, "s0")).then_inc(read["dve"].sem, 1)
                        else:
                            emptied(dve, i, f"s{n - 1}")
                            nc.vector.tensor_tensor(sums[:], full(dve, i, f"s{n}"), sums[:], ALU.add
                                                    ).then_inc(read["dve"].sem, 1)
                        if n == G - 1:
                            emptied(dve, i, f"s{n}")
                            nc.vector.reciprocal(rec[:], sums[:]).then_inc(rec_ok.sem, 1)
                    if stage == "moe":
                        for e in experts_of(n):
                            if e >= 1:
                                emptied(dve, i, f"u{e - 1}")
                            dve.wait_ge(tanh_ok.sem, tanh_ok.at(i, e + 1))
                            nc.vector.scalar_tensor_tensor(out=gated[:], in0=tanh[:, e % 2], scalar=1.0,
                                                           in1=full(dve, i, f"g{e}"), op0=ALU.add, op1=ALU.mult
                                                           ).then_inc(read["dve"].sem, 1)
                            emptied(dve, i, f"g{e}")
                            if e >= 2:
                                dve.wait_ge(hw_ok.sem, hw_ok.at(i, e - 1))
                            nc.vector.tensor_tensor(hidden[:, e % 2], full(dve, i, f"u{e}"), gated[:], ALU.mult
                                                    ).then_inc(read["dve"].sem, 1)
                        if n == 1:
                            nc.vector.tensor_copy(acc[:], full(dve, i, "d0")).then_inc(read["dve"].sem, 1)
                        if n >= 2:
                            emptied(dve, i, f"d{n - 2}")
                            nc.vector.tensor_tensor(acc[:], full(dve, i, f"d{n - 1}"), acc[:], ALU.add
                                                    ).then_inc(read["dve"].sem, 1)
                emptied(dve, i, "d3")
                emptied(dve, i, f"u{E1}")
                nc.vector.tensor_tensor(outT[:], full(dve, i, "out"), acc[:], ALU.add).then_inc(read["dve"].sem, 1)
                dve.wait_ge(res_loaded.sem, res_loaded.at(i, 16))
                nc.vector.tensor_tensor(x_res[:].rearrange("p t d -> p (t d)"), full(dve, i, "outT"),
                                        x_res[:].rearrange("p t d -> p (t d)"), ALU.add).then_inc(read["dve"].sem, 1)

        @block.tensor
        def _(pe):
            pe.wait_ge(loaded, all_loaded)
            pe.wait_ge(prep, 9)
            with pe.Fori(0, batches) as i:
                def bank(name):
                    k = fills.index(name)
                    if k >= 2:
                        emptied(pe, i, fills.names[k - 2])
                    else:
                        for s in read.values():
                            pe.wait_ge(s.sem, s.at(i, 0))
                    return ps_any[:, k % 2]

                def turn(name, blocks):
                    out = bank(name)
                    for b, src in enumerate(blocks):
                        ins = pe.transpose(out[:, b * P:b * P + P], src, ident[:])
                    ins.then_inc(filled.sem, 1)

                def product(name, w, x):
                    pe.matmul(bank(name), w, x, start=True, stop=True).then_inc(filled.sem, 1)

                pe.wait_ge(xn_ok.sem, xn_ok.at(i, TB))
                turn("xnT", [xn[:, t] for t in range(TB)])
                emptied(pe, i, "xnT")
                product("lat", w_kvd[:], xnT[:])
                out = bank("gate")
                for t in range(TB):
                    ins = pe.matmul(out[:, t * E1:t * E1 + E1], xnT[:, t * P:t * P + P], gate_w[:], start=True, stop=True)
                ins.then_inc(filled.sem, 1)
                emptied(pe, i, "lat")

                def max_unit(g, u):
                    t, heads = MAX_UNITS[u]
                    n = NM * g + u
                    w = (t + 1) * P
                    if u == 0:
                        pe.wait_ge(stacked.sem, stacked.at(i, 16 * 12 * (g + 1)))
                    pe.wait_ge(max_read.sem, max_read.at(i, max(n + 1 - SM_BANKS, 0)))
                    for c, h in enumerate(heads):
                        out = ps_max[:, n % SM_BANKS, c * w:c * w + w]
                        pe.matmul(out, q_a[:, g % 2, h, t * P:t * P + P], k_a[:, g % 2, h, 0:w], start=True, stop=False)
                        ins = pe.matmul(out[:, t * P:w], ident_h[:], masks_h[:, 0], start=False, stop=True)
                    ins.then_inc(max_full.sem, 1)

                def exp_unit(p, u):
                    n = 5 * p + u
                    g = p // 2
                    if u == 0 and p % 2 == 0:
                        pe.wait_ge(row_in.sem, row_in.at(i, 16 * (g + 1)))
                    pe.wait_ge(exp_done.sem, exp_done.at(i, max(n + 1 - ST_BANKS, 0)))
                    for r, j, c in EXP1[u]:
                        h = 2 * (p % 2) + r
                        w = T - j * P
                        out = ps_exp[:, n % ST_BANKS, c:c + w]
                        pe.matmul(out, k_a[:, g % 2, h, j * P:j * P + P], q_a[:, g % 2, h, j * P:T], start=True, stop=False)
                        pe.matmul(out, k_b[0:K_B, g % 2, h, j * P:j * P + P], q_b[0:K_B, g % 2, h, j * P:T],
                                  start=False, stop=False)
                        ins = pe.matmul(out[:, 0:P], ident_h[:], masks_h[:, 1], start=False, stop=True)
                    ins.then_inc(exp_full.sem, 1)

                def values(p):
                    pe.wait_ge(pv_read.sem, pv_read.at(i, p))
                    pe.wait_ge(exp_done.sem, exp_done.at(i, 5 * p + 5))
                    pieces = sorted([(j, r, u, c) for u in range(5) for r, j, c in EXP1[u]])
                    for j, r, u, c in pieces:
                        h = 2 * p + r
                        ins = pe.matmul(ps_out[HD1 * r:HD1 * r + HD1, j * P:T], v[:, j, h * HD1:h * HD1 + HD1],
                                        probs[:, p % 2, u, c:c + T - j * P], start=(j == 0), stop=(j == TB - 1))
                    ins.then_inc(pv_done.sem, 1)

                def heads(g):
                    turns = list(range(NM)) if g + 1 < G else []
                    for p in (2 * g, 2 * g + 1):
                        for u in range(5):
                            exp_unit(p, u)
                            if turns:
                                max_unit(g + 1, turns.pop(0))
                        if p >= 1:
                            values(p - 1)
                    while turns:
                        max_unit(g + 1, turns.pop(0))

                for stage, n in LAYER1:
                    if stage == "qk":
                        for r in range(2):
                            p = 2 * n + r
                            product(f"q{p}", w_q[:, p * P:p * P + P], xnT[:])
                        for r in range(2):
                            p = 2 * n + r
                            product(f"k{p}", w_kvu[:, 0, p * P:p * P + P], latT[:])
                    if stage == "values_in":
                        for t in range(TB):
                            for half in range(2):
                                product(f"v{t}{half}", latT[:, t * P:t * P + P], w_kvu[:, 1, half * T:half * T + T])
                    if stage == "route":
                        pe.wait_ge(route_ok.sem, route_ok.at(i, 15))
                        out = bank("cT")
                        for t in range(TB):
                            ins = pe.transpose(out[0:E1, t * P:t * P + P], weight[:, t], ident[:])
                        ins.then_inc(filled.sem, 1)
                    if stage == "max":
                        for u in range(NM):
                            max_unit(n, u)
                    if stage == "turn_max":
                        pe.wait_ge(max_read.sem, max_read.at(i, NM * (n + 1)))
                        pe.transpose(bank(f"m{n}")[0:G * TB, 0:P], neg_max[:, n % 2].rearrange("p h t -> p (h t)"),
                                     ident[:]).then_inc(filled.sem, 1)
                    if stage == "heads":
                        if n == 0:
                            emptied(pe, i, f"v{TB - 1}1")
                        heads(n)
                    if stage == "last":
                        values(PAIRS - 1)
                    if stage == "sums":
                        pe.wait_ge(added.sem, added.at(i, 8 * (n + 1)))
                        out = bank(f"s{n}")
                        for h in range(G):
                            ins = pe.matmul(out[32 * h:32 * h + 32], one_col[:, n], key_sum[:, h], start=True, stop=True)
                        ins.then_inc(filled.sem, 1)
                    if stage == "moe":
                        for e in experts_of(n):
                            product(f"g{e}", w_g[:, e], xnT[:])
                            product(f"u{e}", w_u[:, e], xnT[:])
                        if n >= 1:
                            out = bank(f"d{n - 1}")
                            for k, e in enumerate(experts_of(n - 1)):
                                pe.wait_ge(hw_ok.sem, hw_ok.at(i, e + 1))
                                ins = pe.matmul(out, w_d[:, e], hw[:, (n - 1) % 2, k], start=(k == 0),
                                                stop=(k == CHUNK - 1))
                            ins.then_inc(filled.sem, 1)
                out = bank("out")
                pe.wait_ge(hw_ok.sem, hw_ok.at(i, E1 + 1))
                pe.matmul(out, w_d[:, E1], hw[:, 0, 0], start=True, stop=False)
                for p in range(PAIRS):
                    pe.wait_ge(normed.sem, normed.at(i, p + 1))
                    ins = pe.matmul(out, w_out[:, p], yT[:, p], start=False, stop=(p == PAIRS - 1))
                ins.then_inc(filled.sem, 1)
                emptied(pe, i, "out")
                turn("outT", [outT[:, t * P:t * P + P] for t in range(TB)])


def build(nc, a, out, batches):
    x1_dram = nc.dram_tensor("x1_scratch", [batches, T, D], F32, kind="Internal").ap()
    layer0(nc, a, x1_dram, batches)
    layer1(nc, a, x1_dram, out, batches)


def constants():
    cos, sin = rotary_tables()
    q, k = np.arange(P)[:, None], np.arange(P)[None, :]
    return {"ident": np.eye(P, dtype=np.float32), "cos": cos, "sin": sin,
            "mask": np.where(k > q, np.float32(-1e30), np.float32(0)),
            "maskT": np.where(q > k, np.float32(-1e30), np.float32(0))}


def lay_out(inputs):
    laid = {n: np.asarray(v) for n, v in inputs.items()}
    for n in ("L1_ffn_w_gate", "L1_ffn_w_up", "L1_ffn_w_down"):
        laid[n] = laid[n].transpose(2, 0, 1)
    for n in ("L1_ffn_gate_w", "L1_ffn_shared_gate_w", "L1_ffn_shared_up_w", "L1_ffn_shared_down_w"):
        laid[n] = laid[n].T
    laid["L0_ffn_b1"] = laid["L0_ffn_b1"].reshape(E0, HB, P).transpose(2, 0, 1)
    laid.update(constants())
    return {n: np.ascontiguousarray(v) for n, v in laid.items()}


def kernel(**inputs):
    import concourse.bacc as bacc
    from concourse.bass_utils import run_bass_kernel_spmd

    nc = bacc.Bacc("TRN2", target_bir_lowering=False, num_devices=1)
    laid = lay_out(inputs)
    arrays, a = {}, {}
    for n, v in laid.items():
        arrays[f"in_{n}"] = v
        a[n] = nc.dram_tensor(f"in_{n}", v.shape, mybir.dt.from_np(v.dtype), kind="ExternalInput").ap()
    shape = laid["L0_attn_x"].shape
    out = nc.dram_tensor("out_0", shape, F32, kind="ExternalOutput").ap()
    build(nc, a, out, shape[0])
    r = run_bass_kernel_spmd(nc, [arrays], core_ids=[0])
    return r.results[0]["out_0"]
```

```python
from contextlib import ExitStack

import numpy as np

import concourse.bass as bass
from concourse import mybir

ALU = mybir.AluOpType
ACT = mybir.ActivationFunctionType
AX = mybir.AxisListType
F32 = mybir.dt.float32
F16 = mybir.dt.float16
BF16 = mybir.dt.bfloat16

P = 128
D = 128
T = 512
TB = T // P
H = 16
G = 4
HD0, DR = 8, 32
HD1 = 64
E0, S0 = 8, 64
HID = 512
HB = HID // P
E1 = 16
TOP = 8
EPS = 1e-5
ROUTE = 2.826
SHIFT = 256.0
K_ROPE = 3 * DR
K_MAX0 = K_ROPE + 3 * HD0
K_ALL0 = K_MAX0 + 1

MAX_UNITS = [(0, (0, 1, 2, 3)), (1, (0, 1)), (1, (2, 3))] + [(t, (h,)) for t in (2, 3) for h in range(4)]
NM = len(MAX_UNITS)
EXP0 = ([[(h, 0, 0)] for h in range(4)] + [[(h, 1, 0), (h, 3, 384)] for h in range(4)]
        + [[(h, 2, 0), (h + 1, 2, 256)] for h in (0, 2)])
PARTS0 = ((0, 4), (4, 8), (8, 10))
SM_BANKS, ST_BANKS = 3, 2


class Signal:

    def __init__(self, ctx, nc, name, per, begun=0):
        self.sem = ctx.enter_context(nc.semaphore(name))
        self.per, self.begun = per, begun

    def at(self, i, n):
        assert n + self.begun > 0
        return i * self.per + (n + self.begun)


class Fills:

    def __init__(self, plan, first=None, steady=()):
        self.names = [n for n, _ in plan]
        self.reader = dict(plan)
        self.start = {r: first.count(r) if first else 0 for r in ("all", "act", "dve")}
        self.per = {"all": len(steady)} | {r: sum(1 for _, x in steady if x == r) for r in ("act", "dve")}
        assert len(plan) == len(self.reader) and len(steady) % 2 == 0

    def count(self, reader):
        return sum(1 for n in self.names if reader in ("all", self.reader[n]))

    def before(self, i, who):
        return i * self.per[who] + self.start[who]

    def filled(self, i, name):
        return i * self.per["all"] + (self.start["all"] + self.names.index(name) + 1)

    def emptied(self, i, name):
        who = self.reader[name]
        upto = self.names[:self.names.index(name) + 1]
        return i * self.per[who] + (self.start[who] + sum(1 for n in upto if self.reader[n] == who))

    def bank(self, name):
        return (self.start["all"] + self.names.index(name)) % 2


def weave(steps, others):
    out, k = [], 0
    for n, step in enumerate(steps):
        out.append(step)
        while k < len(others) and (k + 1) * len(steps) <= (n + 1) * len(others) + len(steps) // 2:
            out.append(others[k])
            k += 1
    return out + list(others[k:])


def release(eng, passed):
    eng.sem_inc(passed, 1)


def rotary_tables():
    inv = np.float32(1.0) / np.float32(10000.0) ** (np.arange(0, DR, 2, dtype=np.float32) / np.float32(DR))
    angle = np.outer(np.arange(T, dtype=np.float32), inv).T
    cos, sin = np.cos(angle), np.sin(angle)
    rows = [np.concatenate([cos, cos]), np.concatenate([-sin, sin])]
    return [np.concatenate([x, x]).astype(np.float32) for x in rows]

class TurnFills:

    def __init__(self, plan):
        self.names = [n for n, _ in plan]
        self.reader = dict(plan)
        assert len(plan) == len(self.reader) and len(plan) % 2 == 0

    def count(self, reader):
        return sum(1 for n in self.names if self.reader[n] == reader)

    def index(self, name):
        return self.names.index(name)

    def reads(self, name):
        return sum(1 for n in self.names[:self.index(name) + 1] if self.reader[n] == self.reader[name])



LAYER0 = [("logits_s", 0), ("max", 0), ("dispatch", 0), ("turn_max", 0), ("heads", 0), ("logits_c", 0),
          ("turn_max", 1), ("heads", 1), ("heads_out", 0), ("experts", 0), ("turn_max", 2), ("heads", 2),
          ("heads_out", 1), ("combine", 0), ("turn_max", 3), ("heads", 3), ("heads_out", 2), ("last", 0),
          ("heads_out", 3)]


def layer0_fills():
    plan = [("xnT", "act"), ("xfT", "act"), ("ckv", "act"), ("q", "dve"), ("r", "dve"), ("k", "dve"),
            ("v", "act")]
    both = ("act", "dve")
    for stage, n in LAYER0:
        plan += {"logits_s": [(f"ls{b}", "act") for b in range(4)],
                 "dispatch": [(f"dT{t}", both[t % 2]) for t in range(4)] + [("slots", "act")],
                 "logits_c": [(f"lc{b}", "act") for b in range(4)],
                 "experts": [(f"h{b}", "act") for b in range(4)] + [("eo", "dve")],
                 "combine": [(f"cT{b}", both[b % 2]) for b in range(4)],
                 "turn_max": [(f"m{n}", "act")],
                 "heads_out": [(f"y{n}", "dve")]}.get(stage, [])
    return TurnFills(plan + [("atT", "act"), ("out", "act"), ("outT", "dve")])


def layer0(nc, a, x1_dram, batches):
    with ExitStack() as ctx:
        def sb(name, shape, dt=F32):
            return ctx.enter_context(nc.sbuf_tensor(name, shape, dt))

        def sig(name, per, begun=0):
            return Signal(ctx, nc, name, per, begun)

        def plain(name):
            return ctx.enter_context(nc.semaphore(name))

        stack_dram = nc.dram_tensor("stack_scratch", [2, H, 3 * HD0, T], F16, kind="Internal").ap()
        ps_max = ctx.enter_context(nc.psum_tensor("ps_max", [P, SM_BANKS, T], F32))
        ps_exp = ctx.enter_context(nc.psum_tensor("ps_exp", [P, ST_BANKS, T], F32))
        ps_out = ctx.enter_context(nc.psum_tensor("ps_out", [P, T], F32))
        ps_any = ctx.enter_context(nc.psum_tensor("ps_any", [P, 2, T], F32))

        ident = sb("ident", [P, P])
        ident_h = sb("ident_h", [P, P], BF16)
        mask = sb("mask", [P, P])
        mask_h = sb("mask_h", [P, P], BF16)
        cos = sb("cos", [2 * DR, T])
        sin = sb("sin", [2 * DR, T])
        w_kvd = sb("w_kvd", [P, D])
        w_q = sb("w_q", [P, D])
        w_k = sb("w_k", [P, D])
        w_v = sb("w_v", [P, D])
        w_o = sb("w_o", [P, D])
        w_qr = sb("w_qr", [P, 2, DR])
        w_kr = sb("w_kr", [P, 2, DR])
        gamma = sb("gamma", [P, D])
        slot_gamma = sb("slot_gamma", [P, D])
        w1 = sb("w1", [P, E0, HID])
        w2 = sb("w2", [P, E0, HB, D])
        b1 = sb("b1", [P, E0, HB])
        b2 = sb("b2", [P, E0 // 2, D])
        slot_nat = sb("slot_nat", [P, 4, D])
        slot_n = sb("slot_n", [P, 4, D])
        slot_ss = sb("slot_ss", [P, 4])
        slot_sm = sb("slot_sm", [P, 4])
        slot_r = sb("slot_r", [P, 4])
        snT = sb("snT", [P, T])
        neg_half = sb("neg_half", [P, 4])

        x_in = sb("x_in", [P, TB, D])
        x_res = sb("x_res", [P, TB, D])
        stats = sb("stats", [P, TB, 6])
        mv = sb("mv", [P, TB, 2])
        var_eps = sb("var_eps", [P, TB])
        rstd = sb("rstd", [P, TB])
        xn = sb("xn", [P, TB, D])
        squares = sb("squares", [P, TB, D])
        ss = sb("ss", [P, TB])
        ss_m = sb("ss_m", [P, TB])
        rnorm = sb("rnorm", [P, TB])
        xf = sb("xf", [P, TB, D])
        xnT = sb("xnT", [P, T])
        xfT = sb("xfT", [P, T])
        ckvT = sb("ckvT", [P, T])
        q_hi = sb("q_hi", [P, T], F16)
        q_lo = sb("q_lo", [P, T], F16)
        k_hi = sb("k_hi", [P, T], F16)
        k_lo = sb("k_lo", [P, T], F16)
        rot_a = sb("rot_a", [2 * DR, T])
        rot_b = sb("rot_b", [2 * DR, T])
        rot = sb("rot", [2 * DR, T])
        rot_hi = sb("rot_hi", [2 * DR, T], F16)
        rot_lo = sb("rot_lo", [2 * DR, T], F16)
        q_st = sb("q_st", [P, 2, G, T], F16)
        k_st = sb("k_st", [P, 2, G, T], F16)
        v_aug = sb("v_aug", [P, TB, H, DR])
        neg_max = sb("neg_max", [P, 2, G, TB])
        max_row = sb("max_row", [G * TB, 2, P], F16)
        probs = sb("probs", [P, len(EXP0), T])
        y_un = sb("y_un", [P, T])
        y_rec = sb("y_rec", [P, TB, G])
        attn = sb("attn", [P, TB, D])
        attnT = sb("attnT", [P, T])
        s_neg = sb("s_neg", [P, 4])
        s_sum = sb("s_sum", [P, 4])
        s_rec = sb("s_rec", [P, 4])
        c_neg = sb("c_neg", [P, 4])
        c_sum = sb("c_sum", [P, 4])
        c_rec = sb("c_rec", [P, 4])
        disp_s = sb("disp_s", [P, 4, T])
        disp_n = sb("disp_n", [P, TB, T])
        comb_n = disp_s
        comb_s = disp_n
        slotsT = sb("slotsT", [P, T])
        hT = sb("hT", [P, 4, HB, 2 * S0])
        eo = sb("eo", [P, 4, D])
        outT = sb("outT", [P, T])
        x1 = sb("x1", [P, TB, D])

        fills = layer0_fills()

        loaded, prep, prep_pool, prep_pe, prep_act = [plain(f"l0_{n}") for n in ("loaded", "prep", "prep_pool",
                                                                                 "prep_pe", "prep_act")]
        sp_passed, pool_passed, dve_passed = [plain(f"l0_{n}_passed") for n in ("sp", "pool", "dve")]
        x_loaded = sig("x_loaded", 16)
        res_loaded = sig("res_loaded", 16)
        scratch_in = sig("scratch_in", 16 * 6)
        stacked = sig("stacked", 16 * (2 * 6 + 2 * G))
        row_in = sig("row_in", 16 * G)
        stored = sig("l0_stored", 16, 16)
        stats_ok = sig("stats_ok", 2 * TB + 1)
        rstd_ok = sig("rstd_ok", 1)
        xn_ok = sig("xn_ok", TB, 1)
        ss_ok = sig("ss_ok", TB + 1)
        rnorm_ok = sig("rnorm_ok", 1)
        xf_ok = sig("xf_ok", TB)
        filled = sig("filled", len(fills.names))
        read = {"act": sig("read_act", fills.count("act"), 1), "dve": sig("read_dve", fills.count("dve"), 1)}
        hi_ok = sig("hi_ok", 2)
        rot_ok = sig("rot_ok", 4)
        max_full = sig("max_full", NM * G)
        max_read = sig("max_read", NM * G, 1)
        exp_full = sig("exp_full", 10 * G)
        exp_done = sig("exp_done", 10 * G, 1)
        masked = sig("masked", 4 * G)
        pv_done = sig("pv_done", 3 * G)
        pv_read = sig("pv_read", G, 1)
        rec_ok = sig("rec_ok", G)
        neg_ok = sig("neg_ok", 8)
        srec_ok = sig("srec_ok", 8)
        scaled = sig("scaled", 8)

        def emptied(eng, i, name):
            s = read[fills.reader[name]]
            eng.wait_ge(s.sem, s.at(i, fills.reads(name)))

        def full(eng, i, name):
            eng.wait_ge(filled.sem, filled.at(i, fills.index(name) + 1))
            return ps_any[:, fills.index(name) % 2]

        block = ctx.enter_context(nc.Block())

        rope = [(dst[:, n, c], a[src][:, s]) for dst, src in ((w_qr, "L0_attn_W_q_rope"), (w_kr, "L0_attn_W_k_rope"))
                for n, c, s in ((0, slice(0, DR), slice(0, DR)), (1, slice(0, DR // 2), slice(DR // 2, DR)),
                                (1, slice(DR // 2, DR), slice(0, DR // 2)))]
        loads = [(ident[:], a["ident"]), (mask[:], a["mask"]), (cos[:], a["cos"]), (sin[:], a["sin"]),
                 (slot_nat[:], a["L0_ffn_slot_embeds"].rearrange("e s d -> (e s) d").rearrange("(m p) d -> p m d", p=P)),
                 (slot_gamma[:], a["L0_ffn_slot_norm_gamma"].partition_broadcast(P)),
                 (gamma[:], a["L0_ffn_norm_gamma"].partition_broadcast(P)),
                 (w_kvd[:], a["L0_attn_W_kv_down"]), (w_q[:], a["L0_attn_W_q"]), (w_k[:], a["L0_attn_W_k_up"]),
                 (w_v[:], a["L0_attn_W_v_up"]), (w_o[:], a["L0_attn_W_o"])] + rope + [
                 (b1[:], a["L0_ffn_b1"]),
                 (w1[:], a["L0_ffn_w1"].rearrange("e d h -> d e h")),
                 (w2[:], a["L0_ffn_w2"].rearrange("e (b p) d -> p e b d", p=P))]
        loads += [(b2[S0 * (e % 2):S0 * (e % 2) + S0, e // 2, :], a["L0_ffn_b2"][e].partition_broadcast(S0))
                  for e in range(E0)]
        all_loaded = 16 * len(loads)

        @block.sync
        def _(sp):
            for dst, src in loads:
                sp.dma_start(dst, src).then_inc(loaded, 16)
            with sp.Fori(0, batches) as i:
                sp.wait_ge(xn_ok.sem, xn_ok.at(i, 0))
                release(sp, sp_passed)
                sp.dma_start(x_in[:], a["L0_attn_x"][i].rearrange("(t p) d -> p t d", p=P)).then_inc(x_loaded.sem, 16)
                sp.wait_ge(read["dve"].sem, read["dve"].at(i, 0))
                release(sp, sp_passed)
                sp.dma_start(x_res[:], a["L0_attn_x"][i].rearrange("(t p) d -> p t d", p=P)).then_inc(res_loaded.sem, 16)
                for side, name, parts in ((0, "q", (q_hi, q_lo, q_hi)), (1, "k", (k_hi, k_hi, k_lo))):
                    emptied(sp, i, name)
                    for n in range(3):
                        sp.dma_start(stack_dram[side, :, n * HD0:(n + 1) * HD0, :], parts[n][:]
                                     ).then_inc(scratch_in.sem, 16)
                    if side == 0:
                        sp.wait_ge(rot_ok.sem, rot_ok.at(i, 4))
                        for s in range(2):
                            for n, (qp, kp) in enumerate(((rot_hi, rot_hi), (rot_lo, rot_hi), (rot_hi, rot_lo))):
                                for st, src in ((q_st, qp[0:DR]), (k_st, kp[DR:2 * DR])):
                                    sp.dma_start(st[n * DR:(n + 1) * DR, s], src.unsqueeze(1).to_broadcast([DR, G, T])
                                                 ).then_inc(stacked.sem, 16)
                sp.wait_ge(scratch_in.sem, scratch_in.at(i, 16 * 6))

                def heads_rows(g):
                    for side, st in ((0, q_st), (1, k_st)):
                        sp.dma_start(st[K_ROPE:K_MAX0, g % 2],
                                     stack_dram[side, G * g:G * g + G].rearrange("h r t -> r h t")
                                     ).then_inc(stacked.sem, 16)

                def max_rows(g):
                    emptied(sp, i, f"m{g}")
                    sp.dma_start(q_st[K_MAX0:K_ALL0, g % 2], max_row[:, g % 2]).then_inc(row_in.sem, 16)

                heads_rows(0)
                heads_rows(1)
                for g in range(G):
                    max_rows(g)
                    if g + 2 < G:
                        sp.wait_ge(exp_full.sem, exp_full.at(i, 10 * (g + 1)))
                        heads_rows(g + 2)

        @block.gpsimd
        def _(pool):
            nc.gpsimd.memset(neg_half[:], -0.5).then_inc(prep_pool, 1)
            pool.wait_ge(prep, 7)
            pool.wait_ge(prep_pool, 1)
            nc.gpsimd.tensor_tensor(slot_r[:], slot_sm[:], neg_half[:], ALU.pow).then_inc(prep_pool, 1)
            with pool.Fori(0, batches) as i:
                pool.wait_ge(stats_ok.sem, stats_ok.at(i, 2 * TB + 1))
                nc.gpsimd.tensor_tensor(rstd[:], var_eps[:], neg_half[:], ALU.pow).then_inc(rstd_ok.sem, 1)
                pool.wait_ge(ss_ok.sem, ss_ok.at(i, TB + 1))
                nc.gpsimd.tensor_tensor(rnorm[:], ss_m[:], neg_half[:], ALU.pow).then_inc(rnorm_ok.sem, 1)

                def scale(w, rec, n):
                    for b in range(4):
                        pool.wait_ge(srec_ok.sem, srec_ok.at(i, n + b + 1))
                        release(pool, pool_passed)
                        nc.gpsimd.tensor_scalar(w[:, b], w[:, b], rec[:, b:b + 1], None, ALU.mult
                                                ).then_inc(scaled.sem, 1)

                def heads(g):
                    late = probs[:, 8:10].rearrange("p u (c q) -> p (u c) q", q=2 * P)
                    for last, v in ((4, probs[:, 0:4, 0:P]), (8, probs[:, 4:8, 0:P]), (8, probs[:, 4:8, 3 * P:T]),
                                    (10, late[:, :, 0:P])):
                        pool.wait_ge(exp_done.sem, exp_done.at(i, 10 * g + last))
                        release(pool, pool_passed)
                        nc.gpsimd.affine_select(out=v, in_=v, compare_op=ALU.is_ge, fill=0.0, base=0,
                                                pattern=[[0, 4], [1, P]], channel_multiplier=-1).then_inc(masked.sem, 1)

                for stage, n in LAYER0:
                    if stage == "dispatch":
                        scale(disp_s, s_rec, 0)
                    if stage == "experts":
                        scale(comb_n, c_rec, 4)
                    if stage == "heads":
                        heads(n)

        @block.scalar
        def _(act):
            for s in (read["act"], exp_done, pv_read, stored):
                act.sem_inc(s.sem, s.begun)
            act.wait_ge(prep_pe, 1)
            nc.scalar.activation(snT[:], ps_any[:, 0], ACT.Copy).then_inc(prep_act, 1)
            act.wait_ge(prep, 13)
            act.wait_ge(loaded, all_loaded)
            with act.Fori(0, batches) as i:
                def copy(name, dst):
                    nc.scalar.activation(dst, full(act, i, name), ACT.Copy).then_inc(read["act"].sem, 1)

                def softmax(b, name, neg, w, sums, n):
                    act.wait_ge(neg_ok.sem, neg_ok.at(i, n + b + 1))
                    nc.scalar.activation(w[:, b], full(act, i, name), ACT.Exp, bias=neg[:, b:b + 1],
                                         accum_out=sums[:, b:b + 1]).then_inc(read["act"].sem, 1)

                copy("xnT", xnT[:])
                copy("xfT", xfT[:])
                copy("ckv", ckvT[:])
                for name, dst in (("q", q_hi), ("k", k_hi)):
                    nc.scalar.activation(dst[:], full(act, i, name), ACT.Copy).then_inc(hi_ok.sem, 1)
                nc.scalar.activation(v_aug[:, :, :, 0:HD0], full(act, i, "v").rearrange("p (t h d) -> p t h d", t=TB, h=H),
                                     ACT.Copy).then_inc(read["act"].sem, 1)

                def heads(g):
                    for u in range(10):
                        n = 10 * g + u
                        if u == 4 and g >= 1:
                            out_rows(g - 1)
                        part = (0 if u < 4 else 1 if u < 8 else 2)
                        if g >= 1:
                            act.wait_ge(pv_done.sem, pv_done.at(i, 3 * (g - 1) + part + 1))
                        act.wait_ge(exp_full.sem, exp_full.at(i, n + 1))
                        nc.scalar.activation(probs[:, u], ps_exp[:, n % ST_BANKS], ACT.Exp,
                                             scale=float(HD0 + DR) ** -0.5).then_inc(exp_done.sem, 1)

                def out_rows(g):
                    act.wait_ge(pv_done.sem, pv_done.at(i, 3 * g + 3))
                    if g >= 1:
                        act.wait_ge(filled.sem, filled.at(i, fills.index(f"y{g - 1}") + 1))
                    nc.scalar.activation(y_un[:], ps_out[:], ACT.Copy).then_inc(pv_read.sem, 1)

                for stage, n in LAYER0:
                    if stage == "logits_s":
                        for b in range(4):
                            softmax(b, f"ls{b}", s_neg, disp_s, s_sum, 0)
                    if stage == "dispatch":
                        for t in (0, 2):
                            copy(f"dT{t}", disp_n[:, t])
                        copy("slots", slotsT[:])
                    if stage == "turn_max":
                        nc.scalar.activation(max_row[:, n % 2], full(act, i, f"m{n}")[0:G * TB, 0:P], ACT.Copy,
                                             scale=1.0 / SHIFT).then_inc(read["act"].sem, 1)
                    if stage == "heads":
                        heads(n)
                    if stage == "last":
                        out_rows(G - 1)
                    if stage == "logits_c":
                        for b in range(4):
                            softmax(b, f"lc{b}", c_neg, comb_n, c_sum, 4)
                    if stage == "experts":
                        for b in range(4):
                            bank = full(act, i, f"h{b}")
                            for hb in range(HB):
                                for ee in range(2):
                                    c = (hb * 2 + ee) * S0
                                    ins = nc.scalar.activation(hT[:, b, hb, ee * S0:ee * S0 + S0], bank[:, c:c + S0],
                                                               ACT.Gelu, bias=b1[:, 2 * b + ee, hb:hb + 1])
                            ins.then_inc(read["act"].sem, 1)
                    if stage == "combine":
                        for b in (0, 2):
                            copy(f"cT{b}", comb_s[:, b])
                copy("atT", attnT[:])
                copy("out", outT[:])
                emptied(act, i, "outT")
                act.dma_start(x1_dram[i].rearrange("(t p) d -> p t d", p=P), x1[:]).then_inc(stored.sem, 16)
            act.wait_ge(stored.sem, 16 * batches + 16)

        @block.vector
        def _(dve):
            for s in (read["dve"], xn_ok, max_read):
                dve.sem_inc(s.sem, s.begun)
            nc.vector.memset(v_aug[:], 0.0).then_inc(prep, 1)
            nc.vector.memset(k_st[K_ROPE:P], SHIFT).then_inc(prep, 1)
            dve.wait_ge(loaded, all_loaded)
            for b in range(4):
                nc.vector.tensor_tensor_reduce(squares[:, b], slot_nat[:, b], slot_nat[:, b], 1.0 / D, 0.0, ALU.mult,
                                               ALU.add, slot_ss[:, b:b + 1]).then_inc(prep, 1)
            dve.wait_ge(prep, 6)
            nc.vector.tensor_scalar(slot_sm[:], slot_ss[:], 1e-24 / D, None, ALU.max).then_inc(prep, 1)
            dve.wait_ge(prep_pool, 2)
            for b in range(4):
                nc.vector.scalar_tensor_tensor(out=slot_n[:, b], in0=slot_nat[:, b], scalar=slot_r[:, b:b + 1],
                                               in1=slot_gamma[:], op0=ALU.mult, op1=ALU.mult).then_inc(prep, 1)
            nc.vector.tensor_copy(ident_h[:], ident[:]).then_inc(prep, 1)
            dve.wait_ge(prep, 12)
            nc.vector.memset(v_aug[:, :, :, HD0:HD0 + 1], 1.0).then_inc(prep, 1)
            nc.vector.tensor_copy(mask_h[:], mask[:]).then_inc(prep, 1)

            with dve.Fori(0, batches) as i:
                dve.wait_ge(x_loaded.sem, x_loaded.at(i, 16))
                for t in range(TB):
                    nc.vector.bn_stats(stats[:, t], x_in[:, t]).then_inc(stats_ok.sem, 1)
                dve.wait_ge(stats_ok.sem, stats_ok.at(i, TB))
                release(dve, dve_passed)
                for t in range(TB):
                    nc.vector.bn_aggr(mv[:, t], stats[:, t]).then_inc(stats_ok.sem, 1)
                dve.wait_ge(stats_ok.sem, stats_ok.at(i, 2 * TB))
                nc.vector.tensor_scalar(var_eps[:], mv[:, :, 1], EPS, None, ALU.add).then_inc(stats_ok.sem, 1)
                dve.wait_ge(rstd_ok.sem, rstd_ok.at(i, 1))
                for t in range(TB):
                    nc.vector.tensor_scalar(xn[:, t], x_in[:, t], mv[:, t, 0:1], rstd[:, t:t + 1], ALU.subtract,
                                            ALU.mult).then_inc(xn_ok.sem, 1)
                for t in range(TB):
                    dve.wait_ge(xn_ok.sem, xn_ok.at(i, t + 1))
                    nc.vector.tensor_tensor_reduce(squares[:, t], xn[:, t], xn[:, t], 1.0 / D, 0.0, ALU.mult, ALU.add,
                                                   ss[:, t:t + 1]).then_inc(ss_ok.sem, 1)
                dve.wait_ge(ss_ok.sem, ss_ok.at(i, TB))
                nc.vector.tensor_scalar(ss_m[:], ss[:], 1e-24 / D, None, ALU.max).then_inc(ss_ok.sem, 1)
                dve.wait_ge(rnorm_ok.sem, rnorm_ok.at(i, 1))
                for t in range(TB):
                    nc.vector.scalar_tensor_tensor(out=xf[:, t], in0=xn[:, t], scalar=rnorm[:, t:t + 1], in1=gamma[:],
                                                   op0=ALU.mult, op1=ALU.mult).then_inc(xf_ok.sem, 1)

                def low_part(name, n, hi, lo):
                    dve.wait_ge(hi_ok.sem, hi_ok.at(i, n))
                    nc.vector.tensor_tensor(lo[:], full(dve, i, name), hi[:], ALU.subtract).then_inc(read["dve"].sem, 1)

                low_part("q", 1, q_hi, q_lo)
                bank = full(dve, i, "r")
                nc.vector.tensor_tensor(rot_a[:], bank[0:2 * DR], cos[:], ALU.mult).then_inc(rot_ok.sem, 1)
                nc.vector.tensor_tensor(rot_b[:], bank[2 * DR:P], sin[:], ALU.mult).then_inc(read["dve"].sem, 1)
                dve.wait_ge(rot_ok.sem, rot_ok.at(i, 1))
                emptied(dve, i, "r")
                nc.vector.tensor_tensor(rot[:], rot_a[:], rot_b[:], ALU.add).then_inc(rot_ok.sem, 1)
                dve.wait_ge(rot_ok.sem, rot_ok.at(i, 2))
                nc.vector.tensor_copy(rot_hi[:], rot[:]).then_inc(rot_ok.sem, 1)
                dve.wait_ge(rot_ok.sem, rot_ok.at(i, 3))
                nc.vector.tensor_tensor(rot_lo[:], rot[:], rot_hi[:], ALU.subtract).then_inc(rot_ok.sem, 1)
                low_part("k", 2, k_hi, k_lo)

                def bank_max(b, name, neg):
                    nc.vector.tensor_reduce(neg[:, b:b + 1], full(dve, i, name), AX.X, ALU.max, negate=True
                                            ).then_inc(neg_ok.sem, 1)

                def row_max(g):
                    if g >= 2:
                        dve.wait_ge(filled.sem, filled.at(i, fills.index(f"m{g - 2}") + 1))
                    for u, (t, heads) in enumerate(MAX_UNITS):
                        n = NM * g + u
                        k = len(heads)
                        dve.wait_ge(max_full.sem, max_full.at(i, n + 1))
                        src = ps_max[:, n % SM_BANKS, 0:k * (t + 1) * P].rearrange("p (h k) -> p h k", h=k)
                        nc.vector.tensor_reduce(neg_max[:, g % 2, heads[0]:heads[0] + k, t], src, AX.X, ALU.max,
                                                negate=True).then_inc(max_read.sem, 1)

                def heads_out(g):
                    bank = full(dve, i, f"y{g}").rearrange("p (t s c) -> p t s c", t=TB, s=G)
                    if g >= 1:
                        emptied(dve, i, f"y{g - 1}")
                    nc.vector.reciprocal(y_rec[:], bank[:, :, :, HD0]).then_inc(rec_ok.sem, 1)
                    dve.wait_ge(rec_ok.sem, rec_ok.at(i, g + 1))
                    nc.vector.tensor_tensor(attn[:, :, g * 32:g * 32 + 32].rearrange("p t (s d) -> p t s d", s=G),
                                            bank[:, :, :, 0:HD0], y_rec[:].unsqueeze(3).to_broadcast([P, TB, G, HD0]),
                                            ALU.mult).then_inc(read["dve"].sem, 1)

                for stage, n in LAYER0:
                    if stage == "logits_s":
                        for b in range(4):
                            bank_max(b, f"ls{b}", s_neg)
                    if stage == "dispatch":
                        for b in range(4):
                            emptied(dve, i, f"ls{b}")
                            nc.vector.reciprocal(s_rec[:, b:b + 1], s_sum[:, b:b + 1]).then_inc(srec_ok.sem, 1)
                        for t in (1, 3):
                            nc.vector.tensor_copy(disp_n[:, t], full(dve, i, f"dT{t}")).then_inc(read["dve"].sem, 1)
                    if stage == "max":
                        row_max(n)
                    if stage == "heads" and n + 1 < G:
                        row_max(n + 1)
                    if stage == "logits_c":
                        for b in range(4):
                            bank_max(b, f"lc{b}", c_neg)
                    if stage == "heads_out":
                        heads_out(n)
                    if stage == "experts":
                        for b in range(4):
                            emptied(dve, i, f"lc{b}")
                            nc.vector.reciprocal(c_rec[:, b:b + 1], c_sum[:, b:b + 1]).then_inc(srec_ok.sem, 1)
                        nc.vector.tensor_tensor(eo[:].rearrange("p m d -> p (m d)"), full(dve, i, "eo"),
                                                b2[:].rearrange("p m d -> p (m d)"), ALU.add).then_inc(read["dve"].sem, 1)
                    if stage == "combine":
                        for b in (1, 3):
                            nc.vector.tensor_copy(comb_s[:, b], full(dve, i, f"cT{b}")).then_inc(read["dve"].sem, 1)
                dve.wait_ge(res_loaded.sem, res_loaded.at(i, 16))
                dve.wait_ge(stored.sem, stored.at(i, 0))
                nc.vector.tensor_tensor(x1[:].rearrange("p t d -> p (t d)"), full(dve, i, "outT"),
                                        x_res[:].rearrange("p t d -> p (t d)"), ALU.add).then_inc(read["dve"].sem, 1)

        @block.tensor
        def _(pe):
            pe.wait_ge(loaded, all_loaded)
            pe.wait_ge(prep, 14)
            for b in range(4):
                ins = pe.transpose(ps_any[:, 0, b * P:b * P + P], slot_n[:, b], ident[:])
            ins.then_inc(prep_pe, 1)
            pe.wait_ge(prep_act, 1)
            with pe.Fori(0, batches) as i:
                def bank(name):
                    k = fills.index(name)
                    if k >= 2:
                        emptied(pe, i, fills.names[k - 2])
                    else:
                        for s in read.values():
                            pe.wait_ge(s.sem, s.at(i, 0))
                    return ps_any[:, k % 2]

                def turn(name, blocks):
                    out = bank(name)
                    for b, src in enumerate(blocks):
                        ins = pe.transpose(out[:, b * P:b * P + P], src, ident[:])
                    ins.then_inc(filled.sem, 1)

                def product(name, w, x, n=P):
                    pe.matmul(bank(name)[0:n], w, x, start=True, stop=True).then_inc(filled.sem, 1)

                pe.wait_ge(xn_ok.sem, xn_ok.at(i, TB))
                turn("xnT", [xn[:, t] for t in range(TB)])
                pe.wait_ge(xf_ok.sem, xf_ok.at(i, TB))
                turn("xfT", [xf[:, t] for t in range(TB)])
                emptied(pe, i, "xnT")
                product("ckv", w_kvd[:], xnT[:])
                product("q", w_q[:], xnT[:])
                emptied(pe, i, "ckv")
                out = bank("r")
                for n in range(2):
                    pe.matmul(out[2 * n * DR:(2 * n + 1) * DR], w_qr[:, n], xnT[:], start=True, stop=True)
                    ins = pe.matmul(out[(2 * n + 1) * DR:(2 * n + 2) * DR], w_kr[:, n], ckvT[:], start=True, stop=True)
                ins.then_inc(filled.sem, 1)
                product("k", w_k[:], ckvT[:])
                out = bank("v")
                for t in range(TB):
                    ins = pe.matmul(out[:, t * P:t * P + P], ckvT[:, t * P:t * P + P], w_v[:], start=True, stop=True)
                ins.then_inc(filled.sem, 1)

                def max_unit(g, u):
                    t, heads = MAX_UNITS[u]
                    n = NM * g + u
                    w = (t + 1) * P
                    if u == 0:
                        pe.wait_ge(stacked.sem, stacked.at(i, 16 * (12 + 2 * max(g + 1, 2))))
                    pe.wait_ge(max_read.sem, max_read.at(i, max(n + 1 - SM_BANKS, 0)))
                    for c, h in enumerate(heads):
                        out = ps_max[:, n % SM_BANKS, c * w:c * w + w]
                        pe.matmul(out, q_st[0:K_MAX0, g % 2, h, t * P:t * P + P], k_st[0:K_MAX0, g % 2, h, 0:w],
                                  start=True, stop=False)
                        ins = pe.matmul(out[:, t * P:w], ident_h[:], mask_h[:], start=False, stop=True)
                    ins.then_inc(max_full.sem, 1)

                def exp_unit(g, u):
                    n = 10 * g + u
                    if u == 0:
                        pe.wait_ge(row_in.sem, row_in.at(i, 16 * (g + 1)))
                    pe.wait_ge(exp_done.sem, exp_done.at(i, max(n + 1 - ST_BANKS, 0)))
                    for h, j, c in EXP0[u]:
                        w = T - j * P
                        ins = pe.matmul(ps_exp[:, n % ST_BANKS, c:c + w], k_st[0:K_ALL0, g % 2, h, j * P:j * P + P],
                                        q_st[0:K_ALL0, g % 2, h, j * P:T], start=True, stop=True)
                    ins.then_inc(exp_full.sem, 1)

                def values(g, part):
                    pe.wait_ge(masked.sem, masked.at(i, 4 * g + (1, 3, 4)[part]))
                    if part == 0:
                        pe.wait_ge(pv_read.sem, pv_read.at(i, g))
                        emptied(pe, i, "v")
                    first, last = PARTS0[part]
                    pieces = [(u, h, j, c) for u in range(first, last) for h, j, c in EXP0[u]]
                    pieces.sort(key=lambda x: (x[2], x[1]))
                    for u, h, j, c in pieces:
                        w = T - j * P
                        ins = pe.matmul(ps_out[32 * h:32 * h + 32, j * P:T], v_aug[:, j, G * g + h],
                                        probs[:, u, c:c + w], start=(part == 0), stop=(part == 2))
                    ins.then_inc(pv_done.sem, 1)

                def heads(g):
                    turns = list(range(NM)) if g + 1 < G else []
                    for part, (first, last) in enumerate(PARTS0):
                        for u in range(first, last):
                            exp_unit(g, u)
                            for _ in range(2 if u % 4 == 3 else 1):
                                if turns:
                                    max_unit(g + 1, turns.pop(0))
                        if 3 * g + part >= 1:
                            values(*divmod(3 * g + part - 1, 3))
                    while turns:
                        max_unit(g + 1, turns.pop(0))

                for stage, n in LAYER0:
                    if stage == "logits_s":
                        emptied(pe, i, "xfT")
                        for b in range(4):
                            product(f"ls{b}", snT[:, b * P:b * P + P], xfT[:])
                    if stage == "max":
                        for u in range(NM):
                            max_unit(n, u)
                    if stage == "turn_max":
                        pe.wait_ge(max_read.sem, max_read.at(i, NM * (n + 1)))
                        pe.transpose(bank(f"m{n}")[0:G * TB, 0:P], neg_max[:, n % 2].rearrange("p h t -> p (h t)"),
                                     ident[:]).then_inc(filled.sem, 1)
                    if stage == "heads":
                        heads(n)
                    if stage == "last":
                        values(G - 1, 2)
                    if stage == "heads_out":
                        pe.wait_ge(pv_read.sem, pv_read.at(i, n + 1))
                        turn(f"y{n}", [y_un[:, t * P:t * P + P] for t in range(TB)])
                    if stage == "dispatch":
                        pe.wait_ge(scaled.sem, scaled.at(i, 4))
                        for t in range(TB):
                            turn(f"dT{t}", [disp_s[:, b, t * P:t * P + P] for b in range(4)])
                        out = bank("slots")
                        for t in range(TB):
                            emptied(pe, i, f"dT{t}")
                            ins = pe.matmul(out, xf[:, t], disp_n[:, t], start=(t == 0), stop=(t == TB - 1))
                        ins.then_inc(filled.sem, 1)
                    if stage == "logits_c":
                        for b in range(4):
                            product(f"lc{b}", xfT[:, b * P:b * P + P], snT[:])
                    if stage == "experts":
                        emptied(pe, i, "slots")
                        for b in range(4):
                            out = bank(f"h{b}")
                            for hb in range(HB):
                                for ee in range(2):
                                    c, e = (hb * 2 + ee) * S0, 2 * b + ee
                                    ins = pe.matmul(out[:, c:c + S0], w1[:, e, hb * P:hb * P + P],
                                                    slotsT[:, e * S0:e * S0 + S0], start=True, stop=True)
                            ins.then_inc(filled.sem, 1)
                        out = bank("eo")
                        for b in range(4):
                            emptied(pe, i, f"h{b}")
                            for hb in range(HB):
                                for ee in range(2):
                                    ins = pe.matmul(out[S0 * ee:S0 * ee + S0, b * D:b * D + D],
                                                    hT[:, b, hb, ee * S0:ee * S0 + S0], w2[:, 2 * b + ee, hb],
                                                    start=(hb == 0), stop=(hb == HB - 1))
                        ins.then_inc(filled.sem, 1)
                    if stage == "combine":
                        pe.wait_ge(scaled.sem, scaled.at(i, 8))
                        for b in range(4):
                            turn(f"cT{b}", [comb_n[:, t, b * P:b * P + P] for t in range(TB)])
                emptied(pe, i, f"y{G - 1}")
                turn("atT", [attn[:, t] for t in range(TB)])
                out = bank("out")
                emptied(pe, i, "eo")
                for b in range(4):
                    emptied(pe, i, f"cT{b}")
                    pe.matmul(out, eo[:, b], comb_s[:, b], start=(b == 0), stop=False)
                emptied(pe, i, "atT")
                pe.matmul(out, w_o[:], attnT[:], start=False, stop=True).then_inc(filled.sem, 1)
                emptied(pe, i, "out")
                turn("outT", [outT[:, t * P:t * P + P] for t in range(TB)])


EXP1 = [[(0, 0, 0)], [(1, 0, 0)], [(0, 1, 0), (0, 3, 384)], [(1, 1, 0), (1, 3, 384)], [(0, 2, 0), (1, 2, 256)]]
K_B = HD1 + 1
PAIRS = H // 2
CHUNK = 4


def scores_of(p):
    exps = [("exp", p, u) for u in range(5)]
    if not p:
        return exps
    rec = [("rec", p - 1, t) for t in range(TB)]
    old = [("rec", p - 2, TB - 1), ("scaled", p - 2)] if p >= 2 else []
    return (exps[:1] + old + exps[1:2] + [("values", p - 1)] + exps[2:3] + [("sums", p - 1)] + rec[:1] + exps[3:4]
            + rec[1:2] + exps[4:] + rec[2:3])


def layer1_steps():
    def experts(first, last):
        return [(x, e) for e in range(first, last) for x in ("gate_in", "up_in")]

    def rows_of(g):
        return [("max", g, u) for u in range(NM)]

    def heads_in(g):
        return [("qk", g, k) for k in range(4)]

    def group(g, others, between, after):
        a, b = scores_of(2 * g), scores_of(2 * g + 1)
        return (weave(a, others) + weave(b[:7], weave(rows_of(g + 1), between)) + [("turn_max", g + 1)]
                + weave(b[7:], after))

    values_in = [("v", t, half) for t in range(TB) for half in range(2)]
    steps = group(0, experts(0, 3), experts(3, 4), heads_in(2) + experts(4, 5))
    steps += group(1, [("down", 0)] + experts(5, 8), experts(8, 9), heads_in(3) + experts(9, 10))
    steps += group(2, [("load", 0)] + experts(10, 11) + [("norm", 0)] + experts(11, 12) + [("scale", 0), ("down", 1)]
                   + experts(12, 13), experts(13, 15), experts(15, 17))
    steps += weave(scores_of(6), [("xnT", 0), ("lat", 0), ("down", 2), ("gate", 0)] + heads_in(0) + [("route", 0)])
    steps += weave(scores_of(7), [("down", 3), ("cT", 0)])
    steps += [("rec", 6, 3), ("scaled", 6), ("values", 7)] + values_in[:2] + [("sums", 7)]
    steps += weave(weave(values_in[2:], [("rec", 7, t) for t in range(TB)] + [("scaled", 7)]), rows_of(0))
    steps += heads_in(1)[:1] + [("turn_max", 0)] + heads_in(1)[1:2] + [("out", 0)] + heads_in(1)[2:] + [("outT", 0)]
    return steps


def early1(step):
    name, n = step[:2]
    return name in ("load", "norm", "scale", "xnT", "lat", "gate", "route", "cT", "v") or (
        name in ("max", "turn_max") and n == 0) or (name == "qk" and n <= 1)


def head_bank(step):
    _, n, k = step
    return f"{'qk'[k // 2]}{2 * n + k % 2}"


def layer1_plan(steps):
    plan = []
    for step in steps:
        name, n = step[:2]
        if name == "qk":
            plan.append((head_bank(step), "dve"))
        elif name == "v":
            plan.append((f"v{n}{step[2]}", "act"))
        elif name in ("xnT", "lat", "gate", "cT"):
            plan.append((name, "act"))
        elif name in ("out", "outT"):
            plan.append((name, "dve"))
        elif name in ("turn_max", "sums"):
            plan.append(({"turn_max": f"m{n}", "sums": f"s{n}"}[name], "act"))
        elif name in ("gate_in", "up_in", "down"):
            plan.append((f"{name[0]}{n}", "dve"))
    return plan


def experts_of(chunk):
    return range(CHUNK * chunk, min(CHUNK * chunk + CHUNK, E1 + 1))


def layer1(nc, a, x1_dram, out_dram, batches):
    with ExitStack() as ctx:
        def sb(name, shape, dt=F32):
            return ctx.enter_context(nc.sbuf_tensor("l1_" + name, shape, dt))

        def sig(name, per, begun=0):
            return Signal(ctx, nc, "l1_" + name, per, begun)

        def plain(name):
            return ctx.enter_context(nc.semaphore("l1_" + name))

        route_dram = nc.dram_tensor("route_scratch", [E1, T], F32, kind="Internal").ap()
        ps_max = ctx.enter_context(nc.psum_tensor("l1_ps_max", [P, 2, T], F32))
        ps_exp = ctx.enter_context(nc.psum_tensor("l1_ps_exp", [P, ST_BANKS, T], F32))
        ps_out = ctx.enter_context(nc.psum_tensor("l1_ps_out", [P, 2, T], F32))
        ps_any = ctx.enter_context(nc.psum_tensor("l1_ps_any", [P, 2, T], F32))

        ident = sb("ident", [P, P])
        ident_h = sb("ident_h", [P, P], BF16)
        masks = sb("masks", [P, 2, P])
        masks_h = sb("masks_h", [P, 2, P], BF16)
        w_kvd = sb("w_kvd", [P, D])
        w_kvu = sb("w_kvu", [P, 2, H * HD1])
        w_q = sb("w_q", [P, H * HD1])
        w_out = sb("w_out", [P, PAIRS, D])
        gate_w = sb("gate_w", [P, E1])
        bias = sb("bias", [P, E1])
        w_g = sb("w_g", [P, E1 + 1, D])
        w_u = sb("w_u", [P, E1 + 1, D])
        w_d = sb("w_d", [P, E1 + 1, D])
        ones = sb("ones", [P, HD1])
        neg_half = sb("neg_half", [P, TB])

        x_in = sb("x_in", [P, TB, D])
        x_res = sb("x_res", [P, TB, D])
        stats = sb("stats", [P, TB, 6])
        mv = sb("mv", [P, TB, 2])
        var_eps = sb("var_eps", [P, TB])
        rstd = sb("rstd", [P, TB])
        xn = sb("xn", [P, TB, D])
        xnT = sb("xnT", [P, T])
        latT = sb("latT", [P, T])
        q_hi = sb("q_hi", [P, 2, T], F16)
        q_lo = sb("q_lo", [P, 2, T], F16)
        k_hi = sb("k_hi", [P, 2, T], F16)
        k_lo = sb("k_lo", [P, 2, T], F16)
        q_a = sb("q_a", [P, 2, G, T], F16)
        k_a = sb("k_a", [P, 2, G, T], F16)
        q_b = sb("q_b", [P, 2, G, T], F16)
        k_b = sb("k_b", [P, 2, G, T], F16)
        v = sb("v", [P, TB, H * HD1])
        neg_max = sb("neg_max", [P, 2, G, TB])
        max_row = sb("max_row", [G * TB, 2, P], F16)
        probs = sb("probs", [P, 2, 5, T])
        key_sum = sb("key_sum", [P, G, T])
        yT = sb("yT", [P, PAIRS, T])
        den = sb("den", [P, T])
        rec = sb("rec", [P, T])
        spread = sb("spread", [P, 2, CHUNK, T])
        th = sb("th", [P, TB, E1])
        score = sb("score", [P, TB, E1])
        select = sb("select", [P, TB, E1])
        top = sb("top", [P, TB, TOP])
        others = sb("others", [P, TB, E1])
        keep = sb("keep", [P, TB, E1])
        kept = sb("kept", [P, TB, E1])
        kept_sum = sb("kept_sum", [P, TB])
        kept_rec = sb("kept_rec", [P, TB])
        weight = sb("weight", [P, TB, E1])
        weightT = sb("weightT", [E1, T])
        tanh = sb("tanh", [P, 2, T])
        gated = sb("gated", [P, T])
        hidden = sb("hidden", [P, 2, T])
        hw = sb("hw", [P, 2, CHUNK, T])
        acc = sb("acc", [P, T])
        outT = gated

        steps = layer1_steps()
        ahead = [x for x in steps if early1(x)]
        rest = [x for x in steps if not early1(x)]
        first = Fills(layer1_plan(ahead))
        steady = Fills(layer1_plan(steps), first, layer1_plan(steps))
        final = Fills(layer1_plan(rest), first, layer1_plan(steps))

        def run(eng, turn):
            turn(0, 0, first, ahead)
            with eng.Fori(0, batches - 1) as i:
                turn(i, i + 1, steady, steps)
            turn(batches - 1, None, final, rest)

        loaded, prep, prep_pool = [plain(n) for n in ("loaded", "prep", "prep_pool")]
        sp_passed, pool_passed, dve_passed = [plain(f"{n}_passed") for n in ("sp", "pool", "dve")]
        x_loaded = sig("x_loaded", 16)
        res_loaded = sig("res_loaded", 16)
        stacked = sig("stacked", 16 * 12 * G)
        row_in = sig("row_in", 16 * G)
        route_out = sig("route_out", 16)
        spread_in = [sig(f"spread_in{n}", 16 * E1 // CHUNK // 2) for n in range(2)]
        stored = sig("stored", 16, 16)
        stats_ok = sig("stats_ok", 2 * TB + 1)
        rstd_ok = sig("rstd_ok", 1)
        xn_ok = sig("xn_ok", TB, 1)
        filled, read = plain("filled"), {n: plain(f"read_{n}") for n in ("act", "dve")}
        hi_ok = sig("hi_ok", 4 * G)
        max_full = sig("max_full", NM * G)
        max_read = sig("max_read", NM * G, 1)
        exp_full = sig("exp_full", 5 * PAIRS, 1)
        exp_done = sig("exp_done", 5 * PAIRS, 1)
        added = sig("added", 4 * PAIRS, 8)
        pv_done = sig("pv_done", PAIRS, 2)
        rec_ok = sig("rec_ok", TB * PAIRS)
        normed = sig("normed", PAIRS, 2)
        route_ok = sig("route_ok", 15)
        tanh_ok = sig("tanh_ok", E1 + 1)
        hw_ok = sig("hw_ok", E1 + 1, 1)

        def emptied(eng, i, fills, name):
            eng.wait_ge(read[fills.reader[name]], fills.emptied(i, name))

        def full(eng, i, fills, name):
            eng.wait_ge(filled, fills.filled(i, name))
            return ps_any[:, fills.bank(name)]

        block = ctx.enter_context(nc.Block())

        loads = [(ident[:], a["ident"]), (masks[:, 0], a["mask"]), (masks[:, 1], a["maskT"]),
                 (w_kvd[:], a["L1_attn_w_kv_down"]), (gate_w[:], a["L1_ffn_gate_w"]),
                 (bias[:], a["L1_ffn_expert_bias"].partition_broadcast(P)), (w_q[:], a["L1_attn_w_q"]),
                 (w_kvu[:], a["L1_attn_w_kv_up"].rearrange("p (s n) -> p s n", s=2)),
                 (w_out[:], a["L1_attn_w_out"].rearrange("(k p) d -> p k d", p=P))]
        for w, name in ((w_g, "gate"), (w_u, "up"), (w_d, "down")):
            loads += [(w[:, 0:E1], a[f"L1_ffn_w_{name}"]), (w[:, E1], a[f"L1_ffn_shared_{name}_w"])]
        all_loaded = 16 * len(loads)

        @block.sync
        def _(sp):
            for dst, src in loads:
                sp.dma_start(dst, src).then_inc(loaded, 16)
            def turn(i, b, fills, steps):
                for step in steps:
                    name, n = step[:2]
                    if name == "load":
                        sp.wait_ge(xn_ok.sem, xn_ok.at(b, 0))
                        release(sp, sp_passed)
                        sp.dma_start(x_in[:], x1_dram[b].rearrange("(t p) d -> p t d", p=P)).then_inc(x_loaded.sem, 16)
                    if name == "qk" and step[2] % 2:
                        j = b if early1(step) else i
                        side = step[2] // 2
                        emptied(sp, i, fills, head_bank(step))
                        s = n % 2
                        if side == 0:
                            release(sp, sp_passed)
                            if n >= 2:
                                sp.wait_ge(exp_full.sem, exp_full.at(i, 10 * (n - 1)))
                            elif fills is not first:
                                sp.wait_ge(exp_full.sem, exp_full.at(i, 30 + 10 * n))
                        for r in range(2):
                            rows = slice(HD1 * r, HD1 * r + HD1)
                            for dst, to, src in (((q_a, 0, q_hi), (q_a, HD1, q_hi), (q_b, 0, q_lo)),
                                                 ((k_a, 0, k_hi), (k_a, HD1, k_lo), (k_b, 0, k_hi)))[side]:
                                sp.dma_start(dst[to:to + HD1, s].rearrange("p (q r) t -> p q r t", r=2)[:, :, r],
                                             src[rows]).then_inc(stacked.sem, 16)
                    if name == "turn_max":
                        emptied(sp, i, fills, f"m{n}")
                        sp.dma_start(q_b[HD1:K_B, n % 2], max_row[:, n % 2]).then_inc(row_in.sem, 16)
                    if name == "cT":
                        emptied(sp, i, fills, "cT")
                        release(sp, sp_passed)
                        sp.wait_ge(hw_ok.sem, hw_ok.at(b, 0))
                        sp.dma_start(route_dram, weightT[:]).then_inc(route_out.sem, 16)
                        sp.wait_ge(route_out.sem, route_out.at(b, 16))
                    if name == "cT" or (name == "up_in" and n in (CHUNK, 2 * CHUNK)):
                        if name == "up_in":
                            sp.wait_ge(hw_ok.sem, hw_ok.at(i, n))
                        for c in ((0, 1) if name == "cT" else (n // CHUNK + 1,)):
                            sp.dma_start(spread[:, c % 2],
                                         route_dram[CHUNK * c:CHUNK * c + CHUNK].partition_broadcast(P)
                                         ).then_inc(spread_in[c % 2].sem, 16)
                    if step == ("up_in", E1):
                        sp.wait_ge(stored.sem, stored.at(i, 0))
                        release(sp, sp_passed)
                        sp.dma_start(x_res[:], x1_dram[i].rearrange("(t p) d -> p t d", p=P)
                                     ).then_inc(res_loaded.sem, 16)

            run(sp, turn)

        @block.gpsimd
        def _(pool):
            for s in (added, hw_ok):
                pool.sem_inc(s.sem, s.begun)
            nc.gpsimd.memset(neg_half[:], -0.5).then_inc(prep_pool, 1)
            pool.wait_ge(prep_pool, 1)
            pool.wait_ge(loaded, all_loaded)

            def turn(i, b, fills, steps):
                for step in steps:
                    name, n = step[:2]
                    if name == "norm":
                        pool.wait_ge(stats_ok.sem, stats_ok.at(b, 2 * TB + 1))
                        nc.gpsimd.tensor_tensor(rstd[:], var_eps[:], neg_half[:], ALU.pow).then_inc(rstd_ok.sem, 1)
                    if name == "exp":
                        s = key_sum[:, 2 * (n % 2):2 * (n % 2) + 2]
                        u = probs[:, n % 2]
                        if step[2] == 3:
                            if n >= 2:
                                pool.wait_ge(filled, fills.filled(i, f"s{n - 2}"))
                            else:
                                pool.wait_ge(filled, fills.before(i, "all"))
                            pool.wait_ge(exp_done.sem, exp_done.at(i, 5 * n + 4))
                            release(pool, pool_passed)
                            nc.gpsimd.tensor_copy(s[:, :, 0:P], u[:, 0:2, 0:P]).then_inc(added.sem, 1)
                            nc.gpsimd.tensor_tensor(s[:, :, P:T], u[:, 0:2, P:T], u[:, 2:4, 0:3 * P], ALU.add
                                                    ).then_inc(added.sem, 1)
                        if step[2] == 4:
                            pool.wait_ge(exp_done.sem, exp_done.at(i, 5 * n + 5))
                            pool.wait_ge(added.sem, added.at(i, 4 * n + 2))
                            nc.gpsimd.tensor_tensor(s[:, :, 2 * P:T], s[:, :, 2 * P:T],
                                                    u[:, 4].rearrange("p (h q) -> p h q", h=2), ALU.add
                                                    ).then_inc(added.sem, 1)
                            pool.wait_ge(added.sem, added.at(i, 4 * n + 3))
                            nc.gpsimd.tensor_tensor(s[:, :, 3 * P:T], s[:, :, 3 * P:T], u[:, 2:4, 3 * P:T], ALU.add
                                                    ).then_inc(added.sem, 1)
                    if name == "up_in":
                        c = n // CHUNK
                        if n % CHUNK == 0:
                            if c >= 2:
                                pool.wait_ge(filled, fills.filled(i, f"d{c - 2}"))
                            else:
                                pool.wait_ge(filled, fills.before(i, "all"))
                        emptied(pool, i, fills, f"u{n}")
                        dst = hw[:, c % 2, n % CHUNK]
                        if n < E1:
                            pool.wait_ge(spread_in[c % 2].sem, spread_in[c % 2].at(i, 16 * (c // 2 + 1)))
                            nc.gpsimd.tensor_tensor(dst, hidden[:, n % 2], spread[:, c % 2, n % CHUNK], ALU.mult
                                                    ).then_inc(hw_ok.sem, 1)
                        else:
                            release(pool, pool_passed)
                            nc.gpsimd.tensor_scalar(dst, hidden[:, n % 2], 0.5, None, ALU.mult).then_inc(hw_ok.sem, 1)

            run(pool, turn)

        @block.scalar
        def _(act):
            for s in (exp_done, stored):
                act.sem_inc(s.sem, s.begun)

            def turn(i, b, fills, steps):
                def copy(name, dst):
                    nc.scalar.activation(dst, full(act, i, fills, name), ACT.Copy).then_inc(read["act"], 1)

                for step in steps:
                    name, n = step[:2]
                    if name == "xnT":
                        copy("xnT", xnT[:])
                    if name == "lat":
                        copy("lat", latT[:])
                    if name == "gate":
                        nc.scalar.activation(th[:].rearrange("p t e -> p (t e)"),
                                             full(act, i, fills, "gate")[:, 0:TB * E1], ACT.Tanh, scale=0.5
                                             ).then_inc(read["act"], 1)
                    if name == "qk":
                        j = b if early1(step) else i
                        if step[2] == 0:
                            if n >= 1:
                                act.wait_ge(stacked.sem, stacked.at(j, 16 * 12 * n))
                            elif fills is not first:
                                act.wait_ge(stacked.sem, stacked.at(i, 16 * 12 * G))
                        nc.scalar.activation((q_hi, k_hi)[step[2] // 2][:, step[2] % 2],
                                             full(act, i, fills, head_bank(step)), ACT.Copy).then_inc(hi_ok.sem, 1)
                    if name == "v":
                        copy(f"v{n}{step[2]}", v[:, n, step[2] * T:step[2] * T + T])
                    if name == "sums":
                        act.wait_ge(normed.sem, normed.at(i, n))
                        copy(f"s{n}", den[:])
                    if name == "cT":
                        nc.scalar.activation(weightT[:], full(act, i, fills, "cT")[0:E1], ACT.Copy
                                             ).then_inc(read["act"], 1)
                    if name == "turn_max":
                        nc.scalar.activation(max_row[:, n % 2], full(act, i, fills, f"m{n}")[0:G * TB, 0:P], ACT.Copy,
                                             scale=1.0 / SHIFT).then_inc(read["act"], 1)
                    if name == "exp":
                        u = step[2]
                        if u == 0:
                            act.wait_ge(pv_done.sem, pv_done.at(i, n - 1))
                            act.wait_ge(added.sem, added.at(i, 4 * (n - 1)))
                        act.wait_ge(exp_full.sem, exp_full.at(i, 5 * n + u + 1))
                        nc.scalar.activation(probs[:, n % 2, u], ps_exp[:, (5 * n + u) % ST_BANKS], ACT.Exp,
                                             scale=float(HD1) ** -0.5).then_inc(exp_done.sem, 1)
                    if name == "gate_in":
                        if n >= 2:
                            emptied(act, i, fills, f"g{n - 2}")
                        nc.scalar.activation(tanh[:, n % 2], full(act, i, fills, f"g{n}"), ACT.Tanh, scale=0.5
                                             ).then_inc(tanh_ok.sem, 1)
                    if name == "outT":
                        emptied(act, i, fills, "outT")
                        act.dma_start(out_dram[i].rearrange("(t p) d -> p t d", p=P), x_res[:]
                                      ).then_inc(stored.sem, 16)

            run(act, turn)
            act.wait_ge(stored.sem, 16 * batches + 16)

        @block.vector
        def _(dve):
            for s in (xn_ok, max_read, normed):
                dve.sem_inc(s.sem, s.begun)
            nc.vector.memset(k_b[HD1:P], SHIFT).then_inc(prep, 1)
            nc.vector.memset(ones[:], 1.0).then_inc(prep, 1)
            dve.wait_ge(loaded, all_loaded)
            nc.vector.tensor_copy(ident_h[:], ident[:]).then_inc(prep, 1)
            nc.vector.tensor_copy(masks_h[:], masks[:]).then_inc(prep, 1)

            def turn(i, b, fills, steps):
                def route():
                    def done(k):
                        dve.wait_ge(route_ok.sem, route_ok.at(b, k))

                    emptied(dve, i, fills, "gate")
                    nc.vector.tensor_scalar(score[:], th[:], 0.5, 0.5, ALU.mult, ALU.add).then_inc(route_ok.sem, 1)
                    done(1)
                    nc.vector.tensor_tensor(select[:], score[:], bias[:].unsqueeze(1).to_broadcast([P, TB, E1]), ALU.add
                                            ).then_inc(route_ok.sem, 1)
                    done(2)
                    release(dve, dve_passed)
                    for t in range(TB):
                        nc.vector.max(top[:, t], select[:, t]).then_inc(route_ok.sem, 1)
                    done(2 + TB)
                    release(dve, dve_passed)
                    for t in range(TB):
                        nc.vector.match_replace(out=others[:, t], in_to_replace=top[:, t], in_values=select[:, t],
                                                imm_value=-1e30).then_inc(route_ok.sem, 1)
                    done(2 + 2 * TB)
                    nc.vector.tensor_tensor(keep[:], select[:], others[:], ALU.not_equal).then_inc(route_ok.sem, 1)
                    done(11)
                    nc.vector.tensor_tensor(kept[:], score[:], keep[:], ALU.mult).then_inc(route_ok.sem, 1)
                    done(12)
                    nc.vector.tensor_reduce(kept_sum[:], kept[:], AX.X, ALU.add).then_inc(route_ok.sem, 1)
                    done(13)
                    nc.vector.reciprocal(kept_rec[:], kept_sum[:]).then_inc(route_ok.sem, 1)
                    done(14)
                    nc.vector.scalar_tensor_tensor(out=weight[:], in0=kept[:], scalar=ROUTE / 2,
                                                   in1=kept_rec[:].unsqueeze(2).to_broadcast([P, TB, E1]),
                                                   op0=ALU.mult, op1=ALU.mult).then_inc(route_ok.sem, 1)

                for step in steps:
                    name, n = step[:2]
                    j = b if early1(step) else i
                    if name == "norm":
                        dve.wait_ge(x_loaded.sem, x_loaded.at(b, 16))
                        for t in range(TB):
                            nc.vector.bn_stats(stats[:, t], x_in[:, t]).then_inc(stats_ok.sem, 1)
                        dve.wait_ge(stats_ok.sem, stats_ok.at(b, TB))
                        release(dve, dve_passed)
                        for t in range(TB):
                            nc.vector.bn_aggr(mv[:, t], stats[:, t]).then_inc(stats_ok.sem, 1)
                        dve.wait_ge(stats_ok.sem, stats_ok.at(b, 2 * TB))
                        nc.vector.tensor_scalar(var_eps[:], mv[:, :, 1], EPS, None, ALU.add).then_inc(stats_ok.sem, 1)
                    if name == "scale":
                        dve.wait_ge(rstd_ok.sem, rstd_ok.at(b, 1))
                        for t in range(TB):
                            nc.vector.tensor_scalar(xn[:, t], x_in[:, t], mv[:, t, 0:1], rstd[:, t:t + 1], ALU.subtract,
                                                    ALU.mult).then_inc(xn_ok.sem, 1)
                    if name == "qk":
                        hi, lo = ((q_hi, q_lo), (k_hi, k_lo))[step[2] // 2]
                        r = step[2] % 2
                        dve.wait_ge(hi_ok.sem, hi_ok.at(j, 4 * n + step[2] + 1))
                        nc.vector.tensor_tensor(lo[:, r], full(dve, i, fills, head_bank(step)), hi[:, r],
                                                ALU.subtract).then_inc(read["dve"], 1)
                    if name == "max":
                        u = step[2]
                        if u == 0:
                            if n in (1, 2):
                                dve.wait_ge(filled, fills.before(i, "all"))
                            elif n == 3:
                                dve.wait_ge(filled, fills.filled(i, "m1"))
                            elif fills is not first:
                                dve.wait_ge(filled, fills.filled(i, "m2"))
                        t, heads = MAX_UNITS[u]
                        m = NM * n + u
                        k = len(heads)
                        dve.wait_ge(max_full.sem, max_full.at(j, m + 1))
                        src = ps_max[:, m % 2, 0:k * (t + 1) * P].rearrange("p (h k) -> p h k", h=k)
                        nc.vector.tensor_reduce(neg_max[:, n % 2, heads[0]:heads[0] + k, t], src, AX.X, ALU.max,
                                                negate=True).then_inc(max_read.sem, 1)
                    if name == "route":
                        route()
                    if name == "rec":
                        cols = slice(P * step[2], P * step[2] + P)
                        if step[2] == 0:
                            emptied(dve, i, fills, f"s{n}")
                            dve.wait_ge(normed.sem, normed.at(i, n))
                        nc.vector.reciprocal(rec[:, cols], den[:, cols]).then_inc(rec_ok.sem, 1)
                    if name == "scaled":
                        dve.wait_ge(pv_done.sem, pv_done.at(i, n + 1))
                        dve.wait_ge(rec_ok.sem, rec_ok.at(i, TB * (n + 1)))
                        nc.vector.tensor_tensor(yT[:, n], ps_out[:, n % 2], rec[:], ALU.mult).then_inc(normed.sem, 1)
                    if name == "gate_in":
                        if n >= 1:
                            emptied(dve, i, fills, f"u{n - 1}")
                        dve.wait_ge(tanh_ok.sem, tanh_ok.at(i, n + 1))
                        nc.vector.scalar_tensor_tensor(out=gated[:], in0=tanh[:, n % 2], scalar=1.0,
                                                       in1=full(dve, i, fills, f"g{n}"), op0=ALU.add, op1=ALU.mult
                                                       ).then_inc(read["dve"], 1)
                    if name == "up_in":
                        emptied(dve, i, fills, f"g{n}")
                        dve.wait_ge(hw_ok.sem, hw_ok.at(i, max(n - 1, 0)))
                        nc.vector.tensor_tensor(hidden[:, n % 2], full(dve, i, fills, f"u{n}"), gated[:], ALU.mult
                                                ).then_inc(read["dve"], 1)
                    if name == "down":
                        bank = full(dve, i, fills, f"d{n}")
                        if n == 0:
                            dve.wait_ge(read["dve"], fills.before(i, "dve"))
                            nc.vector.tensor_copy(acc[:], bank).then_inc(read["dve"], 1)
                        else:
                            emptied(dve, i, fills, f"d{n - 1}")
                            nc.vector.tensor_tensor(acc[:], bank, acc[:], ALU.add).then_inc(read["dve"], 1)
                    if name == "out":
                        emptied(dve, i, fills, "d3")
                        emptied(dve, i, fills, f"u{E1}")
                        nc.vector.tensor_tensor(outT[:], full(dve, i, fills, "out"), acc[:], ALU.add
                                                ).then_inc(read["dve"], 1)
                    if name == "outT":
                        dve.wait_ge(res_loaded.sem, res_loaded.at(i, 16))
                        nc.vector.tensor_tensor(x_res[:].rearrange("p t d -> p (t d)"), full(dve, i, fills, "outT"),
                                                x_res[:].rearrange("p t d -> p (t d)"), ALU.add
                                                ).then_inc(read["dve"], 1)

            run(dve, turn)

        @block.tensor
        def _(pe):
            for s in (exp_full, pv_done):
                pe.sem_inc(s.sem, s.begun)
            pe.wait_ge(loaded, all_loaded)
            pe.wait_ge(prep, 4)

            def turn(i, b, fills, steps):
                def bank(name):
                    k = fills.names.index(name)
                    if k >= 2:
                        emptied(pe, i, fills, fills.names[k - 2])
                    elif fills is not first:
                        for who, sem in read.items():
                            pe.wait_ge(sem, fills.before(i, who))
                    return ps_any[:, fills.bank(name)]

                def turned(name, blocks):
                    out = bank(name)
                    for c, src in enumerate(blocks):
                        ins = pe.transpose(out[0:src.shape[-1], c * P:c * P + P], src, ident[:])
                    ins.then_inc(filled, 1)

                def product(name, w, x):
                    pe.matmul(bank(name), w, x, start=True, stop=True).then_inc(filled, 1)

                for step in steps:
                    name, n = step[:2]
                    j = b if early1(step) else i
                    if name == "xnT":
                        pe.wait_ge(xn_ok.sem, xn_ok.at(b, TB))
                        turned("xnT", [xn[:, t] for t in range(TB)])
                    if name == "lat":
                        emptied(pe, i, fills, "xnT")
                        product("lat", w_kvd[:], xnT[:])
                    if name == "gate":
                        out = bank("gate")
                        for t in range(TB):
                            ins = pe.matmul(out[:, t * E1:t * E1 + E1], xnT[:, t * P:t * P + P], gate_w[:],
                                            start=True, stop=True)
                        ins.then_inc(filled, 1)
                    if name == "qk":
                        p = 2 * n + step[2] % 2
                        if step[2] < 2:
                            product(f"q{p}", w_q[:, p * P:p * P + P], xnT[:])
                        else:
                            if n == 0:
                                emptied(pe, i, fills, "lat")
                            product(f"k{p}", w_kvu[:, 0, p * P:p * P + P], latT[:])
                    if name == "v":
                        half = step[2]
                        product(f"v{n}{half}", latT[:, n * P:n * P + P], w_kvu[:, 1, half * T:half * T + T])
                    if name == "cT":
                        pe.wait_ge(route_ok.sem, route_ok.at(b, 15))
                        turned("cT", [weight[:, t] for t in range(TB)])
                    if name == "max":
                        t, heads = MAX_UNITS[step[2]]
                        m = NM * n + step[2]
                        w = (t + 1) * P
                        if step[2] == 0:
                            pe.wait_ge(stacked.sem, stacked.at(j, 16 * 12 * (n + 1)))
                        pe.wait_ge(max_read.sem, max_read.at(j, max(m - 1, 0)))
                        for c, h in enumerate(heads):
                            out = ps_max[:, m % 2, c * w:c * w + w]
                            pe.matmul(out, q_a[:, n % 2, h, t * P:t * P + P], k_a[:, n % 2, h, 0:w],
                                      start=True, stop=False)
                            ins = pe.matmul(out[:, t * P:w], ident_h[:], masks_h[:, 0], start=False, stop=True)
                        ins.then_inc(max_full.sem, 1)
                    if name == "turn_max":
                        pe.wait_ge(max_read.sem, max_read.at(j, NM * (n + 1)))
                        pe.transpose(bank(f"m{n}")[0:G * TB, 0:P], neg_max[:, n % 2].rearrange("p h t -> p (h t)"),
                                     ident[:]).then_inc(filled, 1)
                    if name == "exp":
                        m = 5 * n + step[2]
                        g = n // 2
                        if step[2] == 0 and n % 2 == 0:
                            pe.wait_ge(row_in.sem, row_in.at(i, 16 * (g + 1)))
                        pe.wait_ge(exp_done.sem, exp_done.at(i, max(m + 1 - ST_BANKS, 0)))
                        for r, k, c in EXP1[step[2]]:
                            h = 2 * (n % 2) + r
                            w = T - k * P
                            out = ps_exp[:, m % ST_BANKS, c:c + w]
                            pe.matmul(out, k_a[:, g % 2, h, k * P:k * P + P], q_a[:, g % 2, h, k * P:T],
                                      start=True, stop=False)
                            pe.matmul(out, k_b[0:K_B, g % 2, h, k * P:k * P + P], q_b[0:K_B, g % 2, h, k * P:T],
                                      start=False, stop=False)
                            ins = pe.matmul(out[:, 0:P], ident_h[:], masks_h[:, 1], start=False, stop=True)
                        ins.then_inc(exp_full.sem, 1)
                    if name == "values":
                        if n == 0:
                            pe.wait_ge(read["act"], fills.before(i, "act"))
                        pe.wait_ge(normed.sem, normed.at(i, n - 1))
                        pe.wait_ge(exp_done.sem, exp_done.at(i, 5 * n + 5))
                        pieces = sorted([(k, r, u, c) for u in range(5) for r, k, c in EXP1[u]])
                        for k, r, u, c in pieces:
                            h = 2 * n + r
                            ins = pe.matmul(ps_out[HD1 * r:HD1 * r + HD1, n % 2, k * P:T], v[:, k, h * HD1:h * HD1 + HD1],
                                            probs[:, n % 2, u, c:c + T - k * P], start=(k == 0), stop=(k == TB - 1))
                        ins.then_inc(pv_done.sem, 1)
                    if name == "sums":
                        pe.wait_ge(added.sem, added.at(i, 4 * (n + 1)))
                        out = bank(f"s{n}")
                        for r in range(2):
                            ins = pe.matmul(out[HD1 * r:HD1 * r + HD1], ones[:], key_sum[:, 2 * (n % 2) + r],
                                            start=True, stop=True)
                        ins.then_inc(filled, 1)
                    if name == "gate_in":
                        product(f"g{n}", w_g[:, n], xnT[:])
                    if name == "up_in":
                        product(f"u{n}", w_u[:, n], xnT[:])
                    if name == "down":
                        out = bank(f"d{n}")
                        for k in range(CHUNK):
                            e = CHUNK * n + k
                            pe.wait_ge(hw_ok.sem, hw_ok.at(i, e + 1))
                            ins = pe.matmul(out, w_d[:, e], hw[:, n % 2, k], start=(k == 0), stop=(k == CHUNK - 1))
                        ins.then_inc(filled, 1)
                    if name == "out":
                        out = bank("out")
                        pe.wait_ge(hw_ok.sem, hw_ok.at(i, E1 + 1))
                        pe.matmul(out, w_d[:, E1], hw[:, 0, 0], start=True, stop=False)
                        for p in range(PAIRS):
                            pe.wait_ge(normed.sem, normed.at(i, p + 1))
                            ins = pe.matmul(out, w_out[:, p], yT[:, p], start=False, stop=(p == PAIRS - 1))
                        ins.then_inc(filled, 1)
                    if name == "outT":
                        emptied(pe, i, fills, "out")
                        turned("outT", [outT[:, t * P:t * P + P] for t in range(TB)])

            run(pe, turn)


def build(nc, a, out, batches):
    x1_dram = nc.dram_tensor("x1_scratch", [batches, T, D], F32, kind="Internal").ap()
    layer0(nc, a, x1_dram, batches)
    layer1(nc, a, x1_dram, out, batches)


def constants():
    cos, sin = rotary_tables()
    q, k = np.arange(P)[:, None], np.arange(P)[None, :]
    return {"ident": np.eye(P, dtype=np.float32), "cos": cos, "sin": sin,
            "mask": np.where(k > q, np.float32(-1e30), np.float32(0)),
            "maskT": np.where(q > k, np.float32(-1e30), np.float32(0))}


def lay_out(inputs):
    laid = {n: np.asarray(v) for n, v in inputs.items()}
    for n in ("L1_ffn_w_gate", "L1_ffn_w_up", "L1_ffn_w_down"):
        laid[n] = laid[n].transpose(2, 0, 1)
    for n in ("L1_ffn_gate_w", "L1_ffn_shared_gate_w", "L1_ffn_shared_up_w", "L1_ffn_shared_down_w"):
        laid[n] = laid[n].T
    laid["L0_ffn_b1"] = laid["L0_ffn_b1"].reshape(E0, HB, P).transpose(2, 0, 1)
    laid.update(constants())
    return {n: np.ascontiguousarray(v) for n, v in laid.items()}


def kernel(**inputs):
    import concourse.bacc as bacc
    from concourse.bass_utils import run_bass_kernel_spmd

    nc = bacc.Bacc("TRN2", target_bir_lowering=False, num_devices=1)
    laid = lay_out(inputs)
    arrays, a = {}, {}
    for n, v in laid.items():
        arrays[f"in_{n}"] = v
        a[n] = nc.dram_tensor(f"in_{n}", v.shape, mybir.dt.from_np(v.dtype), kind="ExternalInput").ap()
    shape = laid["L0_attn_x"].shape
    out = nc.dram_tensor("out_0", shape, F32, kind="ExternalOutput").ap()
    build(nc, a, out, shape[0])
    r = run_bass_kernel_spmd(nc, [arrays], core_ids=[0])
    return r.results[0]["out_0"]
```

```python
from contextlib import ExitStack

import numpy as np

import concourse.bass as bass
from concourse import mybir

ALU = mybir.AluOpType
ACT = mybir.ActivationFunctionType
AX = mybir.AxisListType
F32 = mybir.dt.float32
F16 = mybir.dt.float16
BF16 = mybir.dt.bfloat16

P = 128
D = 128
T = 512
TB = T // P
H = 16
G = 4
HD0, DR = 8, 32
HD1 = 64
E0, S0 = 8, 64
HID = 512
HB = HID // P
E1 = 16
TOP = 8
EPS = 1e-5
ROUTE = 2.826
SHIFT = 256.0
K_ROPE = 3 * DR
K_MAX0 = K_ROPE + 3 * HD0
K_ALL0 = K_MAX0 + 1

MAX_UNITS = [(0, (0, 1, 2, 3)), (1, (0, 1)), (1, (2, 3))] + [(t, (h,)) for t in (2, 3) for h in range(4)]
NM = len(MAX_UNITS)
EXP0 = ([[(h, 0, 0)] for h in range(4)] + [[(h, 1, 0), (h, 3, 384)] for h in range(4)]
        + [[(h, 2, 0), (h + 1, 2, 256)] for h in (0, 2)])
RING = 4
ST_BANKS = 2


class Signal:

    def __init__(self, ctx, nc, name, per, begun=0):
        self.sem = ctx.enter_context(nc.semaphore(name))
        self.per, self.begun = per, begun

    def at(self, i, n):
        assert n + self.begun > 0
        return i * self.per + (n + self.begun)


class Fills:

    def __init__(self, plan, first=None, steady=(), order=None):
        self.names = [n for n, _ in plan]
        self.reader = dict(plan)
        self.order = order or self.names
        self.start = {r: first.count(r) if first else 0 for r in ("all", "act", "dve")}
        self.per = {"all": len(steady)} | {r: sum(1 for _, x in steady if x == r) for r in ("act", "dve")}
        self.ends = [[first.reader[n] for n in first.names], [r for _, r in steady]] if first else []
        assert len(plan) == len(self.reader) and len(steady) % RING == 0 and sorted(self.order) == sorted(self.names)
        assert self.order[1 - RING:] == self.names[1 - RING:]

    def count(self, reader):
        return sum(1 for n in self.names if reader in ("all", self.reader[n]))

    def before(self, i, who, but=0):
        last = min(e[len(e) - but:].count(who) for e in self.ends)
        return i * self.per[who] + (self.start[who] - last)

    def filled(self, i, name):
        return i * self.per["all"] + (self.start["all"] + self.names.index(name) + 1)

    def emptied(self, i, name):
        who = self.reader[name]
        upto = self.order[:self.order.index(name) + 1]
        return i * self.per[who] + (self.start[who] + sum(1 for n in upto if self.reader[n] == who))

    def bank(self, name):
        return (self.start["all"] + self.names.index(name)) % RING


def put_off(steps, seconds, before):
    out, waiting = [], []
    for step in steps:
        for x in [x for x in waiting if x[0] <= 0 or before(x[1], step)]:
            out.append(x[1])
            waiting.remove(x)
            if x[1][0] in seconds:
                name, lag = seconds[x[1][0]]
                waiting.append([lag, (name,) + x[1][1:]])
        out.append(step)
        for x in waiting:
            x[0] -= 1
        if step[0] in seconds:
            name, lag = seconds[step[0]]
            waiting.append([lag, (name,) + step[1:]])
    assert not waiting
    return out


def weave(steps, others):
    out, k = [], 0
    for n, step in enumerate(steps):
        out.append(step)
        while k < len(others) and (k + 1) * len(steps) <= (n + 1) * len(others) + len(steps) // 2:
            out.append(others[k])
            k += 1
    return out + list(others[k:])


def release(eng, passed):
    eng.sem_inc(passed, 1)


def rotary_tables():
    inv = np.float32(1.0) / np.float32(10000.0) ** (np.arange(0, DR, 2, dtype=np.float32) / np.float32(DR))
    angle = np.outer(np.arange(T, dtype=np.float32), inv).T
    cos, sin = np.cos(angle), np.sin(angle)
    rows = [np.concatenate([cos, cos]), np.concatenate([-sin, sin])]
    return [np.concatenate([x, x]).astype(np.float32) for x in rows]


PARTS0 = ((0, 4), (4, 8), (8, 10))


def layer0_steps():
    def fill(name, first=0, last=1):
        return [(name, n) for n in range(first, last)]

    def rows_of(g):
        return [("max", g, u) for u in range(NM)]

    def scores_of(g):
        e = [("exp", g, u) for u in range(10)]
        old = [[("values", g - 1, 2)], [("out_rows", g - 1)], [("turn_rows", g - 1)]] if g else [[], [], []]
        return (e[:1] + old[0] + e[1:2] + old[1] + e[2:4] + old[2] + e[4:9] + [("values", g, 0)] + e[9:]
                + [("values", g, 1)])

    def group(g, others, after, rows=NM):
        s = scores_of(g)
        return (s[:2] + weave(s[2:-3], weave(rows_of(g + 1)[NM - rows:], others)) + s[-3:-2]
                + [("turn_max", g + 1)] + weave(s[-2:], after))

    steps = group(0, fill("logits_s", 0, 4), []) + fill("load_heads", 2, 3)
    steps += group(1, [("load", 0)] + fill("dispatch", 0, 4) + [("norm", 0)] + fill("slots") + fill("logits_c", 0, 1)
                   + [("scale", 0)], fill("logits_c", 1, 2))
    steps += fill("load_heads", 3, 4) + weave(fill("hidden", 0, 4), [("max", 3, u) for u in range(8)] + [("square", 0)])
    steps += group(2, [("xf", 0)] + fill("logits_c", 2, 4) + fill("xnT") + fill("ckv") + fill("q") + fill("xfT"),
                   fill("r") + fill("k"), 3)
    steps += fill("load_heads") + weave(scores_of(3), fill("expert_out") + fill("combine", 0, 4))
    steps += fill("load_heads", 1, 2) + [("values", 3, 2)] + fill("v") + rows_of(0)[:2] + [("out_rows", 3)]
    steps += rows_of(0)[2:6] + [("turn_rows", 3)] + rows_of(0)[6:8] + fill("attnT") + rows_of(0)[8:]
    steps += [("turn_max", 0)] + fill("out") + fill("outT")
    return put_off(steps, {"logits_s": ("soft_s", 2), "logits_c": ("soft_c", 2), "soft_s": ("share_s", 2),
                           "soft_c": ("share_c", 2), "q": ("low_q", 1), "k": ("low_k", 1)},
                   lambda second, step: step[0] == "outT")


def early0(step):
    name, n = step[:2]
    return name in ("load", "norm", "scale", "square", "xf", "xnT", "xfT", "ckv", "q", "r", "k", "v", "low_q",
                    "low_k") or (name in ("max", "turn_max") and n == 0) or (name == "load_heads" and n <= 1)


def layer0_order(steps):
    order = []
    for step in steps:
        name, n = step[:2]
        if name in ("soft_s", "soft_c"):
            order.append(f"logits{name[4:]}{n}")
        elif name in ("low_q", "low_k"):
            order.append(name[4:])
        elif name not in ("logits_s", "logits_c", "q", "k"):
            order += [x for x, _ in layer0_plan([step])]
    return order


def layer0_plan(steps):
    plan = []
    for step in steps:
        name, n = step[:2]
        if name == "max":
            plan.append((f"max{n}_{step[2]}", "dve"))
        elif name in ("xnT", "xfT", "ckv", "v", "slots", "attnT", "out"):
            plan.append((name, "act"))
        elif name in ("q", "r", "k", "expert_out", "outT"):
            plan.append((name, "dve"))
        elif name in ("logits_s", "logits_c", "hidden", "turn_max"):
            plan.append((f"{name}{n}", "act"))
        elif name in ("dispatch", "combine"):
            plan.append((f"{name}{n}", ("act", "dve")[n % 2]))
        elif name == "turn_rows":
            plan.append((f"{name}{n}", "dve"))
    return plan


def layer0(nc, a, x1_dram, batches):
    with ExitStack() as ctx:
        def sb(name, shape, dt=F32):
            return ctx.enter_context(nc.sbuf_tensor(name, shape, dt))

        def sig(name, per, begun=0):
            return Signal(ctx, nc, name, per, begun)

        def plain(name):
            return ctx.enter_context(nc.semaphore(name))

        stack_dram = nc.dram_tensor("stack_scratch", [2, H, 3 * HD0, T], F16, kind="Internal").ap()
        ps_exp = ctx.enter_context(nc.psum_tensor("ps_exp", [P, 3, T], F32))
        ps_out = ctx.enter_context(nc.psum_tensor("ps_out", [P, T], F32))
        ps_any = ctx.enter_context(nc.psum_tensor("ps_any", [P, RING, T], F32))

        ident = sb("ident", [P, P])
        ident_h = sb("ident_h", [P, P], BF16)
        mask = sb("mask", [P, P])
        mask_h = sb("mask_h", [P, P], BF16)
        cos = sb("cos", [2 * DR, T])
        sin = sb("sin", [2 * DR, T])
        w_kvd = sb("w_kvd", [P, D])
        w_q = sb("w_q", [P, D])
        w_k = sb("w_k", [P, D])
        w_v = sb("w_v", [P, D])
        w_o = sb("w_o", [P, D])
        w_qr = sb("w_qr", [P, 2, DR])
        w_kr = sb("w_kr", [P, 2, DR])
        gamma = sb("gamma", [P, D])
        slot_gamma = sb("slot_gamma", [P, D])
        w1 = sb("w1", [P, E0, HID])
        w2 = sb("w2", [P, E0, HB, D])
        b1 = sb("b1", [P, E0, HB])
        b2 = sb("b2", [P, E0 // 2, D])
        slot_nat = sb("slot_nat", [P, 4, D])
        slot_n = sb("slot_n", [P, 4, D])
        slot_ss = sb("slot_ss", [P, 4])
        slot_sm = sb("slot_sm", [P, 4])
        slot_r = sb("slot_r", [P, 4])
        snT = sb("snT", [P, T])
        neg_half = sb("neg_half", [P, 4])

        x_in = sb("x_in", [P, TB, D])
        x_res = sb("x_res", [P, TB, D])
        stats = sb("stats", [P, TB, 6])
        mv = sb("mv", [P, TB, 2])
        var_eps = sb("var_eps", [P, TB])
        rstd = sb("rstd", [P, TB])
        xn = sb("xn", [P, TB, D])
        squares = sb("squares", [P, TB, D])
        ss = sb("ss", [P, TB])
        ss_m = sb("ss_m", [P, TB])
        rnorm = sb("rnorm", [P, TB])
        xf = sb("xf", [P, TB, D])
        xnT = sb("xnT", [P, T])
        xfT = sb("xfT", [P, T])
        ckvT = sb("ckvT", [P, T])
        q_hi = sb("q_hi", [P, T], F16)
        q_lo = sb("q_lo", [P, T], F16)
        k_hi = sb("k_hi", [P, T], F16)
        k_lo = sb("k_lo", [P, T], F16)
        rot_a = sb("rot_a", [2 * DR, T])
        rot_b = sb("rot_b", [2 * DR, T])
        rot = sb("rot", [2 * DR, T])
        rot_hi = sb("rot_hi", [2 * DR, T], F16)
        rot_lo = sb("rot_lo", [2 * DR, T], F16)
        q_st = sb("q_st", [P, 2, G, T], F16)
        k_st = sb("k_st", [P, 2, G, T], F16)
        v_aug = sb("v_aug", [P, TB, H, DR])
        neg_max = sb("neg_max", [P, 2, G, TB])
        max_row = sb("max_row", [G * TB, 2, P], F16)
        probs = sb("probs", [P, 2, len(EXP0), T])
        y_un = sb("y_un", [P, T])
        y_rec = sb("y_rec", [P, TB, G])
        attn = sb("attn", [P, TB, D])
        attnT = sb("attnT", [P, T])
        s_neg = sb("s_neg", [P, 4])
        s_sum = sb("s_sum", [P, 4])
        s_rec = sb("s_rec", [P, 4])
        c_neg = sb("c_neg", [P, 4])
        c_sum = sb("c_sum", [P, 4])
        c_rec = sb("c_rec", [P, 4])
        disp_s = sb("disp_s", [P, 4, T])
        disp_n = sb("disp_n", [P, TB, T])
        comb_n = disp_s
        comb_s = disp_n
        slotsT = sb("slotsT", [P, T])
        hT = sb("hT", [P, 4, HB, 2 * S0])
        eo = sb("eo", [P, 4, D])
        outT = sb("outT", [P, T])
        x1 = sb("x1", [P, TB, D])

        steps = layer0_steps()
        ahead = [x for x in steps if early0(x)]
        rest = [x for x in steps if not early0(x)]
        first = Fills(layer0_plan(ahead), order=layer0_order(ahead))
        steady = Fills(layer0_plan(steps), first, layer0_plan(steps), layer0_order(steps))
        final = Fills(layer0_plan(rest), first, layer0_plan(steps), layer0_order(rest))

        def run(eng, turn, uses_late=False):
            turn(0, 0, first, ahead)
            if uses_late:
                eng.wait_ge(late_loaded, all_late)
            with eng.Fori(0, batches - 1) as i:
                turn(i, i + 1, steady, steps)
            turn(batches - 1, None, final, rest)

        loaded, late_loaded, prep, prep_pool, prep_pe, prep_act = [plain(f"l0_{n}") for n in ("loaded", "late", "prep", "prep_pool",
                                                                                 "prep_pe", "prep_act")]
        sp_passed, pool_passed, dve_passed = [plain(f"l0_{n}_passed") for n in ("sp", "pool", "dve")]
        x_loaded = sig("x_loaded", 16)
        res_loaded = sig("res_loaded", 16)
        scratch_in = sig("scratch_in", 16 * 6)
        stacked = [sig(f"stacked{s}", 16 * 10) for s in range(2)]
        row_in = sig("row_in", 16 * G)
        stored = sig("l0_stored", 16, 16)
        stats_ok = sig("stats_ok", 2 * TB + 1)
        rstd_ok = sig("rstd_ok", 1)
        xn_ok = sig("xn_ok", TB, 1)
        ss_ok = sig("ss_ok", TB + 1)
        rnorm_ok = sig("rnorm_ok", 1)
        xf_ok = sig("xf_ok", TB)
        filled, read = plain("filled"), {n: plain(f"read_{n}") for n in ("act", "dve")}
        hi_ok = sig("hi_ok", 2)
        rot_ok = sig("rot_ok", 4)
        exp_full = sig("exp_full", 10 * G)
        exp_done = sig("exp_done", 10 * G, 1)
        masked = sig("masked", 4 * G)
        pv_done = sig("pv_done", 3 * G, 6)
        pv_read = sig("pv_read", G, 1)
        rec_ok = sig("rec_ok", G)
        neg_ok = sig("neg_ok", 8)
        srec_ok = sig("srec_ok", 8)
        scaled = sig("scaled", 8)

        def emptied(eng, i, fills, name):
            eng.wait_ge(read[fills.reader[name]], fills.emptied(i, name))

        def full(eng, i, fills, name):
            eng.wait_ge(filled, fills.filled(i, name))
            return ps_any[:, fills.bank(name)]

        block = ctx.enter_context(nc.Block())

        rope = [(dst[:, n, c], a[src][:, s]) for dst, src in ((w_qr, "L0_attn_W_q_rope"), (w_kr, "L0_attn_W_k_rope"))
                for n, c, s in ((0, slice(0, DR), slice(0, DR)), (1, slice(0, DR // 2), slice(DR // 2, DR)),
                                (1, slice(DR // 2, DR), slice(0, DR // 2)))]
        loads = [(ident[:], a["ident"]), (mask[:], a["mask"]), (cos[:], a["cos"]), (sin[:], a["sin"]),
                 (slot_nat[:], a["L0_ffn_slot_embeds"].rearrange("e s d -> (e s) d").rearrange("(m p) d -> p m d", p=P)),
                 (slot_gamma[:], a["L0_ffn_slot_norm_gamma"].partition_broadcast(P)),
                 (gamma[:], a["L0_ffn_norm_gamma"].partition_broadcast(P)),
                 (w_kvd[:], a["L0_attn_W_kv_down"]), (w_q[:], a["L0_attn_W_q"]), (w_k[:], a["L0_attn_W_k_up"]),
                 (w_v[:], a["L0_attn_W_v_up"]), (w_o[:], a["L0_attn_W_o"])] + rope
        late_loads = [(b1[:], a["L0_ffn_b1"]),
                 (w1[:], a["L0_ffn_w1"].rearrange("e d h -> d e h")),
                 (w2[:], a["L0_ffn_w2"].rearrange("e (b p) d -> p e b d", p=P))]
        late_loads += [(b2[S0 * (e % 2):S0 * (e % 2) + S0, e // 2, :], a["L0_ffn_b2"][e].partition_broadcast(S0))
                  for e in range(E0)]
        all_loaded, all_late = 16 * len(loads), 16 * len(late_loads)

        @block.sync
        def _(sp):
            for dst, src in loads:
                sp.dma_start(dst, src).then_inc(loaded, 16)
            def turn(i, b, fills, steps):
                for step in steps:
                    name, n = step[:2]
                    if name == "load":
                        sp.wait_ge(xn_ok.sem, xn_ok.at(b, 0))
                        release(sp, sp_passed)
                        sp.dma_start(x_in[:], a["L0_attn_x"][b].rearrange("(t p) d -> p t d", p=P)
                                     ).then_inc(x_loaded.sem, 16)
                    if name in ("q", "k"):
                        side, parts = (0, (q_hi, q_lo, q_hi)) if name == "q" else (1, (k_hi, k_hi, k_lo))
                        emptied(sp, i, fills, name)
                        if side == 0 and fills is not first:
                            for s in range(2):
                                sp.wait_ge(stacked[s].sem, stacked[s].at(i, 16 * 10))
                        for k in range(3):
                            sp.dma_start(stack_dram[side, :, k * HD0:(k + 1) * HD0, :], parts[k][:]
                                         ).then_inc(scratch_in.sem, 16)
                    if name == "load_heads":
                        j = b if early0(step) else i
                        s = n % 2
                        if n >= 2:
                            sp.wait_ge(exp_full.sem, exp_full.at(i, 10 * (n - 1)))
                            release(sp, sp_passed)
                        elif fills is not first:
                            sp.wait_ge(exp_full.sem, exp_full.at(i, 30 + 10 * n))
                            release(sp, sp_passed)
                        if n <= 1:
                            sp.wait_ge(rot_ok.sem, rot_ok.at(b, 4))
                            for k, (qp, kp) in enumerate(((rot_hi, rot_hi), (rot_lo, rot_hi), (rot_hi, rot_lo))):
                                for st, src in ((q_st, qp[0:DR]), (k_st, kp[DR:2 * DR])):
                                    sp.dma_start(st[k * DR:(k + 1) * DR, s], src.unsqueeze(1).to_broadcast([DR, G, T])
                                                 ).then_inc(stacked[s].sem, 16)
                            sp.wait_ge(scratch_in.sem, scratch_in.at(b, 16 * 6))
                        for side, st in ((0, q_st), (1, k_st)):
                            sp.dma_start(st[K_ROPE:K_MAX0, s],
                                         stack_dram[side, G * n:G * n + G].rearrange("h r t -> r h t")
                                         ).then_inc(stacked[s].sem, 16)
                    if name == "turn_max":
                        emptied(sp, i, fills, f"turn_max{n}")
                        sp.dma_start(q_st[K_MAX0:K_ALL0, n % 2], max_row[:, n % 2]).then_inc(row_in.sem, 16)
                    if name == "slots":
                        sp.wait_ge(read["dve"], fills.before(i, "dve"))
                        release(sp, sp_passed)
                        sp.dma_start(x_res[:], a["L0_attn_x"][i].rearrange("(t p) d -> p t d", p=P)
                                     ).then_inc(res_loaded.sem, 16)

            run(sp, turn)

        @block.gpsimd
        def _(pool):
            nc.gpsimd.memset(neg_half[:], -0.5).then_inc(prep_pool, 1)
            pool.wait_ge(prep, 7)
            pool.wait_ge(prep_pool, 1)
            nc.gpsimd.tensor_tensor(slot_r[:], slot_sm[:], neg_half[:], ALU.pow).then_inc(prep_pool, 1)

            def turn(i, b, fills, steps):
                for step in steps:
                    name, n = step[:2]
                    if name == "norm":
                        pool.wait_ge(stats_ok.sem, stats_ok.at(b, 2 * TB + 1))
                        nc.gpsimd.tensor_tensor(rstd[:], var_eps[:], neg_half[:], ALU.pow).then_inc(rstd_ok.sem, 1)
                    if name == "square":
                        pool.wait_ge(ss_ok.sem, ss_ok.at(b, TB + 1))
                        nc.gpsimd.tensor_tensor(rnorm[:], ss_m[:], neg_half[:], ALU.pow).then_inc(rnorm_ok.sem, 1)
                    if name in ("share_s", "share_c"):
                        w, rec, k = (disp_s, s_rec, 0) if name == "share_s" else (comb_n, c_rec, 4)
                        pool.wait_ge(srec_ok.sem, srec_ok.at(i, k + n + 1))
                        release(pool, pool_passed)
                        nc.gpsimd.tensor_scalar(w[:, n], w[:, n], rec[:, n:n + 1], None, ALU.mult
                                                ).then_inc(scaled.sem, 1)
                    if name == "exp" and step[2] in (3, 7, 9):
                        u = probs[:, n % 2]
                        late = u[:, 8:10].rearrange("p u (c q) -> p (u c) q", q=2 * P)
                        squares_of = {3: [u[:, 0:4, 0:P]], 7: [u[:, 4:8, 0:P], u[:, 4:8, 3 * P:T]],
                                      9: [late[:, :, 0:P]]}[step[2]]
                        pool.wait_ge(exp_done.sem, exp_done.at(i, 10 * n + step[2] + 1))
                        release(pool, pool_passed)
                        for x in squares_of:
                            nc.gpsimd.affine_select(out=x, in_=x, compare_op=ALU.is_ge, fill=0.0, base=0,
                                                    pattern=[[0, 4], [1, P]], channel_multiplier=-1
                                                    ).then_inc(masked.sem, 1)

            run(pool, turn)

        @block.scalar
        def _(act):
            for s in (exp_done, pv_read, stored):
                act.sem_inc(s.sem, s.begun)
            for dst, src in late_loads:
                act.dma_start(dst, src).then_inc(late_loaded, 16)
            act.wait_ge(prep_pe, 1)
            nc.scalar.activation(snT[:], ps_any[:, 0], ACT.Copy).then_inc(prep_act, 1)
            act.wait_ge(prep, 13)
            act.wait_ge(loaded, all_loaded)

            def turn(i, b, fills, steps):
                def copy(name, dst):
                    nc.scalar.activation(dst, full(act, i, fills, name), ACT.Copy).then_inc(read["act"], 1)

                for step in steps:
                    name, n = step[:2]
                    if name == "xnT":
                        copy("xnT", xnT[:])
                    if name == "xfT":
                        copy("xfT", xfT[:])
                    if name == "ckv":
                        copy("ckv", ckvT[:])
                    if name in ("q", "k"):
                        nc.scalar.activation((q_hi if name == "q" else k_hi)[:], full(act, i, fills, name), ACT.Copy
                                             ).then_inc(hi_ok.sem, 1)
                    if name == "v":
                        nc.scalar.activation(v_aug[:, :, :, 0:HD0],
                                             full(act, i, fills, "v").rearrange("p (t h d) -> p t h d", t=TB, h=H),
                                             ACT.Copy).then_inc(read["act"], 1)
                    if name in ("soft_s", "soft_c"):
                        neg, w, sums, k = ((s_neg, disp_s, s_sum, 0) if name == "soft_s"
                                           else (c_neg, comb_n, c_sum, 4))
                        filling = f"logits{name[4:]}{n}"
                        act.wait_ge(neg_ok.sem, neg_ok.at(i, k + n + 1))
                        if name == "soft_c" and n == 0:
                            act.wait_ge(filled, fills.filled(i, "dispatch3"))
                        nc.scalar.activation(w[:, n], full(act, i, fills, filling), ACT.Exp, bias=neg[:, n:n + 1],
                                             accum_out=sums[:, n:n + 1]).then_inc(read["act"], 1)
                    if name == "dispatch" and n % 2 == 0:
                        copy(f"dispatch{n}", disp_n[:, n])
                    if name == "combine" and n % 2 == 0:
                        copy(f"combine{n}", comb_s[:, n])
                    if name == "slots":
                        copy("slots", slotsT[:])
                    if name == "turn_max":
                        nc.scalar.activation(max_row[:, n % 2], full(act, i, fills, f"turn_max{n}")[0:G * TB, 0:P],
                                             ACT.Copy, scale=1.0 / SHIFT).then_inc(read["act"], 1)
                    if name == "exp":
                        u = step[2]
                        if u == 0:
                            act.wait_ge(pv_done.sem, pv_done.at(i, 3 * (n - 1)))
                        act.wait_ge(exp_full.sem, exp_full.at(i, 10 * n + u + 1))
                        nc.scalar.activation(probs[:, n % 2, u], ps_exp[:, (10 * n + u) % 3], ACT.Exp,
                                             scale=float(HD0 + DR) ** -0.5).then_inc(exp_done.sem, 1)
                    if name == "out_rows":
                        act.wait_ge(pv_done.sem, pv_done.at(i, 3 * n + 3))
                        act.wait_ge(filled, fills.filled(i, f"turn_rows{n - 1}") if n else fills.before(i, "all"))
                        nc.scalar.activation(y_un[:], ps_out[:], ACT.Copy).then_inc(pv_read.sem, 1)
                    if name == "hidden":
                        bank = full(act, i, fills, f"hidden{n}")
                        for hb in range(HB):
                            for ee in range(2):
                                c = (hb * 2 + ee) * S0
                                ins = nc.scalar.activation(hT[:, n, hb, ee * S0:ee * S0 + S0], bank[:, c:c + S0],
                                                           ACT.Gelu, bias=b1[:, 2 * n + ee, hb:hb + 1])
                        ins.then_inc(read["act"], 1)
                    if name == "attnT":
                        copy("attnT", attnT[:])
                    if name == "out":
                        copy("out", outT[:])
                    if name == "outT":
                        emptied(act, i, fills, "outT")
                        act.dma_start(x1_dram[i].rearrange("(t p) d -> p t d", p=P), x1[:]).then_inc(stored.sem, 16)

            run(act, turn, uses_late=True)
            act.wait_ge(stored.sem, 16 * batches + 16)

        @block.vector
        def _(dve):
            for s in (xn_ok,):
                dve.sem_inc(s.sem, s.begun)
            nc.vector.memset(v_aug[:], 0.0).then_inc(prep, 1)
            nc.vector.memset(k_st[K_ROPE:P], SHIFT).then_inc(prep, 1)
            dve.wait_ge(loaded, all_loaded)
            for b in range(4):
                nc.vector.tensor_tensor_reduce(squares[:, b], slot_nat[:, b], slot_nat[:, b], 1.0 / D, 0.0, ALU.mult,
                                               ALU.add, slot_ss[:, b:b + 1]).then_inc(prep, 1)
            dve.wait_ge(prep, 6)
            nc.vector.tensor_scalar(slot_sm[:], slot_ss[:], 1e-24 / D, None, ALU.max).then_inc(prep, 1)
            dve.wait_ge(prep_pool, 2)
            for b in range(4):
                nc.vector.scalar_tensor_tensor(out=slot_n[:, b], in0=slot_nat[:, b], scalar=slot_r[:, b:b + 1],
                                               in1=slot_gamma[:], op0=ALU.mult, op1=ALU.mult).then_inc(prep, 1)
            nc.vector.tensor_copy(ident_h[:], ident[:]).then_inc(prep, 1)
            dve.wait_ge(prep, 12)
            nc.vector.memset(v_aug[:, :, :, HD0:HD0 + 1], 1.0).then_inc(prep, 1)
            nc.vector.tensor_copy(mask_h[:], mask[:]).then_inc(prep, 1)

            def turn(i, b, fills, steps):
                for step in steps:
                    name, n = step[:2]
                    j = b if early0(step) else i
                    if name == "norm":
                        dve.wait_ge(x_loaded.sem, x_loaded.at(b, 16))
                        for t in range(TB):
                            nc.vector.bn_stats(stats[:, t], x_in[:, t]).then_inc(stats_ok.sem, 1)
                        dve.wait_ge(stats_ok.sem, stats_ok.at(b, TB))
                        release(dve, dve_passed)
                        for t in range(TB):
                            nc.vector.bn_aggr(mv[:, t], stats[:, t]).then_inc(stats_ok.sem, 1)
                        dve.wait_ge(stats_ok.sem, stats_ok.at(b, 2 * TB))
                        nc.vector.tensor_scalar(var_eps[:], mv[:, :, 1], EPS, None, ALU.add).then_inc(stats_ok.sem, 1)
                    if name == "scale":
                        dve.wait_ge(rstd_ok.sem, rstd_ok.at(b, 1))
                        for t in range(TB):
                            nc.vector.tensor_scalar(xn[:, t], x_in[:, t], mv[:, t, 0:1], rstd[:, t:t + 1], ALU.subtract,
                                                    ALU.mult).then_inc(xn_ok.sem, 1)
                    if name == "square":
                        for t in range(TB):
                            dve.wait_ge(xn_ok.sem, xn_ok.at(b, t + 1))
                            nc.vector.tensor_tensor_reduce(squares[:, t], xn[:, t], xn[:, t], 1.0 / D, 0.0, ALU.mult,
                                                           ALU.add, ss[:, t:t + 1]).then_inc(ss_ok.sem, 1)
                        dve.wait_ge(ss_ok.sem, ss_ok.at(b, TB))
                        nc.vector.tensor_scalar(ss_m[:], ss[:], 1e-24 / D, None, ALU.max).then_inc(ss_ok.sem, 1)
                    if name == "xf":
                        dve.wait_ge(rnorm_ok.sem, rnorm_ok.at(b, 1))
                        if fills is not first:
                            dve.wait_ge(filled, fills.filled(i, "slots"))
                        for t in range(TB):
                            nc.vector.scalar_tensor_tensor(out=xf[:, t], in0=xn[:, t], scalar=rnorm[:, t:t + 1],
                                                           in1=gamma[:], op0=ALU.mult, op1=ALU.mult
                                                           ).then_inc(xf_ok.sem, 1)
                    if name in ("low_q", "low_k"):
                        hi, lo = (q_hi, q_lo) if name == "low_q" else (k_hi, k_lo)
                        dve.wait_ge(hi_ok.sem, hi_ok.at(b, 1 if name == "low_q" else 2))
                        nc.vector.tensor_tensor(lo[:], full(dve, i, fills, name[4:]), hi[:], ALU.subtract
                                                ).then_inc(read["dve"], 1)
                    if name == "r":
                        bank = full(dve, i, fills, "r")
                        nc.vector.tensor_tensor(rot_a[:], bank[0:2 * DR], cos[:], ALU.mult).then_inc(rot_ok.sem, 1)
                        nc.vector.tensor_tensor(rot_b[:], bank[2 * DR:P], sin[:], ALU.mult).then_inc(read["dve"], 1)
                        dve.wait_ge(rot_ok.sem, rot_ok.at(b, 1))
                        emptied(dve, i, fills, "r")
                        nc.vector.tensor_tensor(rot[:], rot_a[:], rot_b[:], ALU.add).then_inc(rot_ok.sem, 1)
                        dve.wait_ge(rot_ok.sem, rot_ok.at(b, 2))
                        nc.vector.tensor_copy(rot_hi[:], rot[:]).then_inc(rot_ok.sem, 1)
                        dve.wait_ge(rot_ok.sem, rot_ok.at(b, 3))
                        nc.vector.tensor_tensor(rot_lo[:], rot[:], rot_hi[:], ALU.subtract).then_inc(rot_ok.sem, 1)
                    if name == "max":
                        u = step[2]
                        if u == 0:
                            if n in (1, 2):
                                dve.wait_ge(filled, fills.before(i, "all"))
                            elif n == 3:
                                dve.wait_ge(filled, fills.filled(i, "turn_max1"))
                            elif fills is not first:
                                dve.wait_ge(filled, fills.filled(i, "turn_max2"))
                        t, heads = MAX_UNITS[u]
                        k = len(heads)
                        src = full(dve, i, fills, f"max{n}_{u}")[:, 0:k * (t + 1) * P].rearrange("p (h k) -> p h k", h=k)
                        nc.vector.tensor_reduce(neg_max[:, n % 2, heads[0]:heads[0] + k, t], src, AX.X, ALU.max,
                                                negate=True).then_inc(read["dve"], 1)
                    if name in ("logits_s", "logits_c"):
                        neg = s_neg if name == "logits_s" else c_neg
                        nc.vector.tensor_reduce(neg[:, n:n + 1], full(dve, i, fills, f"{name}{n}"), AX.X, ALU.max,
                                                negate=True).then_inc(neg_ok.sem, 1)
                    if name in ("share_s", "share_c"):
                        sums, rec = (s_sum, s_rec) if name == "share_s" else (c_sum, c_rec)
                        emptied(dve, i, fills, f"logits{name[5:]}{n}")
                        nc.vector.reciprocal(rec[:, n:n + 1], sums[:, n:n + 1]).then_inc(srec_ok.sem, 1)
                    if name == "dispatch" and n % 2:
                        nc.vector.tensor_copy(disp_n[:, n], full(dve, i, fills, f"dispatch{n}")
                                              ).then_inc(read["dve"], 1)
                    if name == "combine" and n % 2:
                        nc.vector.tensor_copy(comb_s[:, n], full(dve, i, fills, f"combine{n}")
                                              ).then_inc(read["dve"], 1)
                    if name == "turn_rows":
                        bank = full(dve, i, fills, f"turn_rows{n}").rearrange("p (t s c) -> p t s c", t=TB, s=G)
                        dve.wait_ge(read["dve"], fills.emptied(i, f"turn_rows{n - 1}") if n else
                                    fills.before(i, "dve"))
                        nc.vector.reciprocal(y_rec[:], bank[:, :, :, HD0]).then_inc(rec_ok.sem, 1)
                        dve.wait_ge(rec_ok.sem, rec_ok.at(i, n + 1))
                        nc.vector.tensor_tensor(attn[:, :, n * 32:n * 32 + 32].rearrange("p t (s d) -> p t s d", s=G),
                                                bank[:, :, :, 0:HD0], y_rec[:].unsqueeze(3).to_broadcast([P, TB, G, HD0]),
                                                ALU.mult).then_inc(read["dve"], 1)
                    if name == "expert_out":
                        nc.vector.tensor_tensor(eo[:].rearrange("p m d -> p (m d)"), full(dve, i, fills, "expert_out"),
                                                b2[:].rearrange("p m d -> p (m d)"), ALU.add).then_inc(read["dve"], 1)
                    if name == "outT":
                        dve.wait_ge(res_loaded.sem, res_loaded.at(i, 16))
                        dve.wait_ge(stored.sem, stored.at(i, 0))
                        nc.vector.tensor_tensor(x1[:].rearrange("p t d -> p (t d)"), full(dve, i, fills, "outT"),
                                                x_res[:].rearrange("p t d -> p (t d)"), ALU.add
                                                ).then_inc(read["dve"], 1)

            run(dve, turn, uses_late=True)

        @block.tensor
        def _(pe):
            pe.sem_inc(pv_done.sem, pv_done.begun)
            pe.wait_ge(loaded, all_loaded)
            pe.wait_ge(prep, 14)
            for c in range(4):
                ins = pe.transpose(ps_any[:, 0, c * P:c * P + P], slot_n[:, c], ident[:])
            ins.then_inc(prep_pe, 1)
            pe.wait_ge(prep_act, 1)

            def turn(i, b, fills, steps):
                def bank(name):
                    k = fills.names.index(name)
                    if k >= RING:
                        emptied(pe, i, fills, fills.names[k - RING])
                    elif fills is not first:
                        for who, sem in read.items():
                            pe.wait_ge(sem, fills.before(i, who, RING - 1 - k))
                    return ps_any[:, fills.bank(name)]

                def turned(name, blocks):
                    out = bank(name)
                    for c, src in enumerate(blocks):
                        ins = pe.transpose(out[:, c * P:c * P + P], src, ident[:])
                    ins.then_inc(filled, 1)

                def product(name, w, x):
                    pe.matmul(bank(name), w, x, start=True, stop=True).then_inc(filled, 1)

                for step in steps:
                    name, n = step[:2]
                    j = b if early0(step) else i
                    if name == "xnT":
                        pe.wait_ge(xn_ok.sem, xn_ok.at(b, TB))
                        turned("xnT", [xn[:, t] for t in range(TB)])
                    if name == "xfT":
                        pe.wait_ge(xf_ok.sem, xf_ok.at(b, TB))
                        turned("xfT", [xf[:, t] for t in range(TB)])
                    if name == "ckv":
                        emptied(pe, i, fills, "xnT")
                        product("ckv", w_kvd[:], xnT[:])
                    if name == "q":
                        product("q", w_q[:], xnT[:])
                    if name == "r":
                        emptied(pe, i, fills, "ckv")
                        out = bank("r")
                        for k in range(2):
                            pe.matmul(out[2 * k * DR:(2 * k + 1) * DR], w_qr[:, k], xnT[:], start=True, stop=True)
                            ins = pe.matmul(out[(2 * k + 1) * DR:(2 * k + 2) * DR], w_kr[:, k], ckvT[:],
                                            start=True, stop=True)
                        ins.then_inc(filled, 1)
                    if name == "k":
                        product("k", w_k[:], ckvT[:])
                    if name == "v":
                        out = bank("v")
                        for t in range(TB):
                            ins = pe.matmul(out[:, t * P:t * P + P], ckvT[:, t * P:t * P + P], w_v[:],
                                            start=True, stop=True)
                        ins.then_inc(filled, 1)
                    if name == "max":
                        t, heads = MAX_UNITS[step[2]]
                        w = (t + 1) * P
                        if step[2] == 0:
                            pe.wait_ge(stacked[n % 2].sem, stacked[n % 2].at(j, 16 * (8 + 2 * (n // 2))))
                        scores = bank(f"max{n}_{step[2]}")
                        for c, h in enumerate(heads):
                            out = scores[:, c * w:c * w + w]
                            pe.matmul(out, q_st[0:K_MAX0, n % 2, h, t * P:t * P + P], k_st[0:K_MAX0, n % 2, h, 0:w],
                                      start=True, stop=False)
                            ins = pe.matmul(out[:, t * P:w], ident_h[:], mask_h[:], start=False, stop=True)
                        ins.then_inc(filled, 1)
                    if name == "turn_max":
                        emptied(pe, i, fills, f"max{n}_{NM - 1}")
                        pe.transpose(bank(f"turn_max{n}")[0:G * TB, 0:P],
                                     neg_max[:, n % 2].rearrange("p h t -> p (h t)"), ident[:]).then_inc(filled, 1)
                    if name == "exp":
                        m = 10 * n + step[2]
                        if step[2] == 0:
                            pe.wait_ge(row_in.sem, row_in.at(i, 16 * (n + 1)))
                        pe.wait_ge(exp_done.sem, exp_done.at(i, max(m + 1 - 3, 0)))
                        for h, k, c in EXP0[step[2]]:
                            ins = pe.matmul(ps_exp[:, m % 3, c:c + T - k * P],
                                            k_st[0:K_ALL0, n % 2, h, k * P:k * P + P],
                                            q_st[0:K_ALL0, n % 2, h, k * P:T], start=True, stop=True)
                        ins.then_inc(exp_full.sem, 1)
                    if name == "values":
                        part = step[2]
                        pe.wait_ge(masked.sem, masked.at(i, 4 * n + (1, 3, 4)[part]))
                        if part == 0:
                            pe.wait_ge(pv_read.sem, pv_read.at(i, n))
                            if n == 0:
                                pe.wait_ge(read["act"], fills.before(i, "act"))
                        pieces = [(k, h, u, c) for u in range(*PARTS0[part]) for h, k, c in EXP0[u]]
                        for k, h, u, c in sorted(pieces):
                            ins = pe.matmul(ps_out[32 * h:32 * h + 32, k * P:T], v_aug[:, k, G * n + h],
                                            probs[:, n % 2, u, c:c + T - k * P], start=(part == 0), stop=(part == 2))
                        ins.then_inc(pv_done.sem, 1)
                    if name == "turn_rows":
                        pe.wait_ge(pv_read.sem, pv_read.at(i, n + 1))
                        turned(f"turn_rows{n}", [y_un[:, t * P:t * P + P] for t in range(TB)])
                    if name == "logits_s":
                        if n == 0:
                            pe.wait_ge(read["act"], fills.before(i, "act"))
                        product(f"logits_s{n}", snT[:, n * P:n * P + P], xfT[:])
                    if name == "logits_c":
                        product(f"logits_c{n}", xfT[:, n * P:n * P + P], snT[:])
                    if name == "dispatch":
                        if n == 0:
                            pe.wait_ge(scaled.sem, scaled.at(i, 4))
                        turned(f"dispatch{n}", [disp_s[:, c, n * P:n * P + P] for c in range(4)])
                    if name == "slots":
                        out = bank("slots")
                        for t in range(TB):
                            emptied(pe, i, fills, f"dispatch{t}")
                            ins = pe.matmul(out, xf[:, t], disp_n[:, t], start=(t == 0), stop=(t == TB - 1))
                        ins.then_inc(filled, 1)
                    if name == "hidden":
                        if n == 0:
                            emptied(pe, i, fills, "slots")
                        out = bank(f"hidden{n}")
                        for hb in range(HB):
                            for ee in range(2):
                                c, e = (hb * 2 + ee) * S0, 2 * n + ee
                                ins = pe.matmul(out[:, c:c + S0], w1[:, e, hb * P:hb * P + P],
                                                slotsT[:, e * S0:e * S0 + S0], start=True, stop=True)
                        ins.then_inc(filled, 1)
                    if name == "expert_out":
                        out = bank("expert_out")
                        for m in range(4):
                            emptied(pe, i, fills, f"hidden{m}")
                            for hb in range(HB):
                                for ee in range(2):
                                    ins = pe.matmul(out[S0 * ee:S0 * ee + S0, m * D:m * D + D],
                                                    hT[:, m, hb, ee * S0:ee * S0 + S0], w2[:, 2 * m + ee, hb],
                                                    start=(hb == 0), stop=(hb == HB - 1))
                        ins.then_inc(filled, 1)
                    if name == "combine":
                        if n == 0:
                            pe.wait_ge(scaled.sem, scaled.at(i, 8))
                        turned(f"combine{n}", [comb_n[:, t, n * P:n * P + P] for t in range(TB)])
                    if name == "attnT":
                        emptied(pe, i, fills, f"turn_rows{G - 1}")
                        turned("attnT", [attn[:, t] for t in range(TB)])
                    if name == "out":
                        out = bank("out")
                        emptied(pe, i, fills, "expert_out")
                        for c in range(4):
                            emptied(pe, i, fills, f"combine{c}")
                            pe.matmul(out, eo[:, c], comb_s[:, c], start=(c == 0), stop=False)
                        emptied(pe, i, fills, "attnT")
                        pe.matmul(out, w_o[:], attnT[:], start=False, stop=True).then_inc(filled, 1)
                    if name == "outT":
                        emptied(pe, i, fills, "out")
                        turned("outT", [outT[:, t * P:t * P + P] for t in range(TB)])

            run(pe, turn, uses_late=True)


EXP1 = [[(0, 0, 0)], [(1, 0, 0)], [(0, 1, 0), (0, 3, 384)], [(1, 1, 0), (1, 3, 384)], [(0, 2, 0), (1, 2, 256)]]
X_SCALE, W_SCALE, LAT_SCALE = 64.0, 64.0, 16.0
XW, LW = X_SCALE * W_SCALE, LAT_SCALE * W_SCALE
K_B = HD1 + 1
PAIRS = H // 2
CHUNK = 4


def scores_of(p):
    exps = [("exp", p, u) for u in range(5)]
    if not p:
        return exps
    spread, scaled = ([("spread", p - 2)], [("scaled", p - 2)]) if p >= 2 else ([], [])
    return (exps[:2] + [("values", p - 1)] + exps[2:3] + spread + [("sums", p - 1)] + exps[3:4] + scaled
            + [("rec", p - 1, 0)] + exps[4:] + [("rec", p - 1, 1)])


def layer1_steps():
    def experts(first, last):
        return [(x, e) for e in range(first, last) for x in ("gate_in", "up_in")]

    def rows_of(g):
        return [("max", g, u) for u in range(NM)]

    def heads_in(g):
        return [("qk", g, k) for k in range(4)]

    def group(g, others, between, after):
        a, b = scores_of(2 * g), scores_of(2 * g + 1)
        return (weave(a, others) + weave(b[:6], weave(rows_of(g + 1), between)) + b[6:7] + after[:1]
                + [("turn_max", g + 1)] + weave(b[7:], after[1:]))

    values_in = [("v", t, half) for t in range(TB) for half in range(2)]
    steps = group(0, experts(0, 3), experts(3, 4), heads_in(2) + experts(4, 5))
    steps += group(1, [("down", 0)] + experts(5, 8), experts(8, 9), heads_in(3) + experts(9, 10))
    steps += group(2, [("load", 0)] + experts(10, 11) + [("norm", 0)] + experts(11, 12) + [("scale", 0), ("down", 1)]
                   + experts(12, 13), experts(13, 15), experts(15, 17))
    steps += weave(scores_of(6), [("xnT", 0), ("lat", 0), ("down", 2), ("gate", 0)] + heads_in(0) + [("route", 0)])
    steps += weave(scores_of(7), [("down", 3), ("cT", 0)])
    steps += [("values", 7), ("spread", 6), ("scaled", 6)] + values_in[:2] + [("sums", 7)]
    steps += weave(weave(values_in[2:], [("rec", 7, 0), ("rec", 7, 1)]), rows_of(0)) 
    steps += heads_in(1)[:1] + [("spread", 7), ("turn_max", 0), ("scaled", 7)] + heads_in(1)[1:2]
    steps += [("out", 0)] + heads_in(1)[2:] + [("outT", 0)]
    return steps


def early1(step):
    name, n = step[:2]
    return name in ("load", "norm", "scale", "xnT", "lat", "gate", "route", "cT", "v") or (
        name in ("max", "turn_max") and n == 0) or (name == "qk" and n <= 1)


def head_bank(step):
    _, n, k = step
    return f"{'qk'[k // 2]}{2 * n + k % 2}"


def layer1_plan(steps):
    plan = []
    for step in steps:
        name, n = step[:2]
        if name == "max":
            plan.append((f"max{n}_{step[2]}", "dve"))
        elif name == "qk":
            plan.append((head_bank(step), "dve"))
        elif name == "v":
            plan.append((f"v{n}{step[2]}", "act"))
        elif name in ("xnT", "lat"):
            plan.append((name, "dve"))
        elif name in ("gate", "cT"):
            plan.append((name, "act"))
        elif name in ("out", "outT"):
            plan.append((name, "dve"))
        elif name in ("turn_max", "sums", "spread"):
            plan.append((f"{name}{n}", "act"))
        elif name in ("gate_in", "up_in", "down"):
            plan.append((f"{name[0]}{n}", "dve"))
    return plan


def experts_of(chunk):
    return range(CHUNK * chunk, min(CHUNK * chunk + CHUNK, E1 + 1))


def layer1(nc, a, x1_dram, out_dram, batches):
    with ExitStack() as ctx:
        def sb(name, shape, dt=F32):
            return ctx.enter_context(nc.sbuf_tensor("l1_" + name, shape, dt))

        def sig(name, per, begun=0):
            return Signal(ctx, nc, "l1_" + name, per, begun)

        def plain(name):
            return ctx.enter_context(nc.semaphore("l1_" + name))

        route_dram = nc.dram_tensor("route_scratch", [E1, T], F32, kind="Internal").ap()
        ps_exp = ctx.enter_context(nc.psum_tensor("l1_ps_exp", [P, ST_BANKS, T], F32))
        ps_out = ctx.enter_context(nc.psum_tensor("l1_ps_out", [P, 2, T], F32))
        ps_any = ctx.enter_context(nc.psum_tensor("l1_ps_any", [P, RING, T], F32))

        ident = sb("ident", [P, P])
        ident_h = sb("ident_h", [P, P], BF16)
        masks_h = sb("masks_h", [P, 2, P], BF16)
        w_kvd = sb("w_kvd", [P, D])
        w_kvu = sb("w_kvu", [P, 2, 2, H * HD1], F16)
        w_q = sb("w_q", [P, 2, H * HD1], F16)
        w_out = sb("w_out", [P, PAIRS, D])
        gate_w = sb("gate_w", [P, E1])
        bias = sb("bias", [P, E1])
        w_g = sb("w_g", [P, 2, E1 + 1, D], F16)
        w_u = sb("w_u", [P, 2, E1 + 1, D], F16)
        w_d = sb("w_d", [P, E1 + 1, D])
        ones = sb("ones", [P, 32])
        row_of = sb("row_of", [P, 4, HD1])
        neg_half = sb("neg_half", [P, TB])

        x_in = sb("x_in", [P, TB, D])
        x_res = sb("x_res", [P, TB, D])
        stats = sb("stats", [P, TB, 6])
        mv = sb("mv", [P, TB, 2])
        var_eps = sb("var_eps", [P, TB])
        rstd = sb("rstd", [P, TB])
        xnT = sb("xnT", [P, T])
        xn_p = sb("xn_p", [P, 2, T], F16)
        lat_p = sb("lat_p", [P, 2, T], F16)
        q_hi = sb("q_hi", [P, 2, T], F16)
        q_lo = sb("q_lo", [P, 2, T], F16)
        k_hi = sb("k_hi", [P, 2, T], F16)
        k_lo = sb("k_lo", [P, 2, T], F16)
        q_a = sb("q_a", [P, 2, G, T], F16)
        k_a = sb("k_a", [P, 2, G, T], F16)
        q_b = sb("q_b", [P, 2, G, T], F16)
        k_b = sb("k_b", [P, 2, G, T], F16)
        v = sb("v", [P, TB, H * HD1])
        neg_max = sb("neg_max", [P, 2, G, TB])
        max_row = sb("max_row", [G * TB, 2, P], F16)
        probs = sb("probs", [P, 2, 5, T])
        key_sum = sb("key_sum", [P, G, T])
        yT = sb("yT", [P, PAIRS, T])
        den = sb("den", [P, T // 2])
        rec = sb("rec", [P, T // 2])
        factor = sb("factor", [P, T])
        spread = sb("spread", [P, 2, CHUNK, T])
        th = sb("th", [P, TB, E1])
        score = sb("score", [P, TB, E1])
        select = sb("select", [P, TB, E1])
        top = sb("top", [P, TB, TOP])
        others = sb("others", [P, TB, E1])
        keep = sb("keep", [P, TB, E1])
        kept = sb("kept", [P, TB, E1])
        kept_sum = sb("kept_sum", [P, TB])
        kept_rec = sb("kept_rec", [P, TB])
        weight = sb("weight", [P, TB, E1])
        weightT = sb("weightT", [E1, T])
        tanh = sb("tanh", [P, 2, T])
        gated = sb("gated", [P, T])
        hidden = sb("hidden", [P, 2, T])
        hw = sb("hw", [P, 2, CHUNK, T])
        acc = sb("acc", [P, T])
        outT = gated

        flat = probs[:].rearrange("p s u t -> p (s u t)")
        w_q_in, w_kvu_in = flat[:, 0:H * HD1], flat[:, H * HD1:3 * H * HD1]
        masks = flat[:, 3 * H * HD1:3 * H * HD1 + 2 * P].rearrange("p (s k) -> p s k", s=2)
        w_g_in, w_u_in = [x[:, 0:(E1 + 1) * D].rearrange("p (e d) -> p e d", d=D)
                          for x in (yT[:].rearrange("p n t -> p (n t)"), hw[:].rearrange("p s c t -> p (s c t)"))]

        steps = layer1_steps()
        ahead = [x for x in steps if early1(x)]
        rest = [x for x in steps if not early1(x)]
        first = Fills(layer1_plan(ahead))
        steady = Fills(layer1_plan(steps), first, layer1_plan(steps))
        final = Fills(layer1_plan(rest), first, layer1_plan(steps))

        def run(eng, turn, between=None):
            turn(0, 0, first, ahead)
            if between:
                between(eng)
            with eng.Fori(0, batches - 1) as i:
                turn(i, i + 1, steady, steps)
            turn(batches - 1, None, final, rest)

        loaded, late_loaded, weights_hi, weights_lo, prep, prep_pool = [
            plain(n) for n in ("loaded", "late_loaded", "weights_hi", "weights_lo", "prep", "prep_pool")]
        sp_passed, pool_passed, dve_passed = [plain(f"{n}_passed") for n in ("sp", "pool", "dve")]
        x_loaded = sig("x_loaded", 16)
        res_loaded = sig("res_loaded", 16)
        stacked = sig("stacked", 16 * 12 * G)
        row_in = sig("row_in", 16 * G)
        route_out = sig("route_out", 16)
        spread_in = [sig(f"spread_in{n}", 16 * E1 // CHUNK // 2) for n in range(2)]
        stored = sig("stored", 16, 16)
        stats_ok = sig("stats_ok", 2 * TB + 1)
        rstd_ok = sig("rstd_ok", 1)
        xn_ok = sig("xn_ok", TB, 1)
        filled, read = plain("filled"), {n: plain(f"read_{n}") for n in ("act", "dve")}
        x_hi_ok = sig("x_hi_ok", 3)
        hi_ok = sig("hi_ok", 4 * G)
        exp_full = sig("exp_full", 5 * PAIRS, 1)
        exp_done = sig("exp_done", 5 * PAIRS, 1)
        added = sig("added", 4 * PAIRS, 8)
        pv_done = sig("pv_done", PAIRS, 2)
        rec_ok = sig("rec_ok", 2 * PAIRS, 1)
        normed = sig("normed", PAIRS, 2)
        route_ok = sig("route_ok", 15)
        tanh_ok = sig("tanh_ok", E1 + 1)
        hw_ok = sig("hw_ok", E1 + 1, 1)

        def emptied(eng, i, fills, name):
            eng.wait_ge(read[fills.reader[name]], fills.emptied(i, name))

        def full(eng, i, fills, name):
            eng.wait_ge(filled, fills.filled(i, name))
            return ps_any[:, fills.bank(name)]

        block = ctx.enter_context(nc.Block())

        loads = [(ident[:], a["ident"]), (masks[:, 0], a["mask"]), (masks[:, 1], a["maskT"]),
                 (w_kvd[:], a["L1_attn_w_kv_down"]), (gate_w[:], a["L1_ffn_gate_w"]),
                 (bias[:], a["L1_ffn_expert_bias"].partition_broadcast(P)), (w_q_in, a["L1_attn_w_q"]),
                 (w_kvu_in, a["L1_attn_w_kv_up"])]
        late_loads = [(w_out[:], a["L1_attn_w_out"].rearrange("(k p) d -> p k d", p=P))]
        for w, name in ((w_g_in, "gate"), (w_u_in, "up"), (w_d, "down")):
            late_loads += [(w[:, 0:E1], a[f"L1_ffn_w_{name}"]), (w[:, E1], a[f"L1_ffn_shared_{name}_w"])]
        all_late = 16 * len(late_loads)
        all_loaded = 16 * len(loads)

        @block.sync
        def _(sp):
            for dst, src in loads:
                sp.dma_start(dst, src).then_inc(loaded, 16)
            def turn(i, b, fills, steps):
                for step in steps:
                    name, n = step[:2]
                    if name == "load":
                        if fills is not first:
                            sp.wait_ge(filled, fills.before(i, "all"))
                            release(sp, sp_passed)
                        sp.dma_start(x_in[:], x1_dram[b].rearrange("(t p) d -> p t d", p=P)).then_inc(x_loaded.sem, 16)
                    if name == "qk" and step[2] % 2:
                        j = b if early1(step) else i
                        side = step[2] // 2
                        emptied(sp, i, fills, head_bank(step))
                        s = n % 2
                        if side == 0:
                            release(sp, sp_passed)
                            if n >= 2:
                                sp.wait_ge(exp_full.sem, exp_full.at(i, 10 * (n - 1)))
                            elif fills is not first:
                                sp.wait_ge(exp_full.sem, exp_full.at(i, 30 + 10 * n))
                        for r in range(2):
                            rows = slice(HD1 * r, HD1 * r + HD1)
                            for dst, to, src in (((q_a, 0, q_hi), (q_a, HD1, q_hi), (q_b, 0, q_lo)),
                                                 ((k_a, 0, k_hi), (k_a, HD1, k_lo), (k_b, 0, k_hi)))[side]:
                                sp.dma_start(dst[to:to + HD1, s].rearrange("p (q r) t -> p q r t", r=2)[:, :, r],
                                             src[rows]).then_inc(stacked.sem, 16)
                    if name == "turn_max":
                        emptied(sp, i, fills, f"turn_max{n}")
                        sp.dma_start(q_b[HD1:K_B, n % 2], max_row[:, n % 2]).then_inc(row_in.sem, 16)
                    if name == "cT":
                        emptied(sp, i, fills, "cT")
                        release(sp, sp_passed)
                        sp.wait_ge(hw_ok.sem, hw_ok.at(b, 0))
                        sp.dma_start(route_dram, weightT[:]).then_inc(route_out.sem, 16)
                        sp.wait_ge(route_out.sem, route_out.at(b, 16))
                    if name == "cT" or (name == "up_in" and n in (CHUNK, 2 * CHUNK)):
                        if name == "up_in":
                            sp.wait_ge(hw_ok.sem, hw_ok.at(i, n))
                        for c in ((0, 1) if name == "cT" else (n // CHUNK + 1,)):
                            sp.dma_start(spread[:, c % 2],
                                         route_dram[CHUNK * c:CHUNK * c + CHUNK].partition_broadcast(P)
                                         ).then_inc(spread_in[c % 2].sem, 16)
                    if step == ("up_in", E1):
                        sp.wait_ge(stored.sem, stored.at(i, 0))
                        release(sp, sp_passed)
                        sp.dma_start(x_res[:], x1_dram[i].rearrange("(t p) d -> p t d", p=P)
                                     ).then_inc(res_loaded.sem, 16)

            run(sp, turn)

        @block.gpsimd
        def _(pool):
            for s in (added, hw_ok):
                pool.sem_inc(s.sem, s.begun)
            nc.gpsimd.memset(neg_half[:], -0.5).then_inc(prep_pool, 1)
            pool.wait_ge(prep_pool, 1)
            pool.wait_ge(loaded, all_loaded)

            def turn(i, b, fills, steps):
                for step in steps:
                    name, n = step[:2]
                    if name == "norm":
                        pool.wait_ge(stats_ok.sem, stats_ok.at(b, 2 * TB + 1))
                        nc.gpsimd.tensor_tensor(rstd[:], var_eps[:], neg_half[:], ALU.pow).then_inc(rstd_ok.sem, 1)
                    if name == "exp":
                        s = key_sum[:, 2 * (n % 2):2 * (n % 2) + 2]
                        u = probs[:, n % 2]
                        if step[2] == 3:
                            if n >= 2:
                                pool.wait_ge(filled, fills.filled(i, f"sums{n - 2}"))
                            else:
                                pool.wait_ge(filled, fills.before(i, "all"))
                            pool.wait_ge(exp_done.sem, exp_done.at(i, 5 * n + 4))
                            release(pool, pool_passed)
                            nc.gpsimd.tensor_copy(s[:, :, 0:P], u[:, 0:2, 0:P]).then_inc(added.sem, 1)
                            nc.gpsimd.tensor_tensor(s[:, :, P:T], u[:, 0:2, P:T], u[:, 2:4, 0:3 * P], ALU.add
                                                    ).then_inc(added.sem, 1)
                        if step[2] == 4:
                            pool.wait_ge(exp_done.sem, exp_done.at(i, 5 * n + 5))
                            pool.wait_ge(added.sem, added.at(i, 4 * n + 2))
                            nc.gpsimd.tensor_tensor(s[:, :, 2 * P:T], s[:, :, 2 * P:T],
                                                    u[:, 4].rearrange("p (h q) -> p h q", h=2), ALU.add
                                                    ).then_inc(added.sem, 1)
                            pool.wait_ge(added.sem, added.at(i, 4 * n + 3))
                            nc.gpsimd.tensor_tensor(s[:, :, 3 * P:T], s[:, :, 3 * P:T], u[:, 2:4, 3 * P:T], ALU.add
                                                    ).then_inc(added.sem, 1)
                    if name == "up_in":
                        c = n // CHUNK
                        if n % CHUNK == 0:
                            if c >= 2:
                                pool.wait_ge(filled, fills.filled(i, f"d{c - 2}"))
                            else:
                                pool.wait_ge(filled, fills.before(i, "all"))
                        emptied(pool, i, fills, f"u{n}")
                        dst = hw[:, c % 2, n % CHUNK]
                        if n < E1:
                            pool.wait_ge(spread_in[c % 2].sem, spread_in[c % 2].at(i, 16 * (c // 2 + 1)))
                            nc.gpsimd.tensor_tensor(dst, hidden[:, n % 2], spread[:, c % 2, n % CHUNK], ALU.mult
                                                    ).then_inc(hw_ok.sem, 1)
                        else:
                            release(pool, pool_passed)
                            nc.gpsimd.tensor_scalar(dst, hidden[:, n % 2], 0.5 / XW ** 2, None, ALU.mult
                                                    ).then_inc(hw_ok.sem, 1)

            run(pool, turn)

        @block.scalar
        def _(act):
            for s in (exp_done, stored):
                act.sem_inc(s.sem, s.begun)
            for dst, src in late_loads:
                act.dma_start(dst, src).then_inc(late_loaded, 16)
            act.wait_ge(loaded, all_loaded)
            nc.scalar.activation(w_q[:, 0], w_q_in, ACT.Copy, scale=W_SCALE).then_inc(weights_hi, 1)
            nc.scalar.activation(w_kvu[:, 0].rearrange("p s n -> p (s n)"), w_kvu_in, ACT.Copy, scale=W_SCALE
                                 ).then_inc(weights_hi, 1)

            def split_late(eng):
                eng.wait_ge(late_loaded, all_late)
                for w, src in ((w_g, w_g_in), (w_u, w_u_in)):
                    nc.scalar.activation(w[:, 0], src, ACT.Copy, scale=W_SCALE).then_inc(weights_hi, 1)
                eng.wait_ge(weights_lo, 4)

            def turn(i, b, fills, steps):
                def copy(name, dst):
                    nc.scalar.activation(dst, full(act, i, fills, name), ACT.Copy).then_inc(read["act"], 1)

                for step in steps:
                    name, n = step[:2]
                    if name == "xnT":
                        bank = full(act, i, fills, "xnT")
                        nc.scalar.activation(xnT[:], bank, ACT.Copy).then_inc(x_hi_ok.sem, 1)
                        nc.scalar.activation(xn_p[:, 0], bank, ACT.Copy, scale=X_SCALE).then_inc(x_hi_ok.sem, 1)
                    if name == "lat":
                        nc.scalar.activation(lat_p[:, 0], full(act, i, fills, "lat"), ACT.Copy, scale=LAT_SCALE
                                             ).then_inc(x_hi_ok.sem, 1)
                    if name == "gate":
                        nc.scalar.activation(th[:].rearrange("p t e -> p (t e)"),
                                             full(act, i, fills, "gate")[:, 0:TB * E1], ACT.Tanh, scale=0.5
                                             ).then_inc(read["act"], 1)
                    if name == "qk":
                        j = b if early1(step) else i
                        if step[2] == 0:
                            if n >= 1:
                                act.wait_ge(stacked.sem, stacked.at(j, 16 * 12 * n))
                            elif fills is not first:
                                act.wait_ge(stacked.sem, stacked.at(i, 16 * 12 * G))
                        nc.scalar.activation((q_hi, k_hi)[step[2] // 2][:, step[2] % 2],
                                             full(act, i, fills, head_bank(step)), ACT.Copy,
                                             scale=1.0 / (XW, LW)[step[2] // 2]).then_inc(hi_ok.sem, 1)
                    if name == "v":
                        nc.scalar.activation(v[:, n, step[2] * T:step[2] * T + T],
                                             full(act, i, fills, f"v{n}{step[2]}"), ACT.Copy, scale=1.0 / LW
                                             ).then_inc(read["act"], 1)
                    if name == "sums":
                        act.wait_ge(rec_ok.sem, rec_ok.at(i, 2 * n))
                        nc.scalar.activation(den[:], full(act, i, fills, f"sums{n}")[:, 0:T // 2], ACT.Copy
                                             ).then_inc(read["act"], 1)
                    if name == "spread":
                        act.wait_ge(normed.sem, normed.at(i, n))
                        copy(f"spread{n}", factor[:])
                    if name == "cT":
                        nc.scalar.activation(weightT[:], full(act, i, fills, "cT")[0:E1], ACT.Copy
                                             ).then_inc(read["act"], 1)
                    if name == "turn_max":
                        nc.scalar.activation(max_row[:, n % 2], full(act, i, fills, f"turn_max{n}")[0:G * TB, 0:P], ACT.Copy,
                                             scale=1.0 / SHIFT).then_inc(read["act"], 1)
                    if name == "exp":
                        u = step[2]
                        if u == 0:
                            act.wait_ge(pv_done.sem, pv_done.at(i, n - 1))
                            act.wait_ge(added.sem, added.at(i, 4 * (n - 1)))
                        act.wait_ge(exp_full.sem, exp_full.at(i, 5 * n + u + 1))
                        nc.scalar.activation(probs[:, n % 2, u], ps_exp[:, (5 * n + u) % ST_BANKS], ACT.Exp,
                                             scale=float(HD1) ** -0.5).then_inc(exp_done.sem, 1)
                    if name == "gate_in":
                        if n >= 2:
                            emptied(act, i, fills, f"g{n - 2}")
                        nc.scalar.activation(tanh[:, n % 2], full(act, i, fills, f"g{n}"), ACT.Tanh, scale=0.5 / XW
                                             ).then_inc(tanh_ok.sem, 1)
                    if name == "outT":
                        emptied(act, i, fills, "outT")
                        act.dma_start(out_dram[i].rearrange("(t p) d -> p t d", p=P), x_res[:]
                                      ).then_inc(stored.sem, 16)

            run(act, turn, split_late)
            act.wait_ge(stored.sem, 16 * batches + 16)

        @block.vector
        def _(dve):
            for s in (xn_ok, normed, rec_ok):
                dve.sem_inc(s.sem, s.begun)
            nc.vector.memset(k_b[HD1:P], SHIFT).then_inc(prep, 1)
            nc.vector.memset(ones[:], 1.0).then_inc(prep, 1)
            nc.vector.memset(row_of[:], 0.0).then_inc(prep, 1)
            dve.wait_ge(prep, 3)
            for c in range(4):
                nc.vector.memset(row_of[32 * c:32 * c + 1, c], 1.0).then_inc(prep, 1)
            dve.wait_ge(loaded, all_loaded)
            nc.vector.tensor_copy(ident_h[:], ident[:]).then_inc(prep, 1)
            nc.vector.tensor_copy(masks_h[:], masks).then_inc(prep, 1)

            dve.wait_ge(weights_hi, 2)
            for w, src in ((w_q[:], w_q_in), (w_kvu[:].rearrange("p c s n -> p c (s n)"), w_kvu_in)):
                nc.vector.scalar_tensor_tensor(out=w[:, 1], in0=src, scalar=W_SCALE, in1=w[:, 0], op0=ALU.mult,
                                               op1=ALU.subtract).then_inc(weights_lo, 1)

            def split_late(eng):
                eng.wait_ge(weights_hi, 4)
                for w, src in ((w_g, w_g_in), (w_u, w_u_in)):
                    nc.vector.scalar_tensor_tensor(out=w[:, 1], in0=src, scalar=W_SCALE, in1=w[:, 0], op0=ALU.mult,
                                                   op1=ALU.subtract).then_inc(weights_lo, 1)
                eng.wait_ge(weights_lo, 4)

            def turn(i, b, fills, steps):
                def low_part(name, lo, hi, scale, sem, count):
                    bank = full(dve, i, fills, name)
                    dve.wait_ge(sem.sem, count)
                    nc.vector.scalar_tensor_tensor(out=lo, in0=bank, scalar=scale, in1=hi, op0=ALU.mult,
                                                   op1=ALU.subtract).then_inc(read["dve"], 1)

                def route():
                    def done(k):
                        dve.wait_ge(route_ok.sem, route_ok.at(b, k))

                    emptied(dve, i, fills, "gate")
                    nc.vector.tensor_scalar(score[:], th[:], 0.5, 0.5, ALU.mult, ALU.add).then_inc(route_ok.sem, 1)
                    done(1)
                    nc.vector.tensor_tensor(select[:], score[:], bias[:].unsqueeze(1).to_broadcast([P, TB, E1]), ALU.add
                                            ).then_inc(route_ok.sem, 1)
                    done(2)
                    release(dve, dve_passed)
                    for t in range(TB):
                        nc.vector.max(top[:, t], select[:, t]).then_inc(route_ok.sem, 1)
                    done(2 + TB)
                    release(dve, dve_passed)
                    for t in range(TB):
                        nc.vector.match_replace(out=others[:, t], in_to_replace=top[:, t], in_values=select[:, t],
                                                imm_value=-1e30).then_inc(route_ok.sem, 1)
                    done(2 + 2 * TB)
                    nc.vector.tensor_tensor(keep[:], select[:], others[:], ALU.not_equal).then_inc(route_ok.sem, 1)
                    done(11)
                    nc.vector.tensor_tensor(kept[:], score[:], keep[:], ALU.mult).then_inc(route_ok.sem, 1)
                    done(12)
                    nc.vector.tensor_reduce(kept_sum[:], kept[:], AX.X, ALU.add).then_inc(route_ok.sem, 1)
                    done(13)
                    nc.vector.reciprocal(kept_rec[:], kept_sum[:]).then_inc(route_ok.sem, 1)
                    done(14)
                    nc.vector.scalar_tensor_tensor(out=weight[:], in0=kept[:], scalar=ROUTE / 2 / XW ** 2,
                                                   in1=kept_rec[:].unsqueeze(2).to_broadcast([P, TB, E1]),
                                                   op0=ALU.mult, op1=ALU.mult).then_inc(route_ok.sem, 1)

                for step in steps:
                    name, n = step[:2]
                    j = b if early1(step) else i
                    if name == "norm":
                        dve.wait_ge(x_loaded.sem, x_loaded.at(b, 16))
                        for t in range(TB):
                            nc.vector.bn_stats(stats[:, t], x_in[:, t]).then_inc(stats_ok.sem, 1)
                        dve.wait_ge(stats_ok.sem, stats_ok.at(b, TB))
                        release(dve, dve_passed)
                        for t in range(TB):
                            nc.vector.bn_aggr(mv[:, t], stats[:, t]).then_inc(stats_ok.sem, 1)
                        dve.wait_ge(stats_ok.sem, stats_ok.at(b, 2 * TB))
                        nc.vector.tensor_scalar(var_eps[:], mv[:, :, 1], EPS, None, ALU.add).then_inc(stats_ok.sem, 1)
                    if name == "scale":
                        dve.wait_ge(rstd_ok.sem, rstd_ok.at(b, 1))
                        for t in range(TB):
                            nc.vector.tensor_scalar(x_in[:, t], x_in[:, t], mv[:, t, 0:1], rstd[:, t:t + 1], ALU.subtract,
                                                    ALU.mult).then_inc(xn_ok.sem, 1)
                    if name == "qk":
                        hi, lo, scale = ((q_hi, q_lo, 1 / XW), (k_hi, k_lo, 1 / LW))[step[2] // 2]
                        r = step[2] % 2
                        low_part(head_bank(step), lo[:, r], hi[:, r], scale, hi_ok, hi_ok.at(j, 4 * n + step[2] + 1))
                    if name == "xnT":
                        low_part("xnT", xn_p[:, 1], xn_p[:, 0], X_SCALE, x_hi_ok, x_hi_ok.at(b, 2))
                    if name == "lat":
                        low_part("lat", lat_p[:, 1], lat_p[:, 0], LAT_SCALE, x_hi_ok, x_hi_ok.at(b, 3))
                    if name == "max":
                        u = step[2]
                        if u == 0:
                            if n in (1, 2):
                                dve.wait_ge(filled, fills.before(i, "all"))
                            elif n == 3:
                                dve.wait_ge(filled, fills.filled(i, "turn_max1"))
                            elif fills is not first:
                                dve.wait_ge(filled, fills.filled(i, "turn_max2"))
                        t, heads = MAX_UNITS[u]
                        k = len(heads)
                        src = full(dve, i, fills, f"max{n}_{u}")[:, 0:k * (t + 1) * P].rearrange("p (h k) -> p h k", h=k)
                        nc.vector.tensor_reduce(neg_max[:, n % 2, heads[0]:heads[0] + k, t], src, AX.X, ALU.max,
                                                negate=True).then_inc(read["dve"], 1)
                    if name == "route":
                        route()
                    if name == "rec":
                        cols = slice(P * step[2], P * step[2] + P)
                        if step[2] == 0:
                            emptied(dve, i, fills, f"sums{n}")
                            dve.wait_ge(filled, fills.filled(i, f"spread{n - 1}") if n else fills.before(i, "all"))
                        nc.vector.reciprocal(rec[:, cols], den[:, cols]).then_inc(rec_ok.sem, 1)
                    if name == "scaled":
                        dve.wait_ge(pv_done.sem, pv_done.at(i, n + 1))
                        emptied(dve, i, fills, f"spread{n}")
                        nc.vector.tensor_tensor(yT[:, n], ps_out[:, n % 2], factor[:], ALU.mult).then_inc(normed.sem, 1)
                    if name == "gate_in":
                        if n >= 1:
                            emptied(dve, i, fills, f"u{n - 1}")
                        dve.wait_ge(tanh_ok.sem, tanh_ok.at(i, n + 1))
                        nc.vector.scalar_tensor_tensor(out=gated[:], in0=tanh[:, n % 2], scalar=1.0,
                                                       in1=full(dve, i, fills, f"g{n}"), op0=ALU.add, op1=ALU.mult
                                                       ).then_inc(read["dve"], 1)
                    if name == "up_in":
                        emptied(dve, i, fills, f"g{n}")
                        dve.wait_ge(hw_ok.sem, hw_ok.at(i, max(n - 1, 0)))
                        nc.vector.tensor_tensor(hidden[:, n % 2], full(dve, i, fills, f"u{n}"), gated[:], ALU.mult
                                                ).then_inc(read["dve"], 1)
                    if name == "down":
                        bank = full(dve, i, fills, f"d{n}")
                        if n == 0:
                            dve.wait_ge(read["dve"], fills.before(i, "dve"))
                            nc.vector.tensor_copy(acc[:], bank).then_inc(read["dve"], 1)
                        else:
                            emptied(dve, i, fills, f"d{n - 1}")
                            nc.vector.tensor_tensor(acc[:], bank, acc[:], ALU.add).then_inc(read["dve"], 1)
                    if name == "out":
                        emptied(dve, i, fills, "d3")
                        emptied(dve, i, fills, f"u{E1}")
                        nc.vector.tensor_tensor(outT[:], full(dve, i, fills, "out"), acc[:], ALU.add
                                                ).then_inc(read["dve"], 1)
                    if name == "outT":
                        dve.wait_ge(res_loaded.sem, res_loaded.at(i, 16))
                        nc.vector.tensor_tensor(x_res[:].rearrange("p t d -> p (t d)"), full(dve, i, fills, "outT"),
                                                x_res[:].rearrange("p t d -> p (t d)"), ALU.add
                                                ).then_inc(read["dve"], 1)

            run(dve, turn, split_late)

        @block.tensor
        def _(pe):
            for s in (exp_full, pv_done):
                pe.sem_inc(s.sem, s.begun)
            pe.wait_ge(loaded, all_loaded)
            pe.wait_ge(prep, 9)

            def turn(i, b, fills, steps):
                def bank(name):
                    k = fills.names.index(name)
                    if k >= RING:
                        emptied(pe, i, fills, fills.names[k - RING])
                    elif fills is not first:
                        for who, sem in read.items():
                            pe.wait_ge(sem, fills.before(i, who, RING - 1 - k))
                    return ps_any[:, fills.bank(name)]

                def turned(name, blocks):
                    out = bank(name)
                    for c, src in enumerate(blocks):
                        ins = pe.transpose(out[0:src.shape[-1], c * P:c * P + P], src, ident[:])
                    ins.then_inc(filled, 1)

                def product(name, w, x):
                    pe.matmul(bank(name), w, x, start=True, stop=True).then_inc(filled, 1)

                def split_product(name, w, x):
                    out = bank(name)
                    pe.matmul(out, w(0), x(0), start=True, stop=False)
                    pe.matmul(out, w(0), x(1), start=False, stop=False)
                    pe.matmul(out, w(1), x(0), start=False, stop=True).then_inc(filled, 1)

                def xn_part(c):
                    return xn_p[:, c]

                def lat_part(c):
                    return lat_p[:, c]

                for step in steps:
                    name, n = step[:2]
                    j = b if early1(step) else i
                    if name == "xnT":
                        pe.wait_ge(xn_ok.sem, xn_ok.at(b, TB))
                        turned("xnT", [x_in[:, t] for t in range(TB)])
                    if name == "lat":
                        emptied(pe, i, fills, "xnT")
                        product("lat", w_kvd[:], xnT[:])
                    if name == "gate":
                        out = bank("gate")
                        for t in range(TB):
                            ins = pe.matmul(out[:, t * E1:t * E1 + E1], xnT[:, t * P:t * P + P], gate_w[:],
                                            start=True, stop=True)
                        ins.then_inc(filled, 1)
                    if name == "qk":
                        p = 2 * n + step[2] % 2
                        if step[2] < 2:
                            split_product(f"q{p}", lambda c: w_q[:, c, p * P:p * P + P], xn_part)
                        else:
                            if n == 0:
                                emptied(pe, i, fills, "lat")
                            split_product(f"k{p}", lambda c: w_kvu[:, c, 0, p * P:p * P + P], lat_part)
                    if name == "v":
                        half = step[2]
                        split_product(f"v{n}{half}", lambda c: lat_p[:, c, n * P:n * P + P],
                                      lambda c: w_kvu[:, c, 1, half * T:half * T + T])
                    if name == "cT":
                        pe.wait_ge(route_ok.sem, route_ok.at(b, 15))
                        turned("cT", [weight[:, t] for t in range(TB)])
                    if name == "max":
                        t, heads = MAX_UNITS[step[2]]
                        w = (t + 1) * P
                        if step[2] == 0:
                            pe.wait_ge(stacked.sem, stacked.at(j, 16 * 12 * (n + 1)))
                        scores = bank(f"max{n}_{step[2]}")
                        for c, h in enumerate(heads):
                            out = scores[:, c * w:c * w + w]
                            pe.matmul(out, q_a[:, n % 2, h, t * P:t * P + P], k_a[:, n % 2, h, 0:w],
                                      start=True, stop=False)
                            ins = pe.matmul(out[:, t * P:w], ident_h[:], masks_h[:, 0], start=False, stop=True)
                        ins.then_inc(filled, 1)
                    if name == "turn_max":
                        emptied(pe, i, fills, f"max{n}_{NM - 1}")
                        pe.transpose(bank(f"turn_max{n}")[0:G * TB, 0:P], neg_max[:, n % 2].rearrange("p h t -> p (h t)"),
                                     ident[:]).then_inc(filled, 1)
                    if name == "exp":
                        m = 5 * n + step[2]
                        g = n // 2
                        if step[2] == 0 and n % 2 == 0:
                            pe.wait_ge(row_in.sem, row_in.at(i, 16 * (g + 1)))
                        pe.wait_ge(exp_done.sem, exp_done.at(i, max(m + 1 - ST_BANKS, 0)))
                        for r, k, c in EXP1[step[2]]:
                            h = 2 * (n % 2) + r
                            w = T - k * P
                            out = ps_exp[:, m % ST_BANKS, c:c + w]
                            pe.matmul(out, k_a[:, g % 2, h, k * P:k * P + P], q_a[:, g % 2, h, k * P:T],
                                      start=True, stop=False)
                            pe.matmul(out, k_b[0:K_B, g % 2, h, k * P:k * P + P], q_b[0:K_B, g % 2, h, k * P:T],
                                      start=False, stop=False)
                            ins = pe.matmul(out[:, 0:P], ident_h[:], masks_h[:, 1], start=False, stop=True)
                        ins.then_inc(exp_full.sem, 1)
                    if name == "values":
                        if n == 0:
                            pe.wait_ge(read["act"], fills.before(i, "act"))
                        pe.wait_ge(normed.sem, normed.at(i, n - 1))
                        pe.wait_ge(exp_done.sem, exp_done.at(i, 5 * n + 5))
                        pieces = sorted([(k, r, u, c) for u in range(5) for r, k, c in EXP1[u]])
                        for k, r, u, c in pieces:
                            h = 2 * n + r
                            ins = pe.matmul(ps_out[HD1 * r:HD1 * r + HD1, n % 2, k * P:T], v[:, k, h * HD1:h * HD1 + HD1],
                                            probs[:, n % 2, u, c:c + T - k * P], start=(k == 0), stop=(k == TB - 1))
                        ins.then_inc(pv_done.sem, 1)
                    if name == "sums":
                        pe.wait_ge(added.sem, added.at(i, 4 * (n + 1)))
                        out = bank(f"sums{n}")
                        for c in range(4):
                            cols = slice(T // 2 * (c % 2), T // 2 * (c % 2) + T // 2)
                            ins = pe.matmul(out[32 * c:32 * c + 32, 0:T // 2], ones[:],
                                            key_sum[:, 2 * (n % 2) + c // 2, cols], start=True, stop=True)
                        ins.then_inc(filled, 1)
                    if name == "spread":
                        pe.wait_ge(rec_ok.sem, rec_ok.at(i, 2 * (n + 1)))
                        out = bank(f"spread{n}")
                        for half in range(2):
                            for r in range(2):
                                ins = pe.matmul(out[HD1 * r:HD1 * r + HD1, T // 2 * half:T // 2 * half + T // 2],
                                                row_of[:, 2 * r + half], rec[:], start=True, stop=True)
                        ins.then_inc(filled, 1)
                    if name == "gate_in":
                        split_product(f"g{n}", lambda c: w_g[:, c, n], xn_part)
                    if name == "up_in":
                        split_product(f"u{n}", lambda c: w_u[:, c, n], xn_part)
                    if name == "down":
                        out = bank(f"d{n}")
                        for k in range(CHUNK):
                            e = CHUNK * n + k
                            pe.wait_ge(hw_ok.sem, hw_ok.at(i, e + 1))
                            ins = pe.matmul(out, w_d[:, e], hw[:, n % 2, k], start=(k == 0), stop=(k == CHUNK - 1))
                        ins.then_inc(filled, 1)
                    if name == "out":
                        out = bank("out")
                        pe.wait_ge(hw_ok.sem, hw_ok.at(i, E1 + 1))
                        pe.matmul(out, w_d[:, E1], hw[:, 0, 0], start=True, stop=False)
                        for p in range(PAIRS):
                            pe.wait_ge(normed.sem, normed.at(i, p + 1))
                            ins = pe.matmul(out, w_out[:, p], yT[:, p], start=False, stop=(p == PAIRS - 1))
                        ins.then_inc(filled, 1)
                    if name == "outT":
                        emptied(pe, i, fills, "out")
                        turned("outT", [outT[:, t * P:t * P + P] for t in range(TB)])

            def weights_split(eng):
                eng.wait_ge(weights_lo, 4)
                eng.wait_ge(late_loaded, all_late)

            pe.wait_ge(weights_lo, 2)
            run(pe, turn, weights_split)


def build(nc, a, out, batches):
    x1_dram = nc.dram_tensor("x1_scratch", [batches, T, D], F32, kind="Internal").ap()
    layer0(nc, a, x1_dram, batches)
    layer1(nc, a, x1_dram, out, batches)


def constants():
    cos, sin = rotary_tables()
    q, k = np.arange(P)[:, None], np.arange(P)[None, :]
    return {"ident": np.eye(P, dtype=np.float32), "cos": cos, "sin": sin,
            "mask": np.where(k > q, np.float32(-1e30), np.float32(0)),
            "maskT": np.where(q > k, np.float32(-1e30), np.float32(0))}


def lay_out(inputs):
    laid = {n: np.asarray(v) for n, v in inputs.items()}
    for n in ("L1_ffn_w_gate", "L1_ffn_w_up", "L1_ffn_w_down"):
        laid[n] = laid[n].transpose(2, 0, 1)
    for n in ("L1_ffn_gate_w", "L1_ffn_shared_gate_w", "L1_ffn_shared_up_w", "L1_ffn_shared_down_w"):
        laid[n] = laid[n].T
    laid["L0_ffn_b1"] = laid["L0_ffn_b1"].reshape(E0, HB, P).transpose(2, 0, 1)
    laid.update(constants())
    return {n: np.ascontiguousarray(v) for n, v in laid.items()}


def kernel(**inputs):
    import concourse.bacc as bacc
    from concourse.bass_utils import run_bass_kernel_spmd

    nc = bacc.Bacc("TRN2", target_bir_lowering=False, num_devices=1)
    laid = lay_out(inputs)
    arrays, a = {}, {}
    for n, v in laid.items():
        arrays[f"in_{n}"] = v
        a[n] = nc.dram_tensor(f"in_{n}", v.shape, mybir.dt.from_np(v.dtype), kind="ExternalInput").ap()
    shape = laid["L0_attn_x"].shape
    out = nc.dram_tensor("out_0", shape, F32, kind="ExternalOutput").ap()
    build(nc, a, out, shape[0])
    r = run_bass_kernel_spmd(nc, [arrays], core_ids=[0])
    return r.results[0]["out_0"]
```
